# Optimizing a Trainium2 kernel written in Bass

```python
import numpy as np
import jax
import jax.numpy as jnp

def _softmax(x, axis=-1):
    return jax.nn.softmax(x, axis=axis)

def _gelu(x):
    return jax.nn.gelu(x, approximate=True)

def _silu(x):
    return jax.nn.silu(x)

def _sigmoid(x):
    return jax.nn.sigmoid(x)

def _layernorm(x, axis=-1, eps=1e-05):
    m = jnp.mean(x, axis=axis, keepdims=True)
    v = jnp.var(x, axis=axis, keepdims=True)
    return (x - m) / jnp.sqrt(v + eps)

def _scatter_add(tgt, idx, src, axis=0):
    return tgt.at[idx].add(src)

def _segment_sum(src, seg, n):
    return jax.ops.segment_sum(src, seg, n)
kernel_name = 'mk_hybrid_d1_jaxref_r4_ee2435'

def setup_inputs(seed: int=0):
    np.random.seed(seed)
    _w = jnp.asarray

    def _L0_attn_a_setup():
        import jax, jax.numpy as jnp
        import numpy as np
        E = 256
        H = 16
        D = E // H
        LOCAL_WINDOW = 5
        GATING_THRESHOLD = 0.0
        GAUSS_SIGMA = 2.0
        PERIODIC_STRENGTH = 1.0
        PERIOD = 401.0
        NEG = -1000000000.0
        key = jax.random.key(seed)
        ks = jax.random.split(key, 9)
        B, S = (2, 512)
        sc = 1.0 / np.sqrt(E)
        inp = {'x': jax.random.normal(ks[0], (B, S, E), dtype=jnp.float32), 'wq': jax.random.normal(ks[1], (E, E), dtype=jnp.float32) * sc, 'bq': jnp.zeros((E,), dtype=jnp.float32), 'wk': jax.random.normal(ks[2], (E, E), dtype=jnp.float32) * sc, 'bk': jnp.zeros((E,), dtype=jnp.float32), 'wv': jax.random.normal(ks[3], (E, E), dtype=jnp.float32) * sc, 'bv': jnp.zeros((E,), dtype=jnp.float32), 'wo': jax.random.normal(ks[4], (E, E), dtype=jnp.float32) * sc, 'bo': jnp.zeros((E,), dtype=jnp.float32)}
        return inp
    _L0_attn_a_in = _L0_attn_a_setup()

    def _L0_attn_b_setup():
        import jax, jax.numpy as jnp
        import numpy as np
        B, L, D = (2, 512, 256)
        H, P = (16, 3)
        HD = D // H
        DH = D // 2
        key = jax.random.key(seed)
        ks = jax.random.split(key, 18)
        s = 0.02
        inp = {'x': jax.random.normal(ks[0], (B, L, D), jnp.float32), 'wq': jax.random.normal(ks[1], (D, D), jnp.float32) * s, 'bq': jnp.zeros((D,), jnp.float32), 'wk': jax.random.normal(ks[2], (D, D), jnp.float32) * s, 'bk': jnp.zeros((D,), jnp.float32), 'wv': jax.random.normal(ks[3], (D, D), jnp.float32) * s, 'bv': jnp.zeros((D,), jnp.float32), 'wo': jax.random.normal(ks[4], (D, D), jnp.float32) * s, 'bo': jnp.zeros((D,), jnp.float32), 'pw1': jax.random.normal(ks[5], (P, DH, D), jnp.float32) * s, 'pb1': jnp.zeros((P, DH), jnp.float32), 'pw2': jax.random.normal(ks[6], (P, H, DH), jnp.float32) * s, 'pb2': jnp.zeros((P, H), jnp.float32), 'sw1': jax.random.normal(ks[7], (DH, D), jnp.float32) * s, 'sb1': jnp.zeros((DH,), jnp.float32), 'sw2': jax.random.normal(ks[8], (P, DH), jnp.float32) * s, 'sb2': jnp.zeros((P,), jnp.float32)}
        return inp
    _L0_attn_b_in = _L0_attn_b_setup()

    def _L0_ffn_setup():
        import jax, jax.numpy as jnp
        import numpy as np
        key = jax.random.key(seed)
        k1, k2, k3, k4 = jax.random.split(key, 4)
        B, T, M = (4, 512, 256)
        E, F = (16, 1024)
        x = jax.random.normal(k1, (B, T, M), dtype=jnp.float32) * 0.02
        Wg = jax.random.normal(k2, (M, E), dtype=jnp.float32) * 0.02
        w1 = jax.random.normal(k3, (E, M, F), dtype=jnp.float32) * 0.02
        w2 = jax.random.normal(k4, (E, F, M), dtype=jnp.float32) * 0.02
        return {'x': x, 'Wg': Wg, 'w1': w1, 'w2': w2}
    _L0_ffn_in = _L0_ffn_setup()
    _d = {'L0_attn_a_x': _L0_attn_a_in['x'], 'L0_attn_a_wq': _L0_attn_a_in['wq'], 'L0_attn_a_bq': _L0_attn_a_in['bq'], 'L0_attn_a_wk': _L0_attn_a_in['wk'], 'L0_attn_a_bk': _L0_attn_a_in['bk'], 'L0_attn_a_wv': _L0_attn_a_in['wv'], 'L0_attn_a_bv': _L0_attn_a_in['bv'], 'L0_attn_a_wo': _L0_attn_a_in['wo'], 'L0_attn_a_bo': _L0_attn_a_in['bo'], 'L0_attn_b_wq': _L0_attn_b_in['wq'], 'L0_attn_b_bq': _L0_attn_b_in['bq'], 'L0_attn_b_wk': _L0_attn_b_in['wk'], 'L0_attn_b_bk': _L0_attn_b_in['bk'], 'L0_attn_b_wv': _L0_attn_b_in['wv'], 'L0_attn_b_bv': _L0_attn_b_in['bv'], 'L0_attn_b_wo': _L0_attn_b_in['wo'], 'L0_attn_b_bo': _L0_attn_b_in['bo'], 'L0_attn_b_pw1': _L0_attn_b_in['pw1'], 'L0_attn_b_pb1': _L0_attn_b_in['pb1'], 'L0_attn_b_pw2': _L0_attn_b_in['pw2'], 'L0_attn_b_pb2': _L0_attn_b_in['pb2'], 'L0_attn_b_sw1': _L0_attn_b_in['sw1'], 'L0_attn_b_sb1': _L0_attn_b_in['sb1'], 'L0_attn_b_sw2': _L0_attn_b_in['sw2'], 'L0_attn_b_sb2': _L0_attn_b_in['sb2'], 'L0_ffn_Wg': _L0_ffn_in['Wg'], 'L0_ffn_w1': _L0_ffn_in['w1'], 'L0_ffn_w2': _L0_ffn_in['w2']}
    _x0 = _d['L0_attn_a_x']
    _d['L0_attn_a_x'] = jax.random.normal(jax.random.fold_in(jax.random.key(seed), 1), (16, 512, 256), dtype=_x0.dtype)
    del _x0
    return _d

def reference(L0_attn_a_x, L0_attn_a_wq, L0_attn_a_bq, L0_attn_a_wk, L0_attn_a_bk, L0_attn_a_wv, L0_attn_a_bv, L0_attn_a_wo, L0_attn_a_bo, L0_attn_b_wq, L0_attn_b_bq, L0_attn_b_wk, L0_attn_b_bk, L0_attn_b_wv, L0_attn_b_bv, L0_attn_b_wo, L0_attn_b_bo, L0_attn_b_pw1, L0_attn_b_pb1, L0_attn_b_pw2, L0_attn_b_pb2, L0_attn_b_sw1, L0_attn_b_sb1, L0_attn_b_sw2, L0_attn_b_sb2, L0_ffn_Wg, L0_ffn_w1, L0_ffn_w2):

    def _L0_attn_a_ref(x, wq, bq, wk, bk, wv, bv, wo, bo):
        import jax, jax.numpy as jnp
        import numpy as np
        E = 256
        H = 16
        D = E // H
        LOCAL_WINDOW = 5
        GATING_THRESHOLD = 0.0
        GAUSS_SIGMA = 2.0
        PERIODIC_STRENGTH = 1.0
        PERIOD = 401.0
        NEG = -1000000000.0
        B, S, _ = x.shape
        q = (x @ wq.T + bq).reshape(B, S, H, D).transpose(0, 2, 1, 3)
        k = (x @ wk.T + bk).reshape(B, S, H, D).transpose(0, 2, 1, 3)
        v = (x @ wv.T + bv).reshape(B, S, H, D).transpose(0, 2, 1, 3)
        scores = jnp.einsum('bhid,bhjd->bhij', q, k) / jnp.sqrt(jnp.float32(D))
        idx = jnp.arange(S)
        dist = idx[:, None] - idx[None, :]
        local_mask = jnp.abs(dist) <= LOCAL_WINDOW // 2
        glob = (idx[:, None] == 0) | (idx[None, :] == 0)
        attn_mask = local_mask | glob
        scores = jnp.where(attn_mask[None, None], scores, NEG)
        diff = dist.astype(jnp.float32)
        pos_bias = jnp.exp(-0.5 * (diff / GAUSS_SIGMA) ** 2) + PERIODIC_STRENGTH * jnp.cos(2.0 * jnp.pi * diff / PERIOD)
        scores = scores + pos_bias[None, None]
        scores = jnp.where(scores < GATING_THRESHOLD, NEG, scores)
        probs = jax.nn.softmax(scores, axis=-1)
        ctx = jnp.einsum('bhij,bhjd->bhid', probs, v)
        ctx = ctx.transpose(0, 2, 1, 3).reshape(B, S, E)
        return ctx @ wo.T + bo

    def _L0_attn_b_ref(x, wq, bq, wk, bk, wv, bv, wo, bo, pw1, pb1, pw2, pb2, sw1, sb1, sw2, sb2):
        import jax, jax.numpy as jnp
        import numpy as np
        B, L, D = (2, 512, 256)
        H, P = (16, 3)
        HD = D // H
        DH = D // 2
        b, l, d = x.shape
        h = pw2.shape[1]
        hd = d // h
        scale = jnp.sqrt(jnp.asarray(hd, x.dtype))
        Q = (x @ wq.T + bq).reshape(b, l, h, hd).transpose(0, 2, 1, 3)
        K = (x @ wk.T + bk).reshape(b, l, h, hd).transpose(0, 2, 1, 3)
        V = (x @ wv.T + bv).reshape(b, l, h, hd).transpose(0, 2, 1, 3)
        scores = jnp.einsum('bhqd,bhkd->bhqk', Q, K) / scale
        causal = jnp.triu(jnp.ones((l, l), bool), 1)
        scores = jnp.where(causal[None, None], jnp.asarray(-1000000000.0, x.dtype), scores)
        xm = x.mean(axis=1)
        policy_w = jax.nn.softmax(jax.nn.gelu(xm @ sw1.T + sb1, approximate=False) @ sw2.T + sb2, axis=-1)
        hid = jax.nn.gelu(jnp.einsum('bd,pcd->bpc', xm, pw1) + pb1, approximate=False)
        gates = jax.nn.softmax(jnp.einsum('bpc,phc->bph', hid, pw2) + pb2, axis=-1)
        head_gates = jnp.einsum('bp,bph->bh', policy_w, gates)
        scores = scores * head_gates[:, :, None, None]
        attn = jax.nn.softmax(scores, axis=-1)
        out = jnp.einsum('bhqk,bhkd->bhqd', attn, V)
        out = out.transpose(0, 2, 1, 3).reshape(b, l, d)
        return out @ wo.T + bo

    def _L0_ffn_ref(x, Wg, w1, w2):
        import jax, jax.numpy as jnp
        import numpy as np
        d = x.shape[-1]
        xr = x.reshape(-1, d)
        S = xr.shape[0]
        E = Wg.shape[1]
        C = (S + E - 1) // E
        gate = jax.nn.softmax(xr @ Wg, axis=-1)
        idx = jnp.argmax(gate, axis=1)
        gates_s = jnp.take_along_axis(gate, idx[:, None], axis=1)[:, 0]
        onehot = jax.nn.one_hot(idx, E, dtype=jnp.int32)
        loc = jnp.sum((jnp.cumsum(onehot, axis=0) - 1) * onehot, axis=1)
        valid = loc < C
        loc_pad = jnp.minimum(loc, C)
        dispatched = jnp.zeros((E, C + 1, d), dtype=x.dtype).at[idx, loc_pad].set(xr)
        dispatched = dispatched[:, :C]
        h = jax.nn.relu(jnp.einsum('ecm,emf->ecf', dispatched, w1))
        expert_out = jnp.einsum('ecf,efm->ecm', h, w2)
        gathered = expert_out[idx, jnp.minimum(loc, C - 1)]
        combined = gathered * (gates_s * valid.astype(x.dtype))[:, None]
        return combined.reshape(x.shape)
    x = L0_attn_a_x
    x = x + _L0_attn_a_ref(_layernorm(x, axis=-1), L0_attn_a_wq, L0_attn_a_bq, L0_attn_a_wk, L0_attn_a_bk, L0_attn_a_wv, L0_attn_a_bv, L0_attn_a_wo, L0_attn_a_bo)
    x = x + _L0_ffn_ref(_layernorm(x, axis=-1), L0_ffn_Wg, L0_ffn_w1, L0_ffn_w2)
    x = x + _L0_attn_b_ref(_layernorm(x, axis=-1), L0_attn_b_wq, L0_attn_b_bq, L0_attn_b_wk, L0_attn_b_bk, L0_attn_b_wv, L0_attn_b_bv, L0_attn_b_wo, L0_attn_b_bo, L0_attn_b_pw1, L0_attn_b_pb1, L0_attn_b_pw2, L0_attn_b_pb2, L0_attn_b_sw1, L0_attn_b_sb1, L0_attn_b_sw2, L0_attn_b_sb2)
    x = x + _L0_ffn_ref(_layernorm(x, axis=-1), L0_ffn_Wg, L0_ffn_w1, L0_ffn_w2)
    return x

_drawn_inputs = setup_inputs


def setup_inputs(seed=0):
    import zlib

    import numpy as np

    out = dict(_drawn_inputs(seed))
    spreads = {'L0_attn_a_bq': (0.0, 0.1),
     'L0_attn_a_bk': (0.0, 0.8),
     'L0_attn_a_bv': (0.0, 0.1),
     'L0_attn_a_bo': (0.0, 0.1),
     'L0_attn_b_bq': (0.0, 2.0),
     'L0_attn_b_bk': (0.0, 2.0),
     'L0_attn_b_bv': (0.0, 0.274),
     'L0_attn_b_bo': (0.0, 0.1),
     'L0_attn_b_pb1': (0.0, 2.0),
     'L0_attn_b_pb2': (0.0, 2.0),
     'L0_attn_b_sb1': (0.0, 2.0),
     'L0_attn_b_sb2': (0.0, 2.0)}
    factors = {'L0_attn_b_wq': 25.577,
     'L0_attn_b_wk': 23.847,
     'L0_attn_b_wv': 3.13,
     'L0_attn_b_pw1': 64.0,
     'L0_attn_b_pw2': 45.071,
     'L0_attn_b_sw1': 64.0,
     'L0_attn_b_sw2': 64.0,
     'L0_ffn_w1': 2.818}
    for name, (base, spread) in spreads.items():
        noise = np.random.default_rng([zlib.crc32(name.encode()), seed]).standard_normal(out[name].shape)
        drawn = base * np.exp(spread * noise) if base else spread * noise
        out[name] = jnp.asarray(drawn.astype(out[name].dtype))
    for name, factor in factors.items():
        out[name] = (out[name] * factor).astype(out[name].dtype)
    return out
```

```python
from contextlib import ExitStack

import concourse.bass as bass
from concourse import mybir

F32 = mybir.dt.float32
BF16 = mybir.dt.bfloat16
U32 = mybir.dt.uint32
ALU = mybir.AluOpType
ACT = mybir.ActivationFunctionType
AX = mybir.AxisListType

P = 128
BATCH, SEQ, D = 16, 512, 256
HEADS, HD = 16, 16
N_TOK = BATCH * SEQ
TILES = N_TOK // P
DC = D // P
EPS = 1e-5


def wait(eng, sem, value):
    if not isinstance(value, int) or value > 0:
        eng.wait_ge(sem, value)


class Chain:

    def __init__(self, eng, sem):
        self.eng, self.sem, self.base, self.n, self.turn, self.per_turn = eng, sem, 0, 0, None, 0

    def enter(self, turn, per_turn):
        self.base, self.n, self.turn, self.per_turn = self.base + self.n, 0, turn, per_turn

    def leave(self, turns):
        assert self.n == self.per_turn, (self.n, self.per_turn)
        self.base, self.n, self.turn = self.base + turns * self.per_turn, 0, None

    def mark(self, instruction):
        self.n += 1
        instruction.then_inc(self.sem, 1)

    def settle(self):
        value = self.base + self.n
        if self.turn is not None:
            value = self.turn * self.per_turn + value
        self.eng.wait_ge(self.sem, value)

    def then(self, instruction):
        self.mark(instruction)
        self.settle()


class Stage:

    def __init__(self, nc, name):
        self.nc, self.name, self.ctx = nc, name, ExitStack()
        self.sems = []

    def __enter__(self):
        self.ctx.__enter__()
        self.ctx.callback(self.clear)
        return self

    def clear(self):
        self.nc.clear_and_free_semaphores(self.sems)
        self.nc.all_engine_barrier()

    def __exit__(self, *a):
        return self.ctx.__exit__(*a)

    def sb(self, name, shape, dt=F32):
        return self.ctx.enter_context(self.nc.sbuf_tensor(f"{self.name}_{name}", shape, dt))

    def ps(self, name, shape, dt=F32):
        return self.ctx.enter_context(self.nc.psum_tensor(f"{self.name}_{name}", shape, dt))

    def sem(self, name):
        self.sems.append(self.nc.alloc_semaphore(f"{self.name}_{name}"))
        return self.sems[-1]


CH = 8
CHUNKS = TILES // CH
REACH = 2
EXT = TILES + 2 * REACH
E_FIRST, E_MEAN = EXT, EXT + 1
OLD = 2 * REACH
SLOTS = CH + OLD
NOFF = 2 * REACH + 2
PRO = 2 + OLD
TPB = P // BATCH


def stage_a(nc, x, wq, bq, wk, bk, wv, bv, wo, bo, band_bias, first_bias, out):
    x_v = x.rearrange("(p t) n -> p t n", p=P)
    o_v = out.rearrange("(p t) n -> p t n", p=P)
    x_b = x.rearrange("(b r) n -> b r n", b=BATCH)
    o_b = out.rearrange("(b r) n -> b r n", b=BATCH)
    with Stage(nc, "a") as st:
        sb, ps, sem = st.sb, st.ps, st.sem
        xv = sb("xv", [P, EXT + 2, D])
        qkb = sb("qkb", [P, 2 * SLOTS, 2 * D])
        qkz = sb("qkz", [P, 2 * D])
        wT = sb("wT", [P, DC, 4 * D])
        bias3 = sb("bias3", [P, 4 * D], BF16)
        ones_bf = sb("ones_bf", [P, P], BF16)
        ident = sb("ident", [P, P])
        blk = sb("blk", [P, P])
        stg = sb("stg", [P, 2, D])
        xT = sb("xT", [P, 2, DC, P])
        mean = sb("mean", [P, EXT + 1])
        rstd = sb("rstd", [P, EXT + 1])
        band = sb("band", [P, TILES, NOFF])
        fbias = sb("fbias", [P, TILES])
        prd = sb("prd", [P, CH, D])
        prp = sb("prp", [P, CH, D])
        s6 = sb("s6", [P, CH * HEADS, NOFF])
        e6 = sb("e6", [P, CH * HEADS, NOFF])
        sm = sb("sm", [P, 4, CH * HEADS])
        s0 = sb("s0", [P, TILES, HEADS])
        grp = [sb(f"grp{i}", [P, CH, D]) for i in range(2)]
        cT = sb("cT", [P, 2, DC, P])
        xr = sb("xr", [P, CH, D])
        ob = sb("ob", [P, CH, D])
        r0 = sb("r0", [P, 6, HEADS])
        r0T = sb("r0T", [HEADS, P + BATCH])
        wn = qkb[:, 0:4, :].rearrange("p a (b n) -> p a b n", b=2)
        brow = prd[0:1, :, :].rearrange("p a n -> p (a n)").rearrange("p (b n) -> p b n", b=2)
        bpart = prp[0:1, :, :].bitcast(BF16).rearrange("p a n -> p (a n)").rearrange("p (b n) -> p b n", b=4)
        bn = grp[0][:, 0:2, :].rearrange("p a n -> p (a n)")[:, 0:6 * (EXT + 1)].rearrange("p (a n) -> p a n", n=6)
        tmp = grp[1][:, 0, 0:2 * (EXT + 1)].rearrange("p (a n) -> p a n", a=2)
        first_e = prd[:, 0:4, :].rearrange("p a (b h) -> p (a b) h", h=HEADS)

        p_x = ps("p_x", [P, 2, 512])
        p_qk = ps("p_qk", [P, 2, 512])
        p_v = ps("p_v", [P, 512])
        p_c = ps("p_c", [P, 2, 512])
        p_o = ps("p_o", [P, 512])

        loaded = [sem(f"loaded{c}") for c in range(CHUNKS)]
        (halo, w_in, b_in, tab_in, const, wt_ps, wt_ok, bsplit, bias_in, varok, sdok, normed, sum_ps, mean_ok,
         staged, xt_ps, xt_ok, qkv_ps, qk_ok, wrapped, pooled, pool_red, s_done, e_in, e_out, p_ok, g_dve, g_pool,
         ct_ps, ct_ok, o_ps, o_ok, xr_in, y_ok, y_out, dch, pch, f_e, f_exp, f_tr, f_trd, f_prod, f_used, f_sum,
         f_ctx, f_den, f_zero, f_x, f_y) = [sem(n) for n in (
             "halo", "w_in", "b_in", "tab_in", "const", "wt_ps", "wt_ok", "bsplit", "bias_in", "varok", "sdok",
             "normed", "sum_ps", "mean_ok", "staged", "xt_ps", "xt_ok", "qkv_ps", "qk_ok", "wrapped", "pooled",
             "pool_red", "s_done", "e_in", "e_out", "p_ok", "g_dve", "g_pool", "ct_ps", "ct_ok", "o_ps", "o_ok",
             "xr_in", "y_ok", "y_out", "dve_chain", "pool_chain", "first_e_in", "first_e_out", "first_tr",
             "first_tr_used", "first_prod", "first_used", "first_sum", "first_ctx", "first_den", "first_zero",
             "first_x", "first_y")]
        block = st.ctx.enter_context(nc.Block())

        @block.sync
        def _(sp):
            for c in range(CHUNKS):
                sp.dma_start(xv[:, REACH + c * CH:REACH + (c + 1) * CH, :],
                             x_v[:, c * CH:(c + 1) * CH, :]).then_inc(loaded[c], 16)
            sp.dma_start(xv[1:P, 0:REACH, :], x_v[0:P - 1, TILES - REACH:TILES, :]).then_inc(halo, 16)
            sp.dma_start(xv[0:1, 0:REACH, :], x_v[0:1, 0:REACH, :]).then_inc(halo, 16)
            sp.dma_start(xv[0:P - 1, EXT - REACH:EXT, :], x_v[1:P, 0:REACH, :]).then_inc(halo, 16)
            sp.dma_start(xv[P - 1:P, EXT - REACH:EXT, :], x_v[P - 1:P, 0:REACH, :]).then_inc(halo, 16)
            for g in range(TPB):
                sp.dma_start(xv[g:P:TPB, E_FIRST, :], x_b[:, 0, :]).then_inc(halo, 16)
            sp.wait_ge(bsplit, 1)
            for i in range(3):
                sp.dma_start(bias3[i:i + 1, :], bpart[0:1, i, :]).then_inc(bias_in, 16)
            sp.dma_start(xr[:, :, :], x_v[:, 0:CH, :]).then_inc(xr_in, 16)
            with sp.Fori(1, CHUNKS) as c:
                sp.wait_ge(y_ok, c)
                sp.dma_start(o_v[:, bass.ds(c * CH - CH, CH), :], xr[:, :, :]).then_inc(y_out, 16)
                sp.wait_ge(y_out, c * 16)
                sp.dma_start(xr[:, :, :], x_v[:, bass.ds(c * CH, CH), :]).then_inc(xr_in, 16)
            sp.wait_ge(y_ok, CHUNKS)
            sp.dma_start(o_v[:, (CHUNKS - 1) * CH:, :], xr[:, :, :]).then_inc(y_out, 16)
            sp.wait_ge(y_out, 16 * CHUNKS)
            sp.wait_ge(f_zero, 1)
            sp.dma_start(ob[0:P:TPB, 0, :], x_b[:, 0, :]).then_inc(f_x, 16)
            sp.wait_ge(f_y, 1)
            sp.dma_start(o_b[:, 0, :], ob[0:P:TPB, 1, :]).then_inc(y_out, 16)
            sp.wait_ge(y_out, 16 * CHUNKS + 16)

        @block.gpsimd
        def _(pool):
            ch = Chain(pool, pch)
            for m, v in ((ident, 0.0), (blk, 1.0), (ones_bf, 1.0), (bias3, 0.0)):
                pool.memset(m[:, :], v).then_inc(const, 1)
            pool.wait_ge(const, 4)
            pool.affine_select(out=ident[:, :], in_=ident[:, :], compare_op=ALU.not_equal, fill=1.0,
                               base=0, pattern=[[-1, P]], channel_multiplier=1).then_inc(const, 1)
            blk_v = blk[:, :].rearrange("p (b g) -> p b g", g=TPB)
            ch.then(pool.affine_select(out=blk_v, in_=blk_v, compare_op=ALU.is_ge, fill=0.0, base=0,
                                       pattern=[[-TPB, BATCH], [0, TPB]], channel_multiplier=1))
            pool.affine_select(out=blk_v, in_=blk_v, compare_op=ALU.is_ge, fill=0.0, base=TPB - 1,
                               pattern=[[TPB, BATCH], [0, TPB]], channel_multiplier=-1).then_inc(const, 1)

            def residual(c):
                pool.wait_ge(xr_in, 16 * c + 16)
                pool.wait_ge(o_ok, CH * c + CH)
                pool.tensor_tensor(xr[:, :, :], xr[:, :, :], ob[:, :, :], ALU.add).then_inc(y_ok, 1)

            def chunk(c, par, behind=True):
                own = slice(SLOTS * par + REACH, SLOTS * par + REACH + CH)
                pool.wait_ge(qk_ok, PRO + CH * c + CH)
                wait(pool, pool_red, 2 * c)
                k0 = qkz[:, D:].unsqueeze(1).to_broadcast([P, CH, D])
                q0 = qkz[:, 0:D].unsqueeze(1).to_broadcast([P, CH, D])
                if behind:
                    pool.wait_ge(g_pool, c)
                pool.tensor_tensor(prp[:, :, :], qkb[:, own, 0:D], k0, ALU.mult).then_inc(pooled, 1)
                pool.wait_ge(pool_red, 2 * c + 1)
                pool.tensor_tensor(prp[:, :, :], qkb[:, own, D:], q0, ALU.mult).then_inc(pooled, 1)
                if behind:
                    residual(c - 1)
                pool.wait_ge(p_ok, c + 1)
                pool.wait_ge(pool_red, 2 * c + 2)
                wait(pool, ct_ps, CH * c)
                by_head = lambda a: a.rearrange("p t (h c) -> p t h c", c=HD)
                weight = lambda a: a.rearrange("p (t h) o -> p t h o", h=HEADS).to_broadcast([P, CH, HEADS, HD])
                row = lambda e: by_head(xv[:, e:e + 1, :]).to_broadcast([P, CH, HEADS, HD])
                ch.mark(pool.tensor_tensor(by_head(grp[1][:, :, :]), by_head(xv[:, bass.ds(CH * c + OLD, CH), :]),
                                           weight(e6[:, :, OLD:OLD + 1]), ALU.mult))
                for w, e in ((e6[:, :, NOFF - 1:NOFF], E_FIRST), (sm[:, 1, :].unsqueeze(2), E_MEAN)):
                    ch.then(pool.tensor_tensor(by_head(prp[:, :, :]), row(e), weight(w), ALU.mult))
                    add = pool.tensor_tensor(grp[1][:, :, :], grp[1][:, :, :], prp[:, :, :], ALU.add)
                    if e == E_FIRST:
                        ch.then(add)
                    else:
                        add.then_inc(g_pool, 1)

            chunk(0, 0, behind=False)
            n = ch.n
            chunk(1, 1)
            per = 2 * (ch.n - n)
            with pool.Fori(0, CHUNKS // 2 - 1) as g:
                ch.enter(g, per)
                chunk(2 * g + 2, 0)
                chunk(2 * g + 3, 1)
            ch.leave(CHUNKS // 2 - 1)
            residual(CHUNKS - 1)
            pool.wait_ge(y_ok, CHUNKS)
            pool.memset(ob[:, 0, :], 0.0).then_inc(f_zero, 1)

        @block.scalar
        def _(act):
            for i, w in enumerate((wq, wk, wv, wo)):
                act.dma_start(wn[:, i, :, :], w.rearrange("(c p) n -> p c n", p=P)).then_inc(w_in, 16)
            for i, b in enumerate((bq, bk, bv, bo)):
                act.dma_start(brow[0:1, 0, i * D:(i + 1) * D], b.rearrange("(a n) -> a n", a=1)).then_inc(b_in, 16)
            act.dma_start(band[:, :, :], band_bias).then_inc(tab_in, 16)
            act.dma_start(fbias[:, :], first_bias).then_inc(tab_in, 16)
            for i in range(4):
                act.wait_ge(wt_ps, i + 1)
                src = (p_x[:, 0, :], p_x[:, 1, :], p_qk[:, 0, :], p_qk[:, 1, :])[i].rearrange("p (c n) -> p c n", c=DC)
                nc.scalar.activation(wT[:, :, i * D:(i + 1) * D], src, ACT.Copy, scale=0.25 if i == 0 else 1.0).then_inc(wt_ok, 1)
            act.wait_ge(varok, 1)
            nc.scalar.activation(rstd[:, :], tmp[:, 0, :], ACT.Sqrt).then_inc(sdok, 1)

            def evac_qkv(e, n, dst, par):
                act.wait_ge(qkv_ps, n + 1)
                nc.scalar.copy(dst, p_qk[:, par, :])
                nc.scalar.copy(xv[:, bass.ds(e, 1), :], p_v[:, 0:D].unsqueeze(1)).then_inc(qk_ok, 1)

            def tiles(items):
                for i, (e, n, dst, par) in enumerate(items):
                    wait(act, xt_ps, n - 1)
                    nc.scalar.copy(stg[:, par:par + 1, :], xv[:, bass.ds(e, 1), :]).then_inc(staged, 1)
                    if i:
                        evac_qkv(*items[i - 1])
                    act.wait_ge(xt_ps, n + 1)
                    wait(act, qkv_ps, n - 1)
                    nc.scalar.copy(xT[:, par, :, :], p_x[:, par, 0:D].rearrange("p (c n) -> p c n", c=DC)).then_inc(xt_ok, 1)
                evac_qkv(*items[-1])

            act.wait_ge(mean_ok, 1)
            act.wait_ge(normed, EXT + 1)
            tiles([(E_FIRST, 0, qkz[:, :], 0), (E_MEAN, 1, qkb[:, 0, :], 1)]
                  + [(e, 2 + e, qkb[:, e, :], e % 2) for e in range(OLD)])

            def project(c, par):
                wait(act, s_done, c - 1)
                mine, other = SLOTS * par, SLOTS * (1 - par)
                if not isinstance(c, int) or c > 0:
                    act.wait_ge(qk_ok, PRO + CH * c)
                    nc.scalar.copy(qkb[:, mine:mine + OLD, :], qkb[:, other + CH:other + SLOTS, :])
                tiles([(CH * c + OLD + i, PRO + CH * c + i, qkb[:, mine + OLD + i, :], i % 2) for i in range(CH)])

            def rest(c):
                act.wait_ge(e_in, c + 1)
                nc.scalar.activation(e6[:, :, :], e6[:, :, :], ACT.Exp).then_inc(e_out, 1)
                wait(act, y_ok, c)
                for i in range(CH + 1):
                    if i < CH:
                        act.wait_ge(ct_ps, CH * c + i + 1)
                        wait(act, o_ps, CH * c + i - 1)
                        nc.scalar.copy(cT[:, i % 2, :, :], p_c[:, i % 2, 0:D].rearrange("p (c n) -> p c n", c=DC)).then_inc(ct_ok, 1)
                    if i > 0:
                        act.wait_ge(o_ps, CH * c + i)
                        nc.scalar.copy(ob[:, i - 1, :], p_o[:, 0:D]).then_inc(o_ok, 1)

            project(0, 0)
            project(1, 1)
            rest(0)
            with act.Fori(1, CHUNKS // 2) as g:
                project(2 * g, 0)
                rest(2 * g - 1)
                project(2 * g + 1, 1)
                rest(2 * g)
            rest(CHUNKS - 1)
            act.wait_ge(f_e, 1)
            nc.scalar.activation(first_e, first_e, ACT.Exp).then_inc(f_exp, 1)

        @block.vector
        def _(dve):
            ch = Chain(dve, dch)
            heads = lambda a: a.rearrange("p t (h c) -> p (t h) c", c=HD)
            dve.wait_ge(halo, 16 * (4 + TPB))
            for c in range(CHUNKS):
                dve.wait_ge(loaded[c], 16)
            with dve.Fori(0, EXT + 1) as e:
                ch.enter(e, 1)
                ch.mark(nc.vector.bn_stats(bn[:, bass.ds(e, 1), :].rearrange("p a n -> p (a n)"), xv[:, bass.ds(e, 1), :].rearrange("p a n -> p (a n)")))
            ch.leave(EXT + 1)
            ch.settle()
            ln_stats(nc, ch, bn, mean, tmp, varok)
            dve.wait_ge(sdok, 1)
            ch.then(nc.vector.reciprocal(rstd[:, :], rstd[:, :]))
            with dve.Fori(0, EXT + 1) as e:
                t = xv[:, bass.ds(e, 1), :].rearrange("p a n -> p (a n)")
                nc.vector.tensor_scalar(t, t, mean[:, bass.ds(e, 1)], rstd[:, bass.ds(e, 1)], ALU.subtract, ALU.mult).then_inc(normed, 1)
            dve.wait_ge(b_in, 64)
            ch.then(nc.vector.tensor_scalar(brow[0:1, 0, 0:D], brow[0:1, 0, 0:D], 0.25, None, ALU.mult))
            split3(nc, ch, brow, bpart, bsplit)
            dve.wait_ge(sum_ps, 1)
            nc.vector.tensor_scalar(xv[:, E_MEAN, :], p_v[:, 0:D], 1.0 / SEQ, None, ALU.mult).then_inc(mean_ok, 1)
            dve.wait_ge(tab_in, 32)
            dve.wait_ge(bias_in, 48)

            def chunk(c, par):
                s = SLOTS * par
                dve.wait_ge(qk_ok, PRO + CH * c + CH)
                q = qkb[:, s + REACH:s + REACH + CH, 0:D]
                for d in range(NOFF - 1):
                    ch.then(nc.vector.tensor_tensor(prd[:, :, :], q, qkb[:, s + d:s + d + CH, D:], ALU.mult))
                    ch.then(nc.vector.tensor_reduce(s6[:, :, d:d + 1], heads(prd[:, :, :]), AX.X, ALU.add))
                    if d == 1:
                        dve.wait_ge(pooled, 2 * c + 1)
                        nc.vector.tensor_reduce(s6[:, :, NOFF - 1:NOFF], heads(prp[:, :, :]), AX.X, ALU.add).then_inc(pool_red, 1)
                dve.wait_ge(pooled, 2 * c + 2)
                nc.vector.tensor_reduce(s0[:, bass.ds(c * CH, CH), :].rearrange("p t h -> p (t h)").unsqueeze(2), heads(prp[:, :, :]), AX.X, ALU.add).then_inc(pool_red, 1)
                dve.wait_ge(pool_red, 2 * c + 2)
                s64 = s6[:, :, :].rearrange("p (t h) o -> p t h o", h=HEADS)
                bias = band[:, bass.ds(c * CH, CH), :].unsqueeze(2).to_broadcast([P, CH, HEADS, NOFF])
                every = lambda a: a.unsqueeze(2).to_broadcast([P, CH * HEADS, NOFF])
                nc.vector.tensor_tensor(s64, s64, bias, ALU.add).then_inc(s_done, 1)
                dve.wait_ge(s_done, c + 1)
                ch.then(nc.vector.tensor_reduce(sm[:, 0, :].unsqueeze(2), s6[:, :, :], AX.X, ALU.max))
                wait(dve, g_pool, c)
                ch.mark(nc.vector.tensor_scalar(sm[:, 1, :], sm[:, 0, :], 0.0, None, ALU.is_lt))
                ch.then(nc.vector.tensor_scalar(sm[:, 2, :], sm[:, 0, :], 0.0, None, ALU.max))
                nc.vector.tensor_tensor(e6[:, :, :], s6[:, :, :], every(sm[:, 2, :]), ALU.subtract).then_inc(e_in, 1)
                dve.wait_ge(e_out, c + 1)
                ch.then(nc.vector.scalar_tensor_tensor(e6[:, :, :], s6[:, :, :], 0.0, e6[:, :, :], ALU.is_ge, ALU.mult))
                ch.then(nc.vector.tensor_reduce(sm[:, 3, :].unsqueeze(2), e6[:, :, :], AX.X, ALU.add))
                ch.then(nc.vector.tensor_tensor(sm[:, 3, :], sm[:, 3, :], sm[:, 1, :], ALU.add))
                ch.then(nc.vector.reciprocal(sm[:, 3, :], sm[:, 3, :]))
                nc.vector.tensor_tensor(e6[:, :, :], e6[:, :, :], every(sm[:, 3, :]), ALU.mult).then_inc(p_ok, 1)
                dve.wait_ge(p_ok, c + 1)
                wait(dve, ct_ps, CH * c)
                for d in range(OLD):
                    to = grp[0] if d == 0 else prd
                    v = heads(xv[:, bass.ds(CH * c + d, CH), :])
                    ch.then(nc.vector.tensor_tensor(heads(to[:, :, :]), v, e6[:, :, d:d + 1].to_broadcast([P, CH * HEADS, HD]), ALU.mult))
                    if d > 0:
                        add = nc.vector.tensor_tensor(grp[0][:, :, :], grp[0][:, :, :], prd[:, :, :], ALU.add)
                        if d < OLD - 1:
                            ch.then(add)
                        else:
                            add.then_inc(g_dve, 1)
                dve.wait_ge(g_dve, c + 1)

            n = ch.base + ch.n
            chunk(0, 0)
            per = 2 * (ch.base + ch.n - n)
            chunk(1, 1)
            with dve.Fori(0, CHUNKS // 2 - 1) as g:
                ch.enter(g, per)
                chunk(2 * g + 2, 0)
                chunk(2 * g + 3, 1)
            ch.leave(CHUNKS // 2 - 1)

            hT = lambda a: a.rearrange("p t h -> p h t")
            over_t = lambda a: a.unsqueeze(1).to_broadcast([P, TILES, HEADS])
            ch.then(nc.vector.tensor_tensor(s0[:, :, :], s0[:, :, :], fbias[:, :].unsqueeze(2).to_broadcast([P, TILES, HEADS]), ALU.add))
            nc.vector.tensor_reduce(r0[:, 0, :].unsqueeze(2), hT(s0[:, :, :]), AX.X, ALU.max).then_inc(f_den, 1)
            dve.wait_ge(f_tr, 1)
            ch.then(nc.vector.tensor_reduce(r0T[:, P:].unsqueeze(2), p_x[0:HEADS, 0, 0:P].rearrange("p (b g) -> p b g", g=TPB), AX.X, ALU.max))
            nc.vector.tensor_copy(r0T[:, 0:P].rearrange("p (b g) -> p b g", g=TPB), r0T[:, P:].unsqueeze(2).to_broadcast([HEADS, BATCH, TPB])).then_inc(f_trd, 1)
            dve.wait_ge(f_tr, 2)
            ch.mark(nc.vector.tensor_scalar(r0[:, 1, :], p_x[:, 1, 0:HEADS], 0.0, None, ALU.is_lt))
            ch.then(nc.vector.tensor_scalar(r0[:, 2, :], p_x[:, 1, 0:HEADS], 0.0, None, ALU.max))
            nc.vector.tensor_tensor(first_e, s0[:, :, :], over_t(r0[:, 2, :]), ALU.subtract).then_inc(f_e, 1)
            dve.wait_ge(f_exp, 1)
            flat = lambda a: a.rearrange("p t h -> p (t h)")
            ch.then(nc.vector.scalar_tensor_tensor(flat(s0[:, :, :]), flat(s0[:, :, :]), 0.0, flat(first_e), ALU.is_ge, ALU.mult))
            nc.vector.tensor_reduce(r0[:, 3, :].unsqueeze(2), hT(s0[:, :, :]), AX.X, ALU.add).then_inc(f_den, 1)
            dve.wait_ge(f_tr, 3)
            ch.then(nc.vector.tensor_tensor(r0[:, 4, :], p_x[:, 0, 0:HEADS], r0[:, 1, :], ALU.add))
            ch.then(nc.vector.reciprocal(r0[:, 4, :], r0[:, 4, :]))
            ch.then(nc.vector.tensor_tensor(s0[:, :, :], s0[:, :, :], over_t(r0[:, 4, :]), ALU.mult))
            with dve.Fori(0, CHUNKS) as c:
                dve.wait_ge(f_used, c)
                nc.vector.tensor_tensor(heads(prd[:, :, :]), heads(xv[:, bass.ds(CH * c + REACH, CH), :]),
                                        flat(s0[:, bass.ds(CH * c, CH), :]).unsqueeze(2).to_broadcast([P, CH * HEADS, HD]), ALU.mult).then_inc(f_prod, 1)
            dve.wait_ge(f_sum, 1)
            by_head = lambda a: a.rearrange("p (h c) -> p h c", c=HD)
            ch.then(nc.vector.tensor_tensor(by_head(prd[:, 0, :]), by_head(xv[:, E_MEAN, :]), r0[:, 1, :].unsqueeze(2).to_broadcast([P, HEADS, HD]), ALU.mult))
            nc.vector.tensor_tensor(prd[:, 0, :], prd[:, 0, :], p_v[:, 0:D], ALU.add).then_inc(f_ctx, 1)
            dve.wait_ge(f_tr, 4)
            nc.vector.tensor_copy(cT[:, 0, :, :], p_x[:, 1, 0:D].rearrange("p (c n) -> p c n", c=DC)).then_inc(f_ctx, 1)
            dve.wait_ge(f_tr, 5)
            dve.wait_ge(f_x, 16)
            nc.vector.tensor_tensor(ob[:, 1, :], p_o[:, 0:D], ob[:, 0, :], ALU.add).then_inc(f_y, 1)

        @block.tensor
        def _(pe):
            mm = nc.tensor.matmul
            pe.wait_ge(const, 6)
            pe.wait_ge(w_in, 64)
            for i in range(4):
                dst = (p_x[:, 0, :], p_x[:, 1, :], p_qk[:, 0, :], p_qk[:, 1, :])[i]
                for c in range(DC):
                    for o in range(DC):
                        last = nc.tensor.transpose(dst[:, c * D + o * P:c * D + (o + 1) * P], wn[:, i, o, c * P:(c + 1) * P], ident[:, :])
                last.then_inc(wt_ps, 1)
            pe.wait_ge(normed, REACH + 1)
            mm(p_v[:, 0:D], blk[:, :], xv[:, REACH, :], start=True, stop=False)
            with pe.Fori(REACH + 1, REACH + TILES - 1) as e:
                pe.wait_ge(normed, e + 1)
                mm(p_v[:, 0:D], blk[:, :], xv[:, bass.ds(e, 1), :].rearrange("p a n -> p (a n)"), start=False, stop=False)
            pe.wait_ge(normed, REACH + TILES)
            mm(p_v[:, 0:D], blk[:, :], xv[:, REACH + TILES - 1, :], start=False, stop=True).then_inc(sum_ps, 1)
            pe.wait_ge(wt_ok, 4)
            pe.wait_ge(bias_in, 48)

            def matmuls(n, par):
                pe.wait_ge(xt_ok, n + 1)
                wait(pe, qk_ok, n)
                for lo, hi, dst in ((0, 2 * D, p_qk[:, par, :]), (2 * D, 3 * D, p_v[:, 0:D])):
                    for c in range(DC):
                        mm(dst, xT[:, par, c, :], wT[:, c, lo:hi], start=c == 0, stop=False)
                    last = mm(dst, ones_bf[:, :], bias3[:, lo:hi], start=False, stop=True)
                last.then_inc(qkv_ps, 1)

            def tiles(items):
                for i, (n, par) in enumerate(items):
                    pe.wait_ge(staged, n + 1)
                    wait(pe, xt_ok, n - 1)
                    for c in range(DC):
                        last = nc.tensor.transpose(p_x[:, par, c * P:(c + 1) * P], stg[:, par, c * P:(c + 1) * P], ident[:, :])
                    last.then_inc(xt_ps, 1)
                    if i:
                        matmuls(*items[i - 1])
                matmuls(*items[-1])

            def project(c):
                tiles([(PRO + CH * c + i, i % 2) for i in range(CH)])

            def rest(c):
                pe.wait_ge(g_dve, c + 1)
                pe.wait_ge(g_pool, c + 1)
                for i in range(CH + 1):
                    if i < CH:
                        wait(pe, ct_ok, CH * c + i - 1)
                        for k in range(DC):
                            for g in range(2):
                                last = mm(p_c[:, i % 2, k * P:(k + 1) * P], grp[g][:, i, k * P:(k + 1) * P], ident[:, :], start=g == 0, stop=g == 1)
                        last.then_inc(ct_ps, 1)
                    if i > 0:
                        pe.wait_ge(ct_ok, CH * c + i)
                        wait(pe, o_ok, CH * c + i - 1)
                        out_product((i - 1) % 2).then_inc(o_ps, 1)

            def out_product(par):
                for k in range(DC):
                    mm(p_o[:, 0:D], cT[:, par, k, :], wT[:, k, 3 * D:], start=k == 0, stop=False)
                return mm(p_o[:, 0:D], ones_bf[:, :], bias3[:, 3 * D:], start=False, stop=True)

            tiles([(i, i % 2) for i in range(PRO)])
            project(0)
            project(1)
            rest(0)
            with pe.Fori(1, CHUNKS // 2) as g:
                project(2 * g)
                rest(2 * g - 1)
                project(2 * g + 1)
                rest(2 * g)
            rest(CHUNKS - 1)
            pe.wait_ge(f_den, 1)
            nc.tensor.transpose(p_x[0:HEADS, 0, 0:P], r0[:, 0, :], ident[:, :]).then_inc(f_tr, 1)
            pe.wait_ge(f_trd, 1)
            nc.tensor.transpose(p_x[:, 1, 0:HEADS], r0T[:, 0:P], ident[0:HEADS, 0:HEADS]).then_inc(f_tr, 1)
            pe.wait_ge(f_den, 2)
            mm(p_x[:, 0, 0:HEADS], blk[:, :], r0[:, 3, :], start=True, stop=True).then_inc(f_tr, 1)

            def first_sum(first, last):
                for i in range(CH):
                    ins = mm(p_v[:, 0:D], blk[:, :], prd[:, i, :], start=first and i == 0, stop=last and i == CH - 1)
                return ins

            pe.wait_ge(f_prod, 1)
            first_sum(True, False).then_inc(f_used, 1)
            with pe.Fori(1, CHUNKS - 1) as c:
                pe.wait_ge(f_prod, c + 1)
                first_sum(False, False).then_inc(f_used, 1)
            pe.wait_ge(f_prod, CHUNKS)
            first_sum(False, True).then_inc(f_sum, 1)
            pe.wait_ge(f_ctx, 1)
            for k in range(DC):
                last = nc.tensor.transpose(p_x[:, 1, k * P:(k + 1) * P], prd[:, 0, k * P:(k + 1) * P], ident[:, :])
            last.then_inc(f_tr, 1)
            pe.wait_ge(f_ctx, 2)
            pe.wait_ge(o_ok, TILES)
            out_product(0).then_inc(f_tr, 1)


def ln_stats(nc, ch, bn, mean, tmp, done):
    half = lambda i: bn[:, :, i]
    ch.mark(nc.vector.tensor_tensor(mean[:, :], half(1), half(4), ALU.add))
    ch.mark(nc.vector.tensor_tensor(tmp[:, 0, :], half(2), half(5), ALU.add))
    ch.then(nc.vector.tensor_tensor(tmp[:, 1, :], half(1), half(4), ALU.subtract))
    ch.mark(nc.vector.tensor_scalar(mean[:, :], mean[:, :], 0.5, None, ALU.mult))
    ch.mark(nc.vector.tensor_scalar(tmp[:, 0, :], tmp[:, 0, :], 1.0 / D, EPS, ALU.mult, ALU.add))
    ch.then(nc.vector.tensor_tensor(tmp[:, 1, :], tmp[:, 1, :], tmp[:, 1, :], ALU.mult))
    nc.vector.scalar_tensor_tensor(tmp[:, 0, :], tmp[:, 1, :], 0.25, tmp[:, 0, :], ALU.mult, ALU.add).then_inc(done, 1)


def split3(nc, ch, rest, part, done):
    for i in range(3):
        copy = nc.vector.tensor_copy(part[:, i, :], rest[:, i % 2, :])
        if i == 2:
            copy.then_inc(done, 1)
        else:
            ch.then(copy)
            ch.then(nc.vector.tensor_tensor(rest[:, 1 - i % 2, :], rest[:, i % 2, :], part[:, i, :], ALU.subtract))


def band_tables(np):
    tok = np.arange(N_TOK).reshape(P, TILES)
    i = (tok % SEQ).astype(np.float32)
    bias = lambda diff: (np.exp(np.float32(-0.5) * (diff / np.float32(2.0)) ** 2)
                         + np.cos(np.float32(2.0 * np.pi) * diff / np.float32(401.0))).astype(np.float32)
    table = np.full((P, TILES, NOFF), -1e9, np.float32)
    for d in range(NOFF - 1):
        j = i + d - REACH
        table[:, :, d] = np.where((j >= 0) & (j < SEQ), bias(i - j), np.float32(-1e9))
    table[:, :, NOFF - 1] = np.where(i > REACH, bias(i), np.float32(-1e9))
    return table, bias(i)


EXPERTS, FF = 16, 1024
CAP = N_TOK // EXPERTS
FC = FF // P
ET = CAP // P
RING = 8
GT = 4
GROUPS = TILES // GT


def stage_moe(nc, name, x, wg, w1, w2, tok, rows, answers, out, zero_rows):
    x_v = x.rearrange("(t p) n -> p t n", p=P)
    o_v = out.rearrange("(t p) n -> p t n", p=P)
    rows_v = rows[0:N_TOK, :].rearrange("(e p c) n -> e p (c n)", p=P, c=ET)
    ans_v = answers.rearrange("(e p c) n -> e p (c n)", p=P, c=ET)
    w1_v = w1.rearrange("e (c p) f -> e p c f", p=P)
    w2_v = w2.rearrange("e (j p) n -> e p j n", p=P)
    with Stage(nc, name) as st:
        sb, ps, sem = st.sb, st.ps, st.sem
        xn = sb("xn", [P, TILES, D])
        ident = sb("ident", [P, P])
        before = sb("before", [P, P], BF16)
        ones = sb("ones", [P, P], BF16)
        wg_s = sb("wg", [P, DC, EXPERTS])
        bn = sb("bn", [P, TILES, 6])
        mean = sb("mean", [P, TILES])
        rstd = sb("rstd", [P, TILES])
        tmp = sb("tmp", [P, 2, TILES])
        toks = sb("toks", [P, TILES])
        enum = sb("enum", [P, EXPERTS])
        stg = sb("stg", [P, 2, GT, D])
        xT = sb("xT", [P, 2, DC, GT * P])
        route = sb("route", [P, 8, TILES])
        slot = sb("slot", [P, 2, TILES], U32)
        w1_s = sb("w1", [P, 2, DC, FF])
        w2_s = sb("w2", [P, 2, FC, D])
        xe = sb("xe", [P, 2, ET, D])
        xeT = sb("xeT", [P, DC, CAP])
        hT = sb("hT", [P, FC, CAP])
        ye = sb("ye", [P, 2, ET, D])
        xo = sb("xo", [P, 2, RING, D])
        lg = hT[:, 0:2, :].rearrange("p a (t e) -> p (a t) e", e=EXPERTS)
        ex = hT[:, 2:4, :].rearrange("p a (t e) -> p (a t) e", e=EXPERTS)
        loc = hT[:, 4:6, :].rearrange("p a (t e) -> p (a t) e", e=EXPERTS)
        tot = xeT[:, :, :].rearrange("p a (e t) -> p (a e) t", t=TILES)
        run_ = hT[:, 6:8, :].rearrange("p a (e t) -> p (a e) t", t=TILES)
        keep = w1_s[:, 0, 0, :].rearrange("p (e t) -> p e t", t=TILES)
        hot = w1_s[:, 0, 1, 0:512].bitcast(BF16).rearrange("p (t e) -> p t e", e=EXPERTS)

        p_x = ps("p_x", [P, 2, DC, 512])
        p_h = ps("p_h", [P, 2, 512])
        p_y = ps("p_y", [P, 2, 512])

        loaded = [sem(f"loaded{c}") for c in range(CHUNKS)]
        gathered = [sem(f"gathered{k}") for k in range(RING)]
        (const, wg_in, varok, sdok, normed, staged, xt_ps, xt_ok, lg_ps, lg_ok, ex_in, ex_out,
         hot_ok, cum_ps, slots_ok, zeroed, scattered, xet_ps, xet_act, xet_dve, h_ps, h_act, h_dve,
         y_ps, y_act, y_dve, xo_ok, dch, pch) = [sem(n) for n in (
             "const wg_in varok sdok normed staged xt_ps xt_ok lg_ps lg_ok ex_in ex_out "
             "hot_ok cum_ps slots_ok zeroed scattered xet_ps xet_act xet_dve h_ps h_act "
             "h_dve y_ps y_act y_dve xo_ok dve_chain pool_chain ").split()]
        w_in, xe_in, xo_in, ans_out, x_out = [[sem(f"{n}{k}") for k in range(2)] for n in ("w_in", "xe_in", "xo_in", "ans_out", "x_out")]
        block = st.ctx.enter_context(nc.Block())

        @block.sync
        def _(sp):
            for c in range(CHUNKS):
                sp.dma_start(xn[:, c * CH:(c + 1) * CH, :], x_v[:, c * CH:(c + 1) * CH, :]).then_inc(loaded[c], 16)
            if zero_rows:
                sp.wait_ge(const, 1)
                for e in range(EXPERTS):
                    sp.dma_start(rows_v[e], ye[:, 0, :, :].rearrange("p a n -> p (a n)")).then_inc(zeroed, 16)

            def expert_in(e, par):
                sp.dma_start(w1_s[:, par, :, :].unsqueeze(1), w1_v[bass.ds(e, 1)].rearrange("e p c f -> p e c f")).then_inc(w_in[par], 16)
                sp.dma_start(w2_s[:, par, :, :].unsqueeze(1), w2_v[bass.ds(e, 1)].rearrange("e p j n -> p e j n")).then_inc(w_in[par], 16)
                sp.dma_start(xe[:, par, :, :].rearrange("p a n -> p (a n)").unsqueeze(1), rows_v[bass.ds(e, 1)].rearrange("e p n -> p e n")).then_inc(xe_in[par], 16)

            def expert_out(e, par):
                sp.wait_ge(y_act, ET // 2 * e + ET // 2)
                sp.wait_ge(y_dve, ET // 2 * e + ET // 2)
                sp.dma_start(ans_v[bass.ds(e, 1)].rearrange("e p n -> p e n"), ye[:, par, :, :].rearrange("p a n -> p (a n)").unsqueeze(1)).then_inc(ans_out[par], 16)

            sp.wait_ge(scattered, 16 * TILES)
            expert_in(0, 0)
            expert_in(1, 1)
            with sp.Fori(0, EXPERTS // 2 - 1) as g:
                for par in range(2):
                    expert_out(2 * g + par, par)
                    expert_in(2 * g + 2 + par, par)
            for par in range(2):
                expert_out(EXPERTS - 2 + par, par)
            def res_in(r, par):
                sp.dma_start(xo[:, par, :, :], x_v[:, bass.ds(r * RING, RING), :]).then_inc(xo_in[par], 16)

            def res_out(r, par):
                sp.wait_ge(xo_ok, RING * r + RING)
                sp.dma_start(o_v[:, bass.ds(r * RING, RING), :], xo[:, par, :, :]).then_inc(x_out[par], 16)

            rounds = TILES // RING
            res_in(0, 0)
            res_in(1, 1)
            with sp.Fori(0, rounds // 2 - 1) as g:
                for par in range(2):
                    res_out(2 * g + par, par)
                    sp.wait_ge(x_out[par], g * 16 + 16)
                    res_in(2 * g + 2 + par, par)
            for par in range(2):
                res_out(rounds - 2 + par, par)
                sp.wait_ge(x_out[par], 16 * rounds // 2)

        @block.gpsimd
        def _(pool):
            ch = Chain(pool, pch)
            pool.memset(ye[:, 0, :, :], 0.0).then_inc(const, 1)
            pool.dma_start(wg_s[:, :, :], wg.rearrange("(c p) n -> p c n", p=P)).then_inc(wg_in, 16)
            pool.dma_start(toks[:, :], tok[:, 0:TILES]).then_inc(wg_in, 16)
            pool.dma_start(enum[:, :], tok[:, TILES:TILES + EXPERTS]).then_inc(wg_in, 16)
            ch.mark(pool.memset(ident[:, :], 0.0))
            ch.mark(pool.memset(before[:, :], 1.0))
            ch.then(pool.memset(ones[:, :], 1.0))
            pool.affine_select(out=ident[:, :], in_=ident[:, :], compare_op=ALU.not_equal, fill=1.0,
                               base=0, pattern=[[-1, P]], channel_multiplier=1).then_inc(const, 1)
            pool.affine_select(out=before[:, :], in_=before[:, :], compare_op=ALU.is_gt, fill=0.0,
                               base=0, pattern=[[1, P]], channel_multiplier=-1).then_inc(const, 1)
            def stage(g, par):
                pool.wait_ge(normed, GT * g + GT)
                wait(pool, xt_ps, g - 1)
                pool.tensor_copy(stg[:, par, :, :], xn[:, bass.ds(GT * g, GT), :]).then_inc(staged, 1)

            stage(0, 0)
            stage(1, 1)
            with pool.Fori(1, GROUPS // 2) as i:
                stage(2 * i, 0)
                stage(2 * i + 1, 1)
            pool.wait_ge(slots_ok, 1)
            if zero_rows:
                pool.wait_ge(zeroed, 16 * EXPERTS)
            for t in range(TILES):
                pool.indirect_dma_start(rows[:, :], bass.IndirectOffsetOnAxis(ap=slot[:, 0, t:t + 1], axis=0), xn[:, t, :], None).then_inc(scattered, 16)
            pool.wait_ge(scattered, 16 * TILES)
            for par in range(2):
                pool.wait_ge(ans_out[par], 16 * EXPERTS // 2)
            for t in range(TILES):
                if t >= RING:
                    pool.wait_ge(gathered[t % RING], 16 * (t // RING))
                pool.indirect_dma_start(xn[:, t, :], None, answers[:, :], bass.IndirectOffsetOnAxis(ap=slot[:, 1, t:t + 1], axis=0)).then_inc(gathered[t % RING], 16)

        @block.scalar
        def _(act):
            act.wait_ge(varok, 1)
            nc.scalar.activation(rstd[:, :], tmp[:, 0, :], ACT.Sqrt).then_inc(sdok, 1)

            def turned(g, par):
                act.wait_ge(xt_ps, g + 1)
                wait(act, lg_ps, g - 1)
                nc.scalar.copy(xT[:, par, :, :], p_x[:, par, :, :]).then_inc(xt_ok, 1)

            def logits(g, par):
                act.wait_ge(lg_ps, g + 1)
                nc.scalar.copy(lg[:, bass.ds(GT * g, GT), :], p_h[:, par, 0:GT * EXPERTS].rearrange("p (t e) -> p t e", e=EXPERTS)).then_inc(lg_ok, 1)

            turned(0, 0)
            turned(1, 1)
            logits(0, 0)
            with act.Fori(1, GROUPS // 2) as i:
                turned(2 * i, 0)
                logits(2 * i - 1, 1)
                turned(2 * i + 1, 1)
                logits(2 * i, 0)
            logits(GROUPS - 1, 1)
            act.wait_ge(ex_in, 1)
            nc.scalar.activation(ex, ex, ACT.Exp).then_inc(ex_out, 1)
            act.wait_ge(slots_ok, 1)

            def tokens(e, par):
                act.wait_ge(xet_ps, e + 1)
                nc.scalar.copy(xeT[:, 0, :], p_x[:, par, 0, :]).then_inc(xet_act, 1)

            def hidden(e):
                for j in range(0, FC, 2):
                    act.wait_ge(h_ps, FC * e + j + 1)
                    nc.scalar.activation(hT[:, j, :], p_h[:, 0, :], ACT.Relu).then_inc(h_act, 1)

            def answers_(e, par, half):
                wait(act, ans_out[par], 16 * half)
                for c in range(0, ET, 2):
                    act.wait_ge(y_ps, ET * e + c + 1)
                    nc.scalar.copy(ye[:, par, c, :], p_y[:, 0, 0:D]).then_inc(y_act, 1)

            expert_order(act, tokens, answers_, hidden)

        @block.vector
        def _(dve):
            ch = Chain(dve, dch)
            flat = lambda a: a.rearrange("p a n -> p (a n)")
            for c in range(CHUNKS):
                dve.wait_ge(loaded[c], 16)
                with dve.Fori(c * CH, c * CH + CH) as t:
                    ch.enter(t - c * CH, 1)
                    ch.mark(nc.vector.bn_stats(flat(bn[:, bass.ds(t, 1), :]), flat(xn[:, bass.ds(t, 1), :])))
                ch.leave(CH)
            ch.settle()
            ln_stats(nc, ch, bn, mean, tmp, varok)
            dve.wait_ge(sdok, 1)
            ch.then(nc.vector.reciprocal(rstd[:, :], rstd[:, :]))
            with dve.Fori(0, TILES) as t:
                x_t = flat(xn[:, bass.ds(t, 1), :])
                nc.vector.tensor_scalar(x_t, x_t, mean[:, bass.ds(t, 1)], rstd[:, bass.ds(t, 1)], ALU.subtract, ALU.mult).then_inc(normed, 1)
            dve.wait_ge(wg_in, 48)
            ch.mark(nc.vector.memset(keep, 1.0))
            ch.settle()
            ch.mark(nc.vector.memset(keep[:, :, 0:1], 0.0))
            dve.wait_ge(lg_ok, GROUPS)
            best, rden, idx, place, valid, gate, at, miss = (route[:, i, :] for i in range(8))
            by_tok = lambda a: a.unsqueeze(2).to_broadcast([P, TILES, EXPERTS])
            by_exp = enum[:, :].unsqueeze(1).to_broadcast([P, TILES, EXPERTS])
            one = lambda a: a.unsqueeze(2)
            V = nc.vector
            ch.then(V.tensor_reduce(one(best), lg, AX.X, ALU.max))
            V.tensor_tensor(ex, lg, by_tok(best), ALU.subtract).then_inc(ex_in, 1)
            dve.wait_ge(ex_out, 1)
            ch.then(V.tensor_reduce(one(rden), ex, AX.X, ALU.add))
            ch.mark(V.reciprocal(rden, rden))
            ch.then(V.tensor_tensor(ex, lg, by_tok(best), ALU.is_ge))
            ch.then(V.scalar_tensor_tensor(ex, ex, -float(EXPERTS), by_exp, ALU.mult, ALU.add))
            ch.then(V.tensor_reduce(one(idx), ex, AX.X, ALU.min))
            ch.then(V.tensor_scalar(idx, idx, float(EXPERTS), None, ALU.add))
            ch.then(V.tensor_tensor(ex, by_exp, by_tok(idx), ALU.is_equal))
            V.tensor_copy(hot, ex).then_inc(hot_ok, 1)
            dve.wait_ge(cum_ps, 1)
            turn = lambda a: a.rearrange("p t e -> p e t")
            in_tiles = lambda a: a.rearrange("p a (t e) -> p (a t) e", e=EXPERTS)
            ch.then(V.tensor_copy(tot, turn(in_tiles(p_x[:, 1, :, :]))))
            ch.then(V.tensor_tensor_scan(flat(run_), flat(keep), flat(tot), 0.0, ALU.mult, ALU.add))
            ch.then(V.tensor_tensor(run_, run_, tot, ALU.subtract))
            ch.then(V.tensor_tensor(loc, in_tiles(p_x[:, 0, :, :]), turn(run_), ALU.add))
            ch.then(V.tensor_tensor(loc, loc, ex, ALU.mult))
            ch.then(V.tensor_reduce(one(place), loc, AX.X, ALU.add))
            ch.mark(V.tensor_scalar(valid, place, float(CAP), None, ALU.is_lt))
            ch.mark(V.scalar_tensor_tensor(at, idx, float(CAP), place, ALU.mult, ALU.add))
            ch.then(V.tensor_scalar(place, place, float(CAP - 1), None, ALU.min))
            ch.mark(V.tensor_tensor(gate, rden, valid, ALU.mult))
            ch.mark(V.tensor_tensor(miss, at, toks[:, :], ALU.subtract))
            ch.then(V.scalar_tensor_tensor(place, idx, float(CAP), place, ALU.mult, ALU.add))
            ch.mark(V.tensor_copy(slot[:, 1, :], place))
            ch.then(V.tensor_tensor(miss, miss, valid, ALU.mult))
            ch.then(V.tensor_tensor(miss, miss, toks[:, :], ALU.add))
            V.tensor_copy(slot[:, 0, :], miss).then_inc(slots_ok, 1)

            def tokens(e, par):
                dve.wait_ge(xet_ps, e + 1)
                V.tensor_copy(xeT[:, 1, :], p_x[:, par, 1, :]).then_inc(xet_dve, 1)

            def hidden(e):
                for j in range(1, FC, 2):
                    dve.wait_ge(h_ps, FC * e + j + 1)
                    V.tensor_scalar(hT[:, j, :], p_h[:, 1, :], 0.0, None, ALU.max).then_inc(h_dve, 1)

            def answers_(e, par, half):
                wait(dve, ans_out[par], 16 * half)
                for c in range(1, ET, 2):
                    dve.wait_ge(y_ps, ET * e + c + 1)
                    V.tensor_copy(ye[:, par, c, :], p_y[:, 1, 0:D]).then_inc(y_dve, 1)

            expert_order(dve, tokens, answers_, hidden)

            def combine(r, par, i):
                dve.wait_ge(xo_in[par], i * 16 + 16)
                for k in range(RING):
                    dve.wait_ge(gathered[k], 16 * r + 16)
                    x_t = xo[:, par, k, :]
                    V.scalar_tensor_tensor(x_t, flat(xn[:, bass.ds(r * RING + k, 1), :]), route[:, 5, bass.ds(r * RING + k, 1)], x_t, ALU.mult, ALU.add).then_inc(xo_ok, 1)

            with dve.Fori(0, TILES // RING // 2) as i:
                combine(2 * i, 0, i)
                combine(2 * i + 1, 1, i)

        @block.tensor
        def _(pe):
            mm = nc.tensor.matmul
            pe.wait_ge(const, 3)
            pe.wait_ge(wg_in, 48)

            def turned(g, par):
                pe.wait_ge(staged, g + 1)
                wait(pe, xt_ok, g - 1)
                for c in range(DC):
                    for i in range(GT):
                        last = nc.tensor.transpose(p_x[:, par, c, i * P:(i + 1) * P], stg[:, par, i, c * P:(c + 1) * P], ident[:, :])
                last.then_inc(xt_ps, 1)

            def logits(g, par):
                pe.wait_ge(xt_ok, g + 1)
                wait(pe, lg_ok, g - 1)
                for i in range(GT):
                    for c in range(DC):
                        last = mm(p_h[:, par, i * EXPERTS:(i + 1) * EXPERTS], xT[:, par, c, i * P:(i + 1) * P], wg_s[:, c, :], start=c == 0, stop=c == DC - 1)
                last.then_inc(lg_ps, 1)

            turned(0, 0)
            turned(1, 1)
            logits(0, 0)
            with pe.Fori(1, GROUPS // 2) as i:
                turned(2 * i, 0)
                logits(2 * i - 1, 1)
                turned(2 * i + 1, 1)
                logits(2 * i, 0)
            logits(GROUPS - 1, 1)
            pe.wait_ge(hot_ok, 1)
            half = TILES // 2
            for k, m in enumerate((before, ones)):
                for c in range(2):
                    last = mm(p_x[:, k, c, :], m[:, :], hot[:, c * half:(c + 1) * half, :].rearrange("p t e -> p (t e)"), start=True, stop=True)
            last.then_inc(cum_ps, 1)
            pe.wait_ge(slots_ok, 1)

            def tokens(e, par, half=None):
                half = e // 2 if half is None else half
                pe.wait_ge(xe_in[par], 16 * half + 16)
                for c in range(DC):
                    for i in range(ET):
                        last = nc.tensor.transpose(p_x[:, par, c, i * P:(i + 1) * P], xe[:, par, i, c * P:(c + 1) * P], ident[:, :])
                last.then_inc(xet_ps, 1)

            def hidden(e, par, half):
                pe.wait_ge(w_in[par], 32 * half + 32)
                pe.wait_ge(xet_act, e + 1)
                pe.wait_ge(xet_dve, e + 1)
                for j in range(FC):
                    wait(pe, (h_act, h_dve)[j % 2], FC // 2 * e + j // 2)
                    for c in range(DC):
                        last = mm(p_h[:, j % 2, :], w1_s[:, par, c, j * P:(j + 1) * P], xeT[:, c, :], start=c == 0, stop=c == DC - 1)
                    last.then_inc(h_ps, 1)

            def answers_(e, par):
                pe.wait_ge(h_act, FC // 2 * e + FC // 2)
                pe.wait_ge(h_dve, FC // 2 * e + FC // 2)
                for c in range(ET):
                    wait(pe, (y_act, y_dve)[c % 2], ET // 2 * e + c // 2)
                    for j in range(FC):
                        last = mm(p_y[:, c % 2, 0:D], hT[:, j, c * P:(c + 1) * P], w2_s[:, par, j, :], start=j == 0, stop=j == FC - 1)
                    last.then_inc(y_ps, 1)

            tokens(0, 0)
            hidden(0, 0, 0)
            with pe.Fori(0, EXPERTS // 2 - 1) as i:
                tokens(2 * i + 1, 1, i)
                answers_(2 * i, 0)
                hidden(2 * i + 1, 1, i)
                tokens(2 * i + 2, 0, i + 1)
                answers_(2 * i + 1, 1)
                hidden(2 * i + 2, 0, i + 1)
            e = EXPERTS - 1
            tokens(e, 1)
            answers_(e - 1, 0)
            hidden(e, 1, e // 2)
            answers_(e, 1)


def expert_order(eng, tokens, answers_, hidden):
    tokens(0, 0)
    hidden(0)
    with eng.Fori(0, EXPERTS // 2 - 1) as i:
        tokens(2 * i + 1, 1)
        answers_(2 * i, 0, i)
        hidden(2 * i + 1)
        tokens(2 * i + 2, 0)
        answers_(2 * i + 1, 1, i)
        hidden(2 * i + 2)
    e = EXPERTS - 1
    tokens(e, 1)
    answers_(e - 1, 0, e // 2)
    hidden(e)
    answers_(e, 1, e // 2)


def token_table(np):
    t = N_TOK + np.arange(TILES)[None, :] * P + np.arange(P)[:, None]
    return np.concatenate([t, np.tile(np.arange(EXPERTS), (P, 1))], 1).astype(np.float32)


BT = SEQ // P
POL = 3
SPLIT_Q = (0, 0, 0, 1, 1, 2)
SPLIT_K = (0, 1, 2, 0, 1, 0)
KR = len(SPLIT_Q) * HD
KM = KR + 3
VW = HD + 1
MASKED = -1e30
SPAN = (0, 512, 1024, 896)
WIDTH = 1280


def stage_b(nc, x, wq, bq, wk, bk, wv, bv, wo, bo, pw1, pb1, pw2, pb2, sw1, sb1, sw2, sb2, parts, out):
    x_v = x.rearrange("(t p) n -> p t n", p=P)
    o_v = out.rearrange("(t p) n -> p t n", p=P)
    w_view = parts.rearrange("s i j p n -> s p (i j) n")
    r_view = parts.rearrange("s i (w c) (h d) n -> s i w d (c h) n", c=DC, d=HD)
    with Stage(nc, "b") as st:
        sb, ps, sem = st.sb, st.ps, st.sem
        xn = sb("xn", [P, TILES, D])
        qs = sb("qs", [P, 2, HEADS, SEQ], BF16)
        ks = sb("ks", [P, 2, HEADS, SEQ], BF16)
        ident = sb("ident", [P, P])
        ident_b = sb("ident_b", [P, P], BF16)
        ones_b = sb("ones_b", [P, P], BF16)
        ones = sb("ones", [P, P])
        after = sb("after", [P, P])
        mask_s = sb("mask_s", [P, P], BF16)
        mask_t = sb("mask_t", [P, P], BF16)
        wT = sb("wT", [P, DC, 4 * D])
        bias3 = sb("bias3", [P, D], BF16)
        bvb = sb("bvb", [P, D])
        bcol = sb("bcol", [P, 4])
        stg = sb("stg", [P, BT, D])
        xT = sb("xT", [P, DC, SEQ])
        qf = sb("qf", [P, 4, SEQ])
        qp = sb("qp", [P, 3, 4, SEQ], BF16)
        vw = sb("vw", [P, BT, D])
        va = sb("va", [P, 2, BT, HEADS, VW])
        suf = sb("suf", [P, BT, HEADS, VW])
        ob = sb("ob", [P, HEADS, BT, VW])
        cx = sb("cx", [P, BT, D])
        pt = sb("pt", [P, 2, WIDTH])
        mneg = sb("mneg", [P, 2, HEADS, BT])
        mrest = sb("mrest", [P, 2, HEADS * BT])
        mpart = sb("mpart", [P, 4, HEADS * BT], BF16)
        mT = sb("mT", [P, 2, P], BF16)
        wm = sb("wm", [P, HEADS, BT])
        rd = sb("rd", [P, HEADS, BT])
        gq = sb("gq", [P, DC, BATCH])
        ng = sb("ng", [P, BATCH, HEADS])
        bn = pt[:, 0, 0:6 * TILES].rearrange("p (t n) -> p t n", n=6)
        mean = sb("mean", [P, TILES])
        rstd = sb("rstd", [P, TILES])
        tmp = qf[:, 0, 0:2 * TILES].rearrange("p (a n) -> p a n", a=2)
        mean_sq = tmp[:, 0, :]
        f32 = lambda a: a.rearrange("p h n -> p (h n)").bitcast(F32)
        wn = f32(qs[:, 0, :, :])[:, 0:8 * D].rearrange("p (w o n) -> p w o n", w=4, o=DC)
        hn = f32(qs[:, 0, :, :])[:, 8 * D:12 * D].rearrange("p (w n) -> p w n", w=4)
        hT_ = f32(qs[:, 1, :, :])[:, 0:8 * P].rearrange("p (w c n) -> p w c n", w=4, c=DC)
        pool_ = f32(qs[:, 1, :, :])[:, 8 * P:]
        take = lambda lo, n, parts_=P: pool_[0:parts_, lo:lo + n]
        sel = take(0, 31)
        hb = take(32, 4)
        w2n = take(64, P, POL * HEADS)
        s2n = take(192, P, POL)
        w2T = take(320, POL * HEADS + POL)
        xm = take(384, D, BATCH)
        xmT = take(640, DC * BATCH).rearrange("p (c b) -> p c b", c=DC)
        hid = take(680, 4 * BATCH).rearrange("p (w b) -> p w b", w=4)
        b2 = take(760, POL * HEADS + POL, BATCH)
        gl = take(820, POL * HEADS, BATCH).rearrange("p (a h) -> p a h", a=POL)
        pl = take(880, POL, BATCH)
        gs = take(890, 8, BATCH)
        gate = take(900, HEADS, BATCH)
        gch = take(920, D, BATCH)
        gdiag = take(1180, BATCH * HEADS, BATCH).rearrange("p (b h) -> p b h", b=BATCH)
        brow = f32(ks[:, 0, :, :])[0:1, 0:2 * D].rearrange("p (a n) -> p a n", a=2)
        bpart = ks[0:1, 1, 0:3, 0:D]

        p_s = ps("p_s", [P, 3, 512])
        p_t = ps("p_t", [P, 3, 512])
        p_p = ps("p_p", [P, 2, 512])

        loaded = [sem(f"loaded{c}") for c in range(CHUNKS)]
        names = ("const w_in b_in g_in varok sdok normed wt_ps wt_ok bsplit bias_in mean_ps mean_ok mlp_ps mlp_ok "
                 "gate_ps gate_ok gelu e_in e_out free_ok staged xt_ps xt_ok qk_ps qk_ev qk_hi q_parts v_ps v_ev va_ok "
                 "suf_ps suf_ev ct_ps ct_ok ctx_ok o_ps o_ev s_ps smax t_ps exp_ev pv_ps pv_ev m_ok mt_ps mt_ok "
                 "m_in parts_out xr_in x_out w_ready w_exp ld_free dch pch").split()
        S_ = {n: sem(n) for n in names}
        (const, w_in, b_in, g_in, varok, sdok, normed, wt_ps, wt_ok, bsplit, bias_in, mean_ps, mean_ok, mlp_ps, mlp_ok,
         gate_ps, gate_ok, gelu, e_in, e_out, free_ok, staged, xt_ps, xt_ok, qk_ps, qk_ev, qk_hi, q_parts, v_ps, v_ev, va_ok,
         suf_ps, suf_ev, ct_ps, ct_ok, ctx_ok, o_ps, o_ev, s_ps, smax, t_ps, exp_ev, pv_ps, pv_ev, m_ok, mt_ps, mt_ok,
         m_in, parts_out, xr_in, x_out, w_ready, w_exp, ld_free, dch, pch) = [S_[n] for n in names]
        stacked = [[sem(f"stacked{par}_{g}") for g in range(2)] for par in range(2)]
        block = st.ctx.enter_context(nc.Block())
        flat = lambda a: a.rearrange("p a n -> p (a n)")
        H3, M2 = 3 * HEADS, 2
        GH = HEADS // 2

        def steps(eng, step, ch=None, marks=0):
            step(0, 0, proj=True, s=False, t=False, fin=False)
            step(1, 1, proj=True, s=True, t=False, fin=False)
            step(2, 0, proj=True, s=True, t=True, fin=False)
            with eng.Fori(0, (BATCH - 4) // 2) as i:
                if ch:
                    ch.enter(i, 2 * marks)
                step(2 * i + 3, 1, half=i + 1)
                step(2 * i + 4, 0, half=i + 2)
            if ch:
                ch.leave((BATCH - 4) // 2)
            step(BATCH - 1, 1)
            step(BATCH, 0, proj=False)
            step(BATCH + 1, 1, proj=False, s=False)
            step(BATCH + 2, 0, proj=False, s=False, t=False)

        @block.sync
        def _(sp):
            for c in range(CHUNKS):
                sp.dma_start(xn[:, c * CH:(c + 1) * CH, :], x_v[:, c * CH:(c + 1) * CH, :]).then_inc(loaded[c], 16)
            sp.wait_ge(bsplit, 1)
            sp.wait_ge(const, 6)
            for i in range(3):
                sp.dma_start(bias3[i:i + 1, :], bpart[0:1, i, :]).then_inc(bias_in, 16)

            def step(k, par, proj=True, s=True, t=True, fin=True, half=None):
                half = k // 2 if half is None else half
                if t:
                    sp.wait_ge(mt_ok, k - 1)
                    for i in range(3):
                        sp.dma_start(qs[KR + i:KR + i + 1, par, :, :].rearrange("a h (i n) -> a (h i) n", n=P),
                                     mT[i % 2 * 64:i % 2 * 64 + 64, i // 2, :]).then_inc(m_in, 16)
                if fin:
                    sp.dma_start(xn[:, bass.ds(BT * (k - 3), BT), :], x_v[:, bass.ds(BT * (k - 3), BT), :]).then_inc(xr_in, 16)
                if proj:
                    sp.wait_ge(q_parts, k + 1)
                    sp.dma_start(w_view[par], qp[:, :, :, :].rearrange("p i j n -> p (i j) n")).then_inc(parts_out, 16)
                if fin:
                    sp.wait_ge(o_ev, BT * (k - 2))
                    sp.dma_start(o_v[:, bass.ds(BT * (k - 3), BT), :], xn[:, bass.ds(BT * (k - 3), BT), :]).then_inc(x_out, 16)
                if proj:
                    sp.wait_ge(parts_out, 16 * k + 16)
                    for g in range(2):
                        if t:
                            sp.wait_ge(t_ps, H3 * (k - 2) + 3 * GH * (g + 1))
                        for q, to, order in ((0, qs, SPLIT_Q), (1, ks, SPLIT_K)):
                            for r, part in enumerate(order):
                                sp.dma_start(to[r * HD:(r + 1) * HD, par, g * GH:(g + 1) * GH, :],
                                             r_view[par, part, q, :, g * GH:(g + 1) * GH, :]).then_inc(stacked[par][g], 16)

            sp.wait_ge(free_ok, 1)
            steps(sp, step)
            sp.wait_ge(x_out, 16 * BATCH)

        @block.gpsimd
        def _(pool):
            ch = Chain(pool, pch)
            for a, v in ((ident, 0.0), (ident_b, 0.0), (ones_b, 1.0), (ones, 1.0), (after, 1.0), (mask_s, 0.0), (mask_t, 0.0), (bias3, 0.0)):
                ch.mark(pool.memset(a[:, :], v))
            ch.mark(pool.memset(va[:, :, :, :, :], 1.0))
            ch.mark(pool.memset(sel, 0.0))
            ch.mark(pool.memset(mpart[:, 3, :], 0.0))
            ch.settle()
            aff = lambda a, op, fill, base, step, mult: pool.affine_select(out=a, in_=a, compare_op=op, fill=fill, base=base, pattern=[[step, a.shape[1]]], channel_multiplier=mult)
            aff(ident[:, :], ALU.not_equal, 1.0, 0, -1, 1).then_inc(const, 1)
            aff(ident_b[:, :], ALU.not_equal, 1.0, 0, -1, 1).then_inc(const, 1)
            aff(after[:, :], ALU.is_gt, 0.0, 0, -1, 1).then_inc(const, 1)
            aff(mask_s[:, :], ALU.is_ge, MASKED, 0, -1, 1).then_inc(const, 1)
            aff(mask_t[:, :], ALU.is_ge, MASKED, 0, 1, -1).then_inc(const, 1)
            pool.memset(sel[:, 15:16], 1.0 / SEQ).then_inc(const, 1)
            pool.wait_ge(free_ok, 1)
            pool.wait_ge(g_in, 112)

            def step(k, par, proj=True, s=True, t=True, fin=True, half=None):
                if s:
                    pool.wait_ge(v_ev, BT * k)
                    if t:
                        wait(pool, pv_ps, HEADS * (k - 2) + M2)
                        wait(pool, suf_ps, BT * (k - 2))
                    pool.tensor_tensor(va[:, 1 - par, :, :, 0:HD], vw[:, :, :].rearrange("p t (h c) -> p t h c", c=HD),
                                       bvb[:, :].rearrange("p (h c) -> p h c", c=HD).unsqueeze(1).to_broadcast([P, BT, HEADS, HD]), ALU.add).then_inc(va_ok, 1)
                if proj:
                    wait(pool, xt_ps, k)
                    pool.tensor_copy(stg[:, :, :], xn[:, bass.ds(BT * k, BT), :]).then_inc(staged, 1)
                    pool.wait_ge(qk_hi, k + 1)
                    ch.then(pool.tensor_tensor(flat(qp[:, 1, :, :]), flat(qf[:, :, :]), flat(qp[:, 0, :, :]), ALU.subtract))
                    ch.then(pool.tensor_tensor(flat(qf[:, :, :]), flat(qf[:, :, :]), flat(qp[:, 0, :, :]), ALU.subtract))
                    pool.tensor_tensor(flat(qp[:, 2, :, :]), flat(qf[:, :, :]), flat(qp[:, 1, :, :]), ALU.subtract).then_inc(q_parts, 1)

            steps(pool, step, ch, 2)

        @block.scalar
        def _(act):
            for i, w in enumerate((wq, wk, wv, wo)):
                act.dma_start(wn[:, i, :, :], w.rearrange("(c p) n -> p c n", p=P)).then_inc(w_in, 16)
            act.dma_start(hn[:, 0, :], sw1).then_inc(w_in, 16)
            act.dma_start(hn[:, 1:4, :], pw1.rearrange("a p n -> p a n")).then_inc(w_in, 16)
            act.dma_start(w2n, pw2.rearrange("a h p -> (a h) p")).then_inc(w_in, 16)
            act.dma_start(s2n, sw2).then_inc(w_in, 16)
            act.dma_start(brow[0:1, 0, :], bo.rearrange("(a n) -> a n", a=1)).then_inc(b_in, 16)
            act.dma_start(bvb[:, :], bv.rearrange("(a n) -> a n", a=1).to_broadcast([P, D])).then_inc(g_in, 16)
            with nc.allow_non_contiguous_dma(reason="a few hundred biases to their partitions"):
                for i, b in enumerate((bq, bk)):
                    act.dma_start(bcol[:, 2 * i:2 * i + 2], b.rearrange("(c p) -> p c", p=P)).then_inc(g_in, 16)
                act.dma_start(hb[:, 0:1], sb1.rearrange("(p a) -> p a", a=1)).then_inc(g_in, 16)
                act.dma_start(hb[:, 1:4], pb1.rearrange("a p -> p a")).then_inc(g_in, 16)
            act.dma_start(b2[:, 0:POL * HEADS], pb2.rearrange("(u a) h -> u (a h)", u=1).to_broadcast([BATCH, POL * HEADS])).then_inc(g_in, 16)
            act.dma_start(b2[:, POL * HEADS:], sb2.rearrange("(u a) -> u a", u=1).to_broadcast([BATCH, POL])).then_inc(g_in, 16)
            act.wait_ge(varok, 1)
            nc.scalar.activation(rstd[:, :], mean_sq, ACT.Sqrt).then_inc(sdok, 1)
            for i in range(4):
                act.wait_ge(wt_ps, i + 1)
                nc.scalar.copy(wT[:, :, i * D:(i + 1) * D], (p_s[:, i, :] if i < 3 else p_t[:, 0, :]).rearrange("p (c n) -> p c n", c=DC)).then_inc(wt_ok, 1)
            for i in range(2):
                act.wait_ge(wt_ps, 5 + i)
                nc.scalar.copy(hT_[:, 2 * i:2 * i + 2, :, :], p_t[:, 1 + i, :].rearrange("p (w c n) -> p w c n", w=2, c=DC)).then_inc(wt_ok, 1)
            act.wait_ge(wt_ps, 7)
            nc.scalar.copy(w2T, p_p[:, 0, 0:POL * HEADS + POL]).then_inc(wt_ok, 1)
            act.wait_ge(mlp_ps, 2)
            act.wait_ge(g_in, 112)
            for i in range(4):
                nc.scalar.activation(hid[:, i, :], p_t[:, 0, i * BATCH:(i + 1) * BATCH], ACT.Gelu, bias=hb[:, i:i + 1]).then_inc(gelu, 1)
            act.wait_ge(e_in, 1)
            nc.scalar.activation(gl, gl, ACT.Exp).then_inc(e_out, 1)
            nc.scalar.activation(pl, pl, ACT.Exp).then_inc(e_out, 1)
            act.wait_ge(free_ok, 1)
            act.sem_inc(exp_ev, 3)

            def step(k, par, proj=True, s=True, t=True, fin=True, half=None):
                if t:
                    act.wait_ge(mt_ps, k - 1)
                    wait(act, m_in, 48 * (k - 2))
                    nc.scalar.copy(mT[:, :, :], p_p[:, 1, 0:P].bitcast(BF16).rearrange("p (a n) -> p a n", a=2)).then_inc(mt_ok, 1)
                if proj:
                    act.wait_ge(xt_ps, k + 1)
                    nc.scalar.copy(xT[:, :, :], p_t[:, 0:2, :]).then_inc(xt_ok, 1)
                    act.wait_ge(qk_ev, 4 * k + 4)
                    wait(act, parts_out, 16 * k)
                    nc.scalar.copy(flat(qp[:, 0, :, :]), flat(qf[:, :, :])).then_inc(qk_hi, 1)
                    wait(act, va_ok, k)
                    for i in range(BT):
                        act.wait_ge(v_ps, BT * k + i + 1)
                        nc.scalar.copy(vw[:, i, :], p_p[:, i % 2, 0:D]).then_inc(v_ev, 1)
                if t:
                    wait(act, ctx_ok, k - 2)
                    for i in range(BT):
                        act.wait_ge(suf_ps, BT * (k - 2) + i + 1)
                        nc.scalar.copy(suf[:, i, :, :].rearrange("p h c -> p (h c)"), p_s[:, i % 3, 0:HEADS * VW]).then_inc(suf_ev, 1)
                    act.wait_ge(w_ready, k - 1)
                    nc.scalar.activation(wm[:, :, :], wm[:, :, :], ACT.Exp).then_inc(w_exp, 1)
                if fin:
                    act.wait_ge(ct_ps, k - 2)
                    nc.scalar.copy(xT[:, :, :], p_t[:, 0:2, :]).then_inc(ct_ok, 1)
                if t:
                    with act.Fori(0, HEADS // 2) as j:
                        for q in range(2):
                            head = HEADS * (k - 2) + 2 * j + q
                            act.wait_ge(pv_ps, head + 1)
                            for m, (lo, hi) in enumerate(((0, 512), (512, 1024), (1024, 1280))):
                                act.wait_ge(t_ps, 3 * head + m + 1)
                                nc.scalar.activation(pt[:, q, lo:hi], p_t[:, m, 0:hi - lo], ACT.Exp).then_inc(exp_ev, 1)

            steps(act, step)

        @block.vector
        def _(dve):
            ch = Chain(dve, dch)
            V = nc.vector
            for c in range(CHUNKS):
                dve.wait_ge(loaded[c], 16)
                with dve.Fori(c * CH, c * CH + CH) as t:
                    ch.enter(t - c * CH, 1)
                    ch.mark(V.bn_stats(flat(bn[:, bass.ds(t, 1), :]), flat(xn[:, bass.ds(t, 1), :])))
                ch.leave(CH)
            ch.settle()
            ln_stats(nc, ch, bn, mean, tmp, varok)
            dve.wait_ge(sdok, 1)
            ch.then(V.reciprocal(rstd[:, :], rstd[:, :]))
            with dve.Fori(0, TILES) as t:
                x_t = flat(xn[:, bass.ds(t, 1), :])
                V.tensor_scalar(x_t, x_t, mean[:, bass.ds(t, 1)], rstd[:, bass.ds(t, 1)], ALU.subtract, ALU.mult).then_inc(normed, 1)
            dve.wait_ge(b_in, 16)
            split3(nc, ch, brow, bpart, bsplit)
            dve.wait_ge(mean_ps, 1)
            V.tensor_copy(xm, p_p[0:BATCH, 1, 0:D]).then_inc(mean_ok, 1)
            dve.wait_ge(mlp_ps, 1)
            V.tensor_copy(flat(xmT), p_p[:, 1, 0:DC * BATCH]).then_inc(mlp_ok, 1)
            dve.wait_ge(gate_ps, 1)
            dve.wait_ge(g_in, 112)
            ch.mark(V.tensor_tensor(flat(gl), p_p[0:BATCH, 0, 0:POL * HEADS], b2[:, 0:POL * HEADS], ALU.add))
            ch.then(V.tensor_tensor(pl, p_p[0:BATCH, 0, POL * HEADS:POL * HEADS + POL], b2[:, POL * HEADS:], ALU.add))
            ch.mark(V.tensor_reduce(gs[:, 0:POL].unsqueeze(2), gl, AX.X, ALU.max))
            ch.then(V.tensor_reduce(gs[:, POL:POL + 1], pl, AX.X, ALU.max))
            ch.mark(V.tensor_tensor(gl, gl, gs[:, 0:POL].unsqueeze(2).to_broadcast([BATCH, POL, HEADS]), ALU.subtract))
            V.tensor_scalar(pl, pl, gs[:, POL:POL + 1], None, ALU.subtract).then_inc(e_in, 1)
            dve.wait_ge(e_out, 2)
            ch.mark(V.tensor_reduce(gs[:, 0:POL].unsqueeze(2), gl, AX.X, ALU.add))
            ch.then(V.tensor_reduce(gs[:, POL:POL + 1], pl, AX.X, ALU.add))
            ch.then(V.reciprocal(gs[:, 0:POL + 1], gs[:, 0:POL + 1]))
            ch.then(V.tensor_scalar(pl, pl, gs[:, POL:POL + 1], None, ALU.mult))
            ch.then(V.tensor_tensor(gs[:, 0:POL], gs[:, 0:POL], pl, ALU.mult))
            ch.then(V.tensor_scalar(gate, gl[:, 0, :], gs[:, 0:1], None, ALU.mult))
            for i in range(1, POL):
                ch.then(V.scalar_tensor_tensor(gate, gl[:, i, :], gs[:, i:i + 1], gate, ALU.mult, ALU.add))
            ch.then(V.tensor_scalar(gch.rearrange("p (h c) -> p h c", c=HD), gate.unsqueeze(2).to_broadcast([BATCH, HEADS, HD]), 0.25, None, ALU.mult))
            ch.then(V.tensor_scalar(gate, gate, -1e9, None, ALU.mult))
            V.tensor_tensor(gdiag, ident[0:BATCH, 0:BATCH].unsqueeze(2).to_broadcast([BATCH, BATCH, HEADS]),
                            gate.unsqueeze(1).to_broadcast([BATCH, BATCH, HEADS]), ALU.mult).then_inc(gate_ok, 1)
            dve.wait_ge(gate_ps, 2)
            ch.mark(V.tensor_copy(flat(gq[:, :, :]), p_p[:, 1, 0:DC * BATCH]))
            ch.settle()
            V.tensor_copy(flat(ng[:, :, :]), p_t[:, 1, 0:BATCH * HEADS]).then_inc(free_ok, 1)
            dve.wait_ge(free_ok, 1)
            dve.sem_inc(smax, 3)
            V.memset(ks[KR:P, :, :, :], 1.0).then_inc(ld_free, 1)

            def step(k, par, proj=True, s=True, t=True, fin=True, half=None):
                if proj:
                    wait(dve, q_parts, k)
                    for j in range(4):
                        dve.wait_ge(qk_ps, 4 * k + j + 1)
                        src = p_s[:, j, :] if j < 3 else p_t[:, 2, :]
                        if j < 2:
                            V.tensor_scalar(qf[:, j, :], src, bcol[:, j:j + 1], gq[:, j, bass.ds(k, 1)], ALU.add, ALU.mult).then_inc(qk_ev, 1)
                        else:
                            V.tensor_scalar(qf[:, j, :], src, bcol[:, j:j + 1], None, ALU.add).then_inc(qk_ev, 1)
                if t:
                    V.tensor_tensor(wm[:, :, :], mneg[:, par, :, :], ng[:, bass.ds(k - 2, 1), :].rearrange("p a h -> p h a").to_broadcast([P, HEADS, BT]), ALU.add).then_inc(w_ready, 1)
                if fin:
                    dve.wait_ge(xr_in, 16 * (k - 2))
                    for i in range(BT):
                        dve.wait_ge(o_ps, BT * (k - 3) + i + 1)
                        x_t = flat(xn[:, bass.ds(BT * (k - 3) + i, 1), :])
                        V.tensor_tensor(x_t, p_p[:, i % 2, 0:D], x_t, ALU.add).then_inc(o_ev, 1)
                if s:
                    for q in range(2):
                        head(k, par, q, s, t and q > 0, q)
                    with dve.Fori(1, HEADS // 2) as j:
                        for q in range(2):
                            head(k, par, 2 * j + q, s, t, q)
                elif t:
                    head(k, par, 1, False, True, 1)
                    with dve.Fori(1, HEADS // 2) as j:
                        for q in range(2):
                            head(k, par, 2 * j + q, False, True, q)
                if t:
                    head(k, par, HEADS, False, True, 0)
                if s:
                    dve.wait_ge(smax, H3 * k + 3)
                    wait(dve, mt_ps, k - 1)
                    m = mneg[:, 1 - par, :, :].rearrange("p h i -> p (h i)")
                    ch.then(V.tensor_copy(mpart[:, 0, :], m))
                    ch.then(V.tensor_tensor(mrest[:, 0, :], m, mpart[:, 0, :], ALU.subtract))
                    ch.then(V.tensor_copy(mpart[:, 1, :], mrest[:, 0, :]))
                    ch.then(V.tensor_tensor(mrest[:, 1, :], mrest[:, 0, :], mpart[:, 1, :], ALU.subtract))
                    V.tensor_copy(mpart[:, 2, :], mrest[:, 1, :]).then_inc(m_ok, 1)
                if t:
                    dve.wait_ge(pv_ev, HEADS * (k - 1))
                    dve.wait_ge(suf_ev, BT * (k - 1))
                    dve.wait_ge(w_exp, k - 1)
                    by = lambda a: a.rearrange("p i h c -> p h i c")
                    ch.then(V.tensor_tensor(by(suf[:, :, :, :]), by(suf[:, :, :, :]), wm[:, :, :].unsqueeze(3).to_broadcast([P, HEADS, BT, VW]), ALU.mult))
                    ch.then(V.tensor_tensor(ob[:, :, :, :], ob[:, :, :, :], by(suf[:, :, :, :]), ALU.add))
                    ch.then(V.reciprocal(rd[:, :, :].unsqueeze(3), ob[:, :, :, HD:VW]))
                    wait(dve, ct_ps, k - 2)
                    V.tensor_tensor(cx[:, :, :].rearrange("p i (h c) -> p h i c", c=HD), ob[:, :, :, 0:HD],
                                    rd[:, :, :].unsqueeze(3).to_broadcast([P, HEADS, BT, HD]), ALU.mult).then_inc(ctx_ok, 1)
                    dve.wait_ge(ctx_ok, k - 1)

            def head(k, par, h, s, t, q):
                if s:
                    first = 3 * (HEADS * (k - 1) + h)
                    to = lambda i: mneg[:, 1 - par, bass.ds(h, 1), i]
                    red = lambda i, src: V.tensor_reduce(to(i), src, AX.X, ALU.max, negate=True)
                    dve.wait_ge(s_ps, first + 1)
                    red(3, p_s[:, 0, :]).then_inc(smax, 1)
                    dve.wait_ge(s_ps, first + 2)
                    red(2, p_s[:, 1, 0:384])
                    red(0, p_s[:, 1, 384:512]).then_inc(smax, 1)
                    dve.wait_ge(s_ps, first + 3)
                    red(1, p_s[:, 2, 0:256]).then_inc(smax, 1)
                if t:
                    dve.wait_ge(pv_ps, HEADS * (k - 2) + h + M2)
                    V.tensor_copy(ob[:, bass.ds(h - 1, 1), :, :].rearrange("p a i c -> p (a i c)"), p_p[:, 1 - q, 0:BT * VW]).then_inc(pv_ev, 1)

            steps(dve, step, ch, 7)

        @block.tensor
        def _(pe):
            mm = nc.tensor.matmul
            tr = nc.tensor.transpose
            pe.wait_ge(const, 6)
            pe.wait_ge(w_in, 128)
            for i in range(4):
                dst = p_s[:, i, :] if i < 3 else p_t[:, 0, :]
                for c in range(DC):
                    for o in range(DC):
                        last = tr(dst[:, c * D + o * P:c * D + (o + 1) * P], wn[:, i, o, c * P:(c + 1) * P], ident[:, :])
                last.then_inc(wt_ps, 1)
            for i in range(2):
                for w in range(2):
                    for c in range(DC):
                        last = tr(p_t[:, 1 + i, (2 * w + c) * P:(2 * w + c + 1) * P], hn[:, 2 * i + w, c * P:(c + 1) * P], ident[:, :])
                last.then_inc(wt_ps, 1)
            tr(p_p[:, 0, 0:POL * HEADS], w2n, ident[0:POL * HEADS, 0:POL * HEADS])
            tr(p_p[:, 0, POL * HEADS:POL * HEADS + POL], s2n, ident[0:POL, 0:POL]).then_inc(wt_ps, 1)
            for b in range(BATCH):
                pe.wait_ge(normed, BT * (b + 1))
                for i in range(BT):
                    last = mm(p_p[0:BATCH, 1, 0:D], sel[:, 15 - b:31 - b], xn[:, BT * b + i, :], start=b + i == 0, stop=b == BATCH - 1 and i == BT - 1)
            last.then_inc(mean_ps, 1)
            pe.wait_ge(mean_ok, 1)
            for c in range(DC):
                last = tr(p_p[:, 1, c * BATCH:(c + 1) * BATCH], xm[:, c * P:(c + 1) * P], ident[0:BATCH, 0:BATCH])
            last.then_inc(mlp_ps, 1)
            pe.wait_ge(mlp_ok, 1)
            pe.wait_ge(wt_ok, 7)
            for w in range(4):
                for c in range(DC):
                    last = mm(p_t[:, 0, w * BATCH:(w + 1) * BATCH], hT_[:, w, c, :], xmT[:, c, :], start=c == 0, stop=c == DC - 1)
            last.then_inc(mlp_ps, 1)
            pe.wait_ge(gelu, 4)
            for a in range(POL):
                mm(p_p[0:BATCH, 0, a * HEADS:(a + 1) * HEADS], hid[:, 1 + a, :], w2T[:, a * HEADS:(a + 1) * HEADS], start=True, stop=True)
            mm(p_p[0:BATCH, 0, POL * HEADS:POL * HEADS + POL], hid[:, 0, :], w2T[:, POL * HEADS:], start=True, stop=True).then_inc(gate_ps, 1)
            pe.wait_ge(gate_ok, 1)
            for c in range(DC):
                tr(p_p[:, 1, c * BATCH:(c + 1) * BATCH], gch[:, c * P:(c + 1) * P], ident[0:BATCH, 0:BATCH])
            mm(p_t[:, 1, 0:BATCH * HEADS], ones[0:BATCH, :], gdiag.rearrange("p b h -> p (b h)"), start=True, stop=True).then_inc(gate_ps, 1)
            pe.wait_ge(free_ok, 1)
            pe.wait_ge(bias_in, 48)
            pe.wait_ge(ld_free, 1)
            pe.sem_inc(pv_ps, M2)

            def step(k, par, proj=True, s=True, t=True, fin=True, half=None):
                half = k // 2 if half is None else half
                if t:
                    pe.wait_ge(m_ok, k - 1)
                    wait(pe, pv_ev, HEADS * (k - 2))
                    pe.wait_ge(v_ev, BT * k if proj else BT * min(k, BATCH))
                    for i in range(2):
                        last = tr(p_p[:, 1, i * P // 2:(i + 1) * P // 2].bitcast(BF16), mpart[:, 2 * i:2 * i + 2, :].rearrange("p a n -> p (a n)"), ident_b[:, :])
                    last.then_inc(mt_ps, 1)
                if proj:
                    pe.wait_ge(staged, k + 1)
                    if t:
                        wait(pe, exp_ev, H3 * (k - 2) + 3)
                    for c in range(DC):
                        for i in range(BT):
                            last = tr(p_t[:, c, i * P:(i + 1) * P], stg[:, i, c * P:(c + 1) * P], ident[:, :])
                    last.then_inc(xt_ps, 1)
                    pe.wait_ge(xt_ok, k + 1)
                    if s:
                        wait(pe, smax, H3 * (k - 1) + 3)
                    for j in range(4):
                        dst = p_s[:, j, :] if j < 3 else p_t[:, 2, :]
                        for c in range(DC):
                            last = mm(dst, wT[:, c, j * P:(j + 1) * P], xT[:, c, :], start=c == 0, stop=c == DC - 1)
                        last.then_inc(qk_ps, 1)
                    if t:
                        pe.wait_ge(mt_ok, k - 1)
                    for i in range(BT):
                        wait(pe, v_ev, BT * k + i - 1)
                        for c in range(DC):
                            last = mm(p_p[:, i % 2, 0:D], xT[:, c, i * P:(i + 1) * P], wT[:, c, 2 * D:3 * D], start=c == 0, stop=c == DC - 1)
                        last.then_inc(v_ps, 1)
                if t:
                    pe.wait_ge(va_ok, k - 1)
                    if proj:
                        pe.wait_ge(qk_ev, 4 * k + 3)
                    else:
                        pe.wait_ge(smax, H3 * min(k - 1, BATCH) + 3)
                    for i in range(BT):
                        if i == 3:
                            pe.wait_ge(suf_ev, BT * (k - 2) + 1)
                        val = lambda j: va[:, par, j, :, :].rearrange("p h c -> p (h c)")
                        dst = p_s[:, i % 3, 0:HEADS * VW]
                        last = mm(dst, after[:, :], val(i), start=True, stop=i == BT - 1)
                        for j in range(i + 1, BT):
                            last = mm(dst, ones[:, :], val(j), start=False, stop=j == BT - 1)
                        last.then_inc(suf_ps, 1)
                if fin:
                    pe.wait_ge(ctx_ok, k - 2)
                    if proj:
                        pe.wait_ge(v_ev, BT * k + BT)
                    else:
                        pe.wait_ge(exp_ev, H3 * (min(k, BATCH + 2) - 2) + 3)
                        pe.wait_ge(pv_ev, HEADS * (min(k, BATCH + 2) - 2))
                        if t:
                            pe.wait_ge(mt_ok, k - 1)
                    for c in range(DC):
                        for i in range(BT):
                            last = tr(p_t[:, c, i * P:(i + 1) * P], cx[:, i, c * P:(c + 1) * P], ident[:, :])
                    last.then_inc(ct_ps, 1)
                    pe.wait_ge(ct_ok, k - 2)
                    for i in range(BT):
                        if i >= 2:
                            pe.wait_ge(o_ev, BT * (k - 3) + i - 1)
                        for c in range(DC):
                            mm(p_p[:, i % 2, 0:D], xT[:, c, i * P:(i + 1) * P], wT[:, c, 3 * D:], start=c == 0, stop=False)
                        mm(p_p[:, i % 2, 0:D], ones_b[:, :], bias3[:, :], start=False, stop=True).then_inc(o_ps, 1)
                if s:
                    half_s = half - 1 if par == 0 else half
                    for g in range(2):
                        pe.wait_ge(stacked[1 - par][g], 192 * half_s + 192)
                if t:
                    pe.wait_ge(m_in, 48 * (k - 1))
                    wait(pe, suf_ev, BT * (k - 1))
                    wait(pe, o_ev, BT * (k - 2))
                    if proj:
                        pe.wait_ge(qk_ev, 4 * k + 4)
                        pe.wait_ge(v_ev, BT * k + BT)
                    else:
                        pe.wait_ge(mt_ok, k - 1)
                elif s:
                    pe.wait_ge(qk_ev, 4 * k + 4)
                if not (s or t):
                    return
                pair(k, par, 0, s, t, first=True)
                with pe.Fori(1, HEADS // 2) as j:
                    pair(k, par, j, s, t)
                if t:
                    sums(k, par, HEADS - 1, 1)

            def pair(k, par, j, s, t, first=False):
                for q in range(2):
                    h = 2 * j + q
                    if s:
                        scores(k, par, h)
                    if t:
                        weights(k, par, h)
                        if not (first and q == 0):
                            sums(k, par, h - 1, 1 - q)

            def scores(k, par, h):
                n = 3 * (HEADS * (k - 1) + h)
                query = lambda i: qs[0:KR, 1 - par, bass.ds(h, 1), i * P:(i + 1) * P].rearrange("p a n -> p (a n)")
                keys = lambda i: ks[0:KR, 1 - par, bass.ds(h, 1), 0:(i + 1) * P].rearrange("p a n -> p (a n)")
                for m, blocks in enumerate((((3, 0),), ((2, 0), (0, 384)), ((1, 0),))):
                    pe.wait_ge(smax, n + m + 1)
                    for i, lo in blocks:
                        hi = lo + (i + 1) * P
                        mm(p_s[:, m, lo:hi], query(i), keys(i), start=True, stop=False, skip_group_check=True)
                        last = mm(p_s[:, m, hi - P:hi], ident_b[:, :], mask_s[:, :], start=False, stop=True, skip_group_check=True)
                    last.then_inc(s_ps, 1)

            def weights(k, par, h):
                n = 3 * (HEADS * (k - 2) + h)
                key = lambda j: ks[0:KM, par, bass.ds(h, 1), j * P:(j + 1) * P].rearrange("p a n -> p (a n)")
                queries = lambda j: qs[0:KM, par, bass.ds(h, 1), j * P:SEQ].rearrange("p a n -> p (a n)")
                for m, blocks in enumerate((((0, 0),), ((1, 0), (3, 384)), ((2, 0),))):
                    pe.wait_ge(exp_ev, n + m + 1)
                    for j, lo in blocks:
                        mm(p_t[:, m, lo:lo + SEQ - j * P], key(j), queries(j), start=True, stop=False, skip_group_check=True)
                        last = mm(p_t[:, m, lo:lo + P], ident_b[:, :], mask_t[:, :], start=False, stop=True, skip_group_check=True)
                    last.then_inc(t_ps, 1)

            def sums(k, par, h, q):
                head = HEADS * (k - 2) + h
                pe.wait_ge(exp_ev, 3 * head + 6)
                wait(pe, pv_ev, head - 1)
                for i in range(BT):
                    for j in range(i + 1):
                        lo = SPAN[j] + (i - j) * P
                        last = mm(p_p[:, q, i * VW:(i + 1) * VW], pt[:, q, lo:lo + P], va[:, par, j, bass.ds(h, 1), :].rearrange("p a c -> p (a c)"), start=j == 0, stop=j == i)
                last.then_inc(pv_ps, 1)

            steps(pe, step)


def build(nc, x, a, b, ffn, tables, out):
    dram = lambda name, shape, dt=F32: nc.dram_tensor(name, shape, dt, kind="Internal").ap()
    rows_of = lambda t: t.rearrange("b s n -> (b s) n")
    x1, x2, x3 = (dram(f"x{i}", (N_TOK, D)) for i in (1, 2, 3))
    rows = dram("rows", (2 * N_TOK, D))
    answers = dram("answers", (N_TOK, D))
    parts = dram("parts", (2, 3, 4, P, SEQ), BF16)
    tok, band_bias, first_bias = tables
    stage_a(nc, rows_of(x), *a, band_bias, first_bias, x1)
    stage_moe(nc, "m", x1, *ffn, tok, rows, answers, x2, zero_rows=True)
    stage_b(nc, x2, *b, parts, x3)
    stage_moe(nc, "n", x3, *ffn, tok, rows, answers, rows_of(out), zero_rows=False)


ATTN = ("wq", "bq", "wk", "bk", "wv", "bv", "wo", "bo")
GATES = ("pw1", "pb1", "pw2", "pb2", "sw1", "sb1", "sw2", "sb2")


def kernel(**inputs):
    import numpy as np
    import concourse.bacc as bacc
    from concourse.bass_utils import run_bass_kernel_spmd

    nc = bacc.Bacc("TRN2", target_bir_lowering=False, num_devices=1)
    arrays = {}

    def given(name, array):
        arrays[name] = np.ascontiguousarray(array)
        return nc.dram_tensor(name, array.shape, mybir.dt.from_np(array.dtype), kind="ExternalInput").ap()

    take = lambda prefix, names: [given(f"in_{prefix}{n}", inputs[prefix + n]) for n in names]
    x, = take("L0_attn_a_", ("x",))
    a = take("L0_attn_a_", ATTN)
    b = take("L0_attn_b_", ATTN + GATES)
    ffn = take("L0_ffn_", ("Wg", "w1", "w2"))
    band_bias, first_bias = band_tables(np)
    tables = given("token_table", token_table(np)), given("band_bias", band_bias), given("first_bias", first_bias)
    out = nc.dram_tensor("out_x", (BATCH, SEQ, D), F32, kind="ExternalOutput").ap()
    build(nc, x, a, b, ffn, tables, out)
    r = run_bass_kernel_spmd(nc, [arrays], core_ids=[0])
    return r.results[0]["out_x"]
```

```python
from contextlib import ExitStack

import concourse.bass as bass
from concourse import mybir

F32 = mybir.dt.float32
BF16 = mybir.dt.bfloat16
U32 = mybir.dt.uint32
ALU = mybir.AluOpType
ACT = mybir.ActivationFunctionType
AX = mybir.AxisListType

P = 128
BATCH, SEQ, D = 16, 512, 256
HEADS, HD = 16, 16
N_TOK = BATCH * SEQ
TILES = N_TOK // P
DC = D // P
EPS = 1e-5


def wait(eng, sem, value):
    if not isinstance(value, int) or value > 0:
        eng.wait_ge(sem, value)


class Chain:

    def __init__(self, eng, sem):
        self.eng, self.sem, self.base, self.n, self.turn, self.per_turn = eng, sem, 0, 0, None, 0

    def enter(self, turn, per_turn):
        self.base, self.n, self.turn, self.per_turn = self.base + self.n, 0, turn, per_turn

    def leave(self, turns):
        assert self.n == self.per_turn, (self.n, self.per_turn)
        self.base, self.n, self.turn = self.base + turns * self.per_turn, 0, None

    def mark(self, instruction):
        self.n += 1
        instruction.then_inc(self.sem, 1)

    def settle(self):
        value = self.base + self.n
        if self.turn is not None:
            value = self.turn * self.per_turn + value
        self.eng.wait_ge(self.sem, value)

    def then(self, instruction):
        self.mark(instruction)
        self.settle()


class Stage:

    def __init__(self, nc, name):
        self.nc, self.name, self.ctx = nc, name, ExitStack()
        self.sems = []

    def __enter__(self):
        self.ctx.__enter__()
        self.ctx.callback(self.clear)
        return self

    def clear(self):
        self.nc.clear_and_free_semaphores(self.sems)
        self.nc.all_engine_barrier()

    def __exit__(self, *a):
        return self.ctx.__exit__(*a)

    def sb(self, name, shape, dt=F32):
        return self.ctx.enter_context(self.nc.sbuf_tensor(f"{self.name}_{name}", shape, dt))

    def ps(self, name, shape, dt=F32):
        return self.ctx.enter_context(self.nc.psum_tensor(f"{self.name}_{name}", shape, dt))

    def sem(self, name):
        self.sems.append(self.nc.alloc_semaphore(f"{self.name}_{name}"))
        return self.sems[-1]


CH = 8
CHUNKS = TILES // CH
REACH = 2
EXT = TILES + 2 * REACH
E_FIRST, E_MEAN = EXT, EXT + 1
OLD = 2 * REACH
SLOTS = CH + OLD
NOFF = 2 * REACH + 2
PRO = 2 + OLD
TPB = P // BATCH


def stage_a(nc, x, wq, bq, wk, bk, wv, bv, wo, bo, band_bias, first_bias, out):
    x_v = x.rearrange("(p t) n -> p t n", p=P)
    o_v = out.rearrange("(p t) n -> p t n", p=P)
    x_b = x.rearrange("(b r) n -> b r n", b=BATCH)
    o_b = out.rearrange("(b r) n -> b r n", b=BATCH)
    with Stage(nc, "a") as st:
        sb, ps, sem = st.sb, st.ps, st.sem
        xv = sb("xv", [P, EXT + 2, D])
        qkb = sb("qkb", [P, 2 * SLOTS, 2 * D])
        qkz = sb("qkz", [P, 2 * D])
        wT = sb("wT", [P, DC, 4 * D])
        bias3 = sb("bias3", [P, 4 * D], BF16)
        ones_bf = sb("ones_bf", [P, P], BF16)
        ident = sb("ident", [P, P])
        blk = sb("blk", [P, P])
        stg = sb("stg", [P, 2, D])
        xT = sb("xT", [P, 2, DC, P])
        mean = sb("mean", [P, EXT + 1])
        rstd = sb("rstd", [P, EXT + 1])
        band = sb("band", [P, TILES, NOFF])
        fbias = sb("fbias", [P, TILES])
        prd = sb("prd", [P, CH, D])
        prp = sb("prp", [P, CH, D])
        s6 = sb("s6", [P, CH * HEADS, NOFF])
        e6 = sb("e6", [P, CH * HEADS, NOFF])
        sm = sb("sm", [P, 4, CH * HEADS])
        s0 = sb("s0", [P, TILES, HEADS])
        grp = [sb(f"grp{i}", [P, CH, D]) for i in range(2)]
        cT = sb("cT", [P, 2, DC, P])
        xr = sb("xr", [P, CH, D])
        ob = sb("ob", [P, CH, D])
        r0 = sb("r0", [P, 6, HEADS])
        r0T = sb("r0T", [HEADS, P + BATCH])
        wn = qkb[:, 0:4, :].rearrange("p a (b n) -> p a b n", b=2)
        brow = prd[0:1, :, :].rearrange("p a n -> p (a n)").rearrange("p (b n) -> p b n", b=2)
        bpart = prp[0:1, :, :].bitcast(BF16).rearrange("p a n -> p (a n)").rearrange("p (b n) -> p b n", b=4)
        bn = grp[0][:, 0:2, :].rearrange("p a n -> p (a n)")[:, 0:6 * (EXT + 1)].rearrange("p (a n) -> p a n", n=6)
        tmp = grp[1][:, 0, 0:2 * (EXT + 1)].rearrange("p (a n) -> p a n", a=2)
        first_e = prd[:, 0:4, :].rearrange("p a (b h) -> p (a b) h", h=HEADS)

        p_x = ps("p_x", [P, 2, 512])
        p_qk = ps("p_qk", [P, 2, 512])
        p_v = ps("p_v", [P, 512])
        p_c = ps("p_c", [P, 2, 512])
        p_o = ps("p_o", [P, 512])

        loaded = [sem(f"loaded{c}") for c in range(CHUNKS)]
        (halo, w_in, b_in, tab_in, const, wt_ps, wt_ok, bsplit, bias_in, varok, sdok, normed, sum_ps, mean_ok,
         staged, xt_ps, xt_ok, qkv_ps, qk_ok, wrapped, pooled, pool_red, s_done, e_in, e_out, p_ok, g_dve, g_pool,
         ct_ps, ct_ok, o_ps, o_ok, xr_in, y_ok, y_out, dch, pch, f_e, f_exp, f_tr, f_trd, f_prod, f_used, f_sum,
         f_ctx, f_den, f_zero, f_x, f_y) = [sem(n) for n in (
             "halo", "w_in", "b_in", "tab_in", "const", "wt_ps", "wt_ok", "bsplit", "bias_in", "varok", "sdok",
             "normed", "sum_ps", "mean_ok", "staged", "xt_ps", "xt_ok", "qkv_ps", "qk_ok", "wrapped", "pooled",
             "pool_red", "s_done", "e_in", "e_out", "p_ok", "g_dve", "g_pool", "ct_ps", "ct_ok", "o_ps", "o_ok",
             "xr_in", "y_ok", "y_out", "dve_chain", "pool_chain", "first_e_in", "first_e_out", "first_tr",
             "first_tr_used", "first_prod", "first_used", "first_sum", "first_ctx", "first_den", "first_zero",
             "first_x", "first_y")]
        block = st.ctx.enter_context(nc.Block())

        @block.sync
        def _(sp):
            for c in range(CHUNKS):
                sp.dma_start(xv[:, REACH + c * CH:REACH + (c + 1) * CH, :],
                             x_v[:, c * CH:(c + 1) * CH, :]).then_inc(loaded[c], 16)
            sp.dma_start(xv[1:P, 0:REACH, :], x_v[0:P - 1, TILES - REACH:TILES, :]).then_inc(halo, 16)
            sp.dma_start(xv[0:1, 0:REACH, :], x_v[0:1, 0:REACH, :]).then_inc(halo, 16)
            sp.dma_start(xv[0:P - 1, EXT - REACH:EXT, :], x_v[1:P, 0:REACH, :]).then_inc(halo, 16)
            sp.dma_start(xv[P - 1:P, EXT - REACH:EXT, :], x_v[P - 1:P, 0:REACH, :]).then_inc(halo, 16)
            for g in range(TPB):
                sp.dma_start(xv[g:P:TPB, E_FIRST, :], x_b[:, 0, :]).then_inc(halo, 16)
            sp.wait_ge(bsplit, 1)
            for i in range(3):
                sp.dma_start(bias3[i:i + 1, :], bpart[0:1, i, :]).then_inc(bias_in, 16)
            sp.dma_start(xr[:, :, :], x_v[:, 0:CH, :]).then_inc(xr_in, 16)
            with sp.Fori(1, CHUNKS) as c:
                sp.wait_ge(y_ok, c)
                sp.dma_start(o_v[:, bass.ds(c * CH - CH, CH), :], xr[:, :, :]).then_inc(y_out, 16)
                sp.wait_ge(y_out, c * 16)
                sp.dma_start(xr[:, :, :], x_v[:, bass.ds(c * CH, CH), :]).then_inc(xr_in, 16)
            sp.wait_ge(y_ok, CHUNKS)
            sp.dma_start(o_v[:, (CHUNKS - 1) * CH:, :], xr[:, :, :]).then_inc(y_out, 16)
            sp.wait_ge(y_out, 16 * CHUNKS)
            sp.wait_ge(f_zero, 1)
            sp.dma_start(ob[0:P:TPB, 0, :], x_b[:, 0, :]).then_inc(f_x, 16)
            sp.wait_ge(f_y, 1)
            sp.dma_start(o_b[:, 0, :], ob[0:P:TPB, 1, :]).then_inc(y_out, 16)
            sp.wait_ge(y_out, 16 * CHUNKS + 16)

        @block.gpsimd
        def _(pool):
            ch = Chain(pool, pch)
            for m, v in ((ident, 0.0), (blk, 1.0), (ones_bf, 1.0), (bias3, 0.0)):
                pool.memset(m[:, :], v).then_inc(const, 1)
            pool.wait_ge(const, 4)
            pool.affine_select(out=ident[:, :], in_=ident[:, :], compare_op=ALU.not_equal, fill=1.0,
                               base=0, pattern=[[-1, P]], channel_multiplier=1).then_inc(const, 1)
            blk_v = blk[:, :].rearrange("p (b g) -> p b g", g=TPB)
            ch.then(pool.affine_select(out=blk_v, in_=blk_v, compare_op=ALU.is_ge, fill=0.0, base=0,
                                       pattern=[[-TPB, BATCH], [0, TPB]], channel_multiplier=1))
            pool.affine_select(out=blk_v, in_=blk_v, compare_op=ALU.is_ge, fill=0.0, base=TPB - 1,
                               pattern=[[TPB, BATCH], [0, TPB]], channel_multiplier=-1).then_inc(const, 1)

            def residual(c):
                pool.wait_ge(xr_in, 16 * c + 16)
                pool.wait_ge(o_ok, CH * c + CH)
                pool.tensor_tensor(xr[:, :, :], xr[:, :, :], ob[:, :, :], ALU.add).then_inc(y_ok, 1)

            def chunk(c, par, behind=True):
                own = slice(SLOTS * par + REACH, SLOTS * par + REACH + CH)
                pool.wait_ge(qk_ok, PRO + CH * c + CH)
                wait(pool, pool_red, 2 * c)
                k0 = qkz[:, D:].unsqueeze(1).to_broadcast([P, CH, D])
                q0 = qkz[:, 0:D].unsqueeze(1).to_broadcast([P, CH, D])
                if behind:
                    pool.wait_ge(g_pool, c)
                pool.tensor_tensor(prp[:, :, :], qkb[:, own, 0:D], k0, ALU.mult).then_inc(pooled, 1)
                pool.wait_ge(pool_red, 2 * c + 1)
                pool.tensor_tensor(prp[:, :, :], qkb[:, own, D:], q0, ALU.mult).then_inc(pooled, 1)
                if behind:
                    residual(c - 1)
                pool.wait_ge(p_ok, c + 1)
                pool.wait_ge(pool_red, 2 * c + 2)
                wait(pool, ct_ps, CH * c)
                by_head = lambda a: a.rearrange("p t (h c) -> p t h c", c=HD)
                weight = lambda a: a.rearrange("p (t h) o -> p t h o", h=HEADS).to_broadcast([P, CH, HEADS, HD])
                row = lambda e: by_head(xv[:, e:e + 1, :]).to_broadcast([P, CH, HEADS, HD])
                ch.mark(pool.tensor_tensor(by_head(grp[1][:, :, :]), by_head(xv[:, bass.ds(CH * c + OLD, CH), :]),
                                           weight(e6[:, :, OLD:OLD + 1]), ALU.mult))
                for w, e in ((e6[:, :, NOFF - 1:NOFF], E_FIRST), (sm[:, 1, :].unsqueeze(2), E_MEAN)):
                    ch.then(pool.tensor_tensor(by_head(prp[:, :, :]), row(e), weight(w), ALU.mult))
                    add = pool.tensor_tensor(grp[1][:, :, :], grp[1][:, :, :], prp[:, :, :], ALU.add)
                    if e == E_FIRST:
                        ch.then(add)
                    else:
                        add.then_inc(g_pool, 1)

            chunk(0, 0, behind=False)
            n = ch.n
            chunk(1, 1)
            per = 2 * (ch.n - n)
            with pool.Fori(0, CHUNKS // 2 - 1) as g:
                ch.enter(g, per)
                chunk(2 * g + 2, 0)
                chunk(2 * g + 3, 1)
            ch.leave(CHUNKS // 2 - 1)
            residual(CHUNKS - 1)
            pool.wait_ge(y_ok, CHUNKS)
            pool.memset(ob[:, 0, :], 0.0).then_inc(f_zero, 1)

        @block.scalar
        def _(act):
            for i, w in enumerate((wq, wk, wv, wo)):
                act.dma_start(wn[:, i, :, :], w.rearrange("(c p) n -> p c n", p=P)).then_inc(w_in, 16)
            for i, b in enumerate((bq, bk, bv, bo)):
                act.dma_start(brow[0:1, 0, i * D:(i + 1) * D], b.rearrange("(a n) -> a n", a=1)).then_inc(b_in, 16)
            act.dma_start(band[:, :, :], band_bias).then_inc(tab_in, 16)
            act.dma_start(fbias[:, :], first_bias).then_inc(tab_in, 16)
            for i in range(4):
                act.wait_ge(wt_ps, i + 1)
                src = (p_x[:, 0, :], p_x[:, 1, :], p_qk[:, 0, :], p_qk[:, 1, :])[i].rearrange("p (c n) -> p c n", c=DC)
                nc.scalar.activation(wT[:, :, i * D:(i + 1) * D], src, ACT.Copy, scale=0.25 if i == 0 else 1.0).then_inc(wt_ok, 1)
            act.wait_ge(varok, 1)
            nc.scalar.activation(rstd[:, :], tmp[:, 0, :], ACT.Sqrt).then_inc(sdok, 1)

            def evac_qkv(e, n, dst, par):
                act.wait_ge(qkv_ps, n + 1)
                nc.scalar.copy(dst, p_qk[:, par, :])
                nc.scalar.copy(xv[:, bass.ds(e, 1), :], p_v[:, 0:D].unsqueeze(1)).then_inc(qk_ok, 1)

            def tiles(items):
                for i, (e, n, dst, par) in enumerate(items):
                    wait(act, xt_ps, n - 1)
                    nc.scalar.copy(stg[:, par:par + 1, :], xv[:, bass.ds(e, 1), :]).then_inc(staged, 1)
                    if i:
                        evac_qkv(*items[i - 1])
                    act.wait_ge(xt_ps, n + 1)
                    wait(act, qkv_ps, n - 1)
                    nc.scalar.copy(xT[:, par, :, :], p_x[:, par, 0:D].rearrange("p (c n) -> p c n", c=DC)).then_inc(xt_ok, 1)
                evac_qkv(*items[-1])

            act.wait_ge(mean_ok, 1)
            act.wait_ge(normed, EXT + 1)
            tiles([(E_FIRST, 0, qkz[:, :], 0), (E_MEAN, 1, qkb[:, 0, :], 1)]
                  + [(e, 2 + e, qkb[:, e, :], e % 2) for e in range(OLD)])

            def project(c, par):
                wait(act, s_done, c - 1)
                mine, other = SLOTS * par, SLOTS * (1 - par)
                if not isinstance(c, int) or c > 0:
                    act.wait_ge(qk_ok, PRO + CH * c)
                    nc.scalar.copy(qkb[:, mine:mine + OLD, :], qkb[:, other + CH:other + SLOTS, :])
                tiles([(CH * c + OLD + i, PRO + CH * c + i, qkb[:, mine + OLD + i, :], i % 2) for i in range(CH)])

            def rest(c):
                act.wait_ge(e_in, c + 1)
                nc.scalar.activation(e6[:, :, :], e6[:, :, :], ACT.Exp).then_inc(e_out, 1)
                wait(act, y_ok, c)
                for i in range(CH + 1):
                    if i < CH:
                        act.wait_ge(ct_ps, CH * c + i + 1)
                        wait(act, o_ps, CH * c + i - 1)
                        nc.scalar.copy(cT[:, i % 2, :, :], p_c[:, i % 2, 0:D].rearrange("p (c n) -> p c n", c=DC)).then_inc(ct_ok, 1)
                    if i > 0:
                        act.wait_ge(o_ps, CH * c + i)
                        nc.scalar.copy(ob[:, i - 1, :], p_o[:, 0:D]).then_inc(o_ok, 1)

            project(0, 0)
            project(1, 1)
            rest(0)
            with act.Fori(1, CHUNKS // 2) as g:
                project(2 * g, 0)
                rest(2 * g - 1)
                project(2 * g + 1, 1)
                rest(2 * g)
            rest(CHUNKS - 1)
            act.wait_ge(f_e, 1)
            nc.scalar.activation(first_e, first_e, ACT.Exp).then_inc(f_exp, 1)

        @block.vector
        def _(dve):
            ch = Chain(dve, dch)
            heads = lambda a: a.rearrange("p t (h c) -> p (t h) c", c=HD)
            dve.wait_ge(halo, 16 * (4 + TPB))
            for c in range(CHUNKS):
                dve.wait_ge(loaded[c], 16)
            with dve.Fori(0, EXT + 1) as e:
                ch.enter(e, 1)
                ch.mark(nc.vector.bn_stats(bn[:, bass.ds(e, 1), :].rearrange("p a n -> p (a n)"), xv[:, bass.ds(e, 1), :].rearrange("p a n -> p (a n)")))
            ch.leave(EXT + 1)
            ch.settle()
            ln_stats(nc, ch, bn, mean, tmp, varok)
            dve.wait_ge(sdok, 1)
            ch.then(nc.vector.reciprocal(rstd[:, :], rstd[:, :]))
            with dve.Fori(0, EXT + 1) as e:
                t = xv[:, bass.ds(e, 1), :].rearrange("p a n -> p (a n)")
                nc.vector.tensor_scalar(t, t, mean[:, bass.ds(e, 1)], rstd[:, bass.ds(e, 1)], ALU.subtract, ALU.mult).then_inc(normed, 1)
            dve.wait_ge(b_in, 64)
            ch.then(nc.vector.tensor_scalar(brow[0:1, 0, 0:D], brow[0:1, 0, 0:D], 0.25, None, ALU.mult))
            split3(nc, ch, brow, bpart, bsplit)
            dve.wait_ge(sum_ps, 1)
            nc.vector.tensor_scalar(xv[:, E_MEAN, :], p_v[:, 0:D], 1.0 / SEQ, None, ALU.mult).then_inc(mean_ok, 1)
            dve.wait_ge(tab_in, 32)
            dve.wait_ge(bias_in, 48)

            def chunk(c, par):
                s = SLOTS * par
                dve.wait_ge(qk_ok, PRO + CH * c + CH)
                q = qkb[:, s + REACH:s + REACH + CH, 0:D]
                for d in range(NOFF - 1):
                    ch.then(nc.vector.tensor_tensor(prd[:, :, :], q, qkb[:, s + d:s + d + CH, D:], ALU.mult))
                    ch.then(nc.vector.tensor_reduce(s6[:, :, d:d + 1], heads(prd[:, :, :]), AX.X, ALU.add))
                    if d == 1:
                        dve.wait_ge(pooled, 2 * c + 1)
                        nc.vector.tensor_reduce(s6[:, :, NOFF - 1:NOFF], heads(prp[:, :, :]), AX.X, ALU.add).then_inc(pool_red, 1)
                dve.wait_ge(pooled, 2 * c + 2)
                nc.vector.tensor_reduce(s0[:, bass.ds(c * CH, CH), :].rearrange("p t h -> p (t h)").unsqueeze(2), heads(prp[:, :, :]), AX.X, ALU.add).then_inc(pool_red, 1)
                dve.wait_ge(pool_red, 2 * c + 2)
                s64 = s6[:, :, :].rearrange("p (t h) o -> p t h o", h=HEADS)
                bias = band[:, bass.ds(c * CH, CH), :].unsqueeze(2).to_broadcast([P, CH, HEADS, NOFF])
                every = lambda a: a.unsqueeze(2).to_broadcast([P, CH * HEADS, NOFF])
                nc.vector.tensor_tensor(s64, s64, bias, ALU.add).then_inc(s_done, 1)
                dve.wait_ge(s_done, c + 1)
                ch.then(nc.vector.tensor_reduce(sm[:, 0, :].unsqueeze(2), s6[:, :, :], AX.X, ALU.max))
                wait(dve, g_pool, c)
                ch.mark(nc.vector.tensor_scalar(sm[:, 1, :], sm[:, 0, :], 0.0, None, ALU.is_lt))
                ch.then(nc.vector.tensor_scalar(sm[:, 2, :], sm[:, 0, :], 0.0, None, ALU.max))
                nc.vector.tensor_tensor(e6[:, :, :], s6[:, :, :], every(sm[:, 2, :]), ALU.subtract).then_inc(e_in, 1)
                dve.wait_ge(e_out, c + 1)
                ch.then(nc.vector.scalar_tensor_tensor(e6[:, :, :], s6[:, :, :], 0.0, e6[:, :, :], ALU.is_ge, ALU.mult))
                ch.then(nc.vector.tensor_reduce(sm[:, 3, :].unsqueeze(2), e6[:, :, :], AX.X, ALU.add))
                ch.then(nc.vector.tensor_tensor(sm[:, 3, :], sm[:, 3, :], sm[:, 1, :], ALU.add))
                ch.then(nc.vector.reciprocal(sm[:, 3, :], sm[:, 3, :]))
                nc.vector.tensor_tensor(e6[:, :, :], e6[:, :, :], every(sm[:, 3, :]), ALU.mult).then_inc(p_ok, 1)
                dve.wait_ge(p_ok, c + 1)
                wait(dve, ct_ps, CH * c)
                for d in range(OLD):
                    to = grp[0] if d == 0 else prd
                    v = heads(xv[:, bass.ds(CH * c + d, CH), :])
                    ch.then(nc.vector.tensor_tensor(heads(to[:, :, :]), v, e6[:, :, d:d + 1].to_broadcast([P, CH * HEADS, HD]), ALU.mult))
                    if d > 0:
                        add = nc.vector.tensor_tensor(grp[0][:, :, :], grp[0][:, :, :], prd[:, :, :], ALU.add)
                        if d < OLD - 1:
                            ch.then(add)
                        else:
                            add.then_inc(g_dve, 1)
                dve.wait_ge(g_dve, c + 1)

            n = ch.base + ch.n
            chunk(0, 0)
            per = 2 * (ch.base + ch.n - n)
            chunk(1, 1)
            with dve.Fori(0, CHUNKS // 2 - 1) as g:
                ch.enter(g, per)
                chunk(2 * g + 2, 0)
                chunk(2 * g + 3, 1)
            ch.leave(CHUNKS // 2 - 1)

            hT = lambda a: a.rearrange("p t h -> p h t")
            over_t = lambda a: a.unsqueeze(1).to_broadcast([P, TILES, HEADS])
            ch.then(nc.vector.tensor_tensor(s0[:, :, :], s0[:, :, :], fbias[:, :].unsqueeze(2).to_broadcast([P, TILES, HEADS]), ALU.add))
            nc.vector.tensor_reduce(r0[:, 0, :].unsqueeze(2), hT(s0[:, :, :]), AX.X, ALU.max).then_inc(f_den, 1)
            dve.wait_ge(f_tr, 1)
            ch.then(nc.vector.tensor_reduce(r0T[:, P:].unsqueeze(2), p_x[0:HEADS, 0, 0:P].rearrange("p (b g) -> p b g", g=TPB), AX.X, ALU.max))
            nc.vector.tensor_copy(r0T[:, 0:P].rearrange("p (b g) -> p b g", g=TPB), r0T[:, P:].unsqueeze(2).to_broadcast([HEADS, BATCH, TPB])).then_inc(f_trd, 1)
            dve.wait_ge(f_tr, 2)
            ch.mark(nc.vector.tensor_scalar(r0[:, 1, :], p_x[:, 1, 0:HEADS], 0.0, None, ALU.is_lt))
            ch.then(nc.vector.tensor_scalar(r0[:, 2, :], p_x[:, 1, 0:HEADS], 0.0, None, ALU.max))
            nc.vector.tensor_tensor(first_e, s0[:, :, :], over_t(r0[:, 2, :]), ALU.subtract).then_inc(f_e, 1)
            dve.wait_ge(f_exp, 1)
            flat = lambda a: a.rearrange("p t h -> p (t h)")
            ch.then(nc.vector.scalar_tensor_tensor(flat(s0[:, :, :]), flat(s0[:, :, :]), 0.0, flat(first_e), ALU.is_ge, ALU.mult))
            nc.vector.tensor_reduce(r0[:, 3, :].unsqueeze(2), hT(s0[:, :, :]), AX.X, ALU.add).then_inc(f_den, 1)
            dve.wait_ge(f_tr, 3)
            ch.then(nc.vector.tensor_tensor(r0[:, 4, :], p_x[:, 0, 0:HEADS], r0[:, 1, :], ALU.add))
            ch.then(nc.vector.reciprocal(r0[:, 4, :], r0[:, 4, :]))
            ch.then(nc.vector.tensor_tensor(s0[:, :, :], s0[:, :, :], over_t(r0[:, 4, :]), ALU.mult))
            with dve.Fori(0, CHUNKS) as c:
                dve.wait_ge(f_used, c + 1)
                nc.vector.tensor_tensor(heads(prd[:, :, :]), heads(xv[:, bass.ds(CH * c + REACH, CH), :]),
                                        flat(s0[:, bass.ds(CH * c, CH), :]).unsqueeze(2).to_broadcast([P, CH * HEADS, HD]), ALU.mult).then_inc(f_prod, 1)
            dve.wait_ge(f_sum, 1)
            by_head = lambda a: a.rearrange("p (h c) -> p h c", c=HD)
            ch.then(nc.vector.tensor_tensor(by_head(prd[:, 0, :]), by_head(xv[:, E_MEAN, :]), r0[:, 1, :].unsqueeze(2).to_broadcast([P, HEADS, HD]), ALU.mult))
            nc.vector.tensor_tensor(prd[:, 0, :], prd[:, 0, :], p_v[:, 0:D], ALU.add).then_inc(f_ctx, 1)
            dve.wait_ge(f_tr, 4)
            nc.vector.tensor_copy(cT[:, 0, :, :], p_x[:, 1, 0:D].rearrange("p (c n) -> p c n", c=DC)).then_inc(f_ctx, 1)
            dve.wait_ge(f_tr, 5)
            dve.wait_ge(f_x, 16)
            nc.vector.tensor_tensor(ob[:, 1, :], p_o[:, 0:D], ob[:, 0, :], ALU.add).then_inc(f_y, 1)

        @block.tensor
        def _(pe):
            mm = nc.tensor.matmul
            pe.wait_ge(const, 6)
            pe.wait_ge(w_in, 64)
            for i in range(4):
                dst = (p_x[:, 0, :], p_x[:, 1, :], p_qk[:, 0, :], p_qk[:, 1, :])[i]
                for c in range(DC):
                    for o in range(DC):
                        last = nc.tensor.transpose(dst[:, c * D + o * P:c * D + (o + 1) * P], wn[:, i, o, c * P:(c + 1) * P], ident[:, :])
                last.then_inc(wt_ps, 1)
            pe.wait_ge(normed, REACH + 1)
            mm(p_v[:, 0:D], blk[:, :], xv[:, REACH, :], start=True, stop=False)
            with pe.Fori(REACH + 1, REACH + TILES - 1) as e:
                pe.wait_ge(normed, e + 1)
                mm(p_v[:, 0:D], blk[:, :], xv[:, bass.ds(e, 1), :].rearrange("p a n -> p (a n)"), start=False, stop=False)
            pe.wait_ge(normed, REACH + TILES)
            mm(p_v[:, 0:D], blk[:, :], xv[:, REACH + TILES - 1, :], start=False, stop=True).then_inc(sum_ps, 1)
            pe.wait_ge(wt_ok, 4)
            pe.wait_ge(bias_in, 48)

            def matmuls(n, par):
                pe.wait_ge(xt_ok, n + 1)
                wait(pe, qk_ok, n)
                for lo, hi, dst in ((0, 2 * D, p_qk[:, par, :]), (2 * D, 3 * D, p_v[:, 0:D])):
                    for c in range(DC):
                        mm(dst, xT[:, par, c, :], wT[:, c, lo:hi], start=c == 0, stop=False)
                    last = mm(dst, ones_bf[:, :], bias3[:, lo:hi], start=False, stop=True)
                last.then_inc(qkv_ps, 1)

            def tiles(items):
                for i, (n, par) in enumerate(items):
                    pe.wait_ge(staged, n + 1)
                    wait(pe, xt_ok, n - 1)
                    for c in range(DC):
                        last = nc.tensor.transpose(p_x[:, par, c * P:(c + 1) * P], stg[:, par, c * P:(c + 1) * P], ident[:, :])
                    last.then_inc(xt_ps, 1)
                    if i:
                        matmuls(*items[i - 1])
                matmuls(*items[-1])

            def project(c):
                tiles([(PRO + CH * c + i, i % 2) for i in range(CH)])

            def rest(c):
                pe.wait_ge(g_dve, c + 1)
                pe.wait_ge(g_pool, c + 1)
                for i in range(CH + 1):
                    if i < CH:
                        wait(pe, ct_ok, CH * c + i - 1)
                        for k in range(DC):
                            for g in range(2):
                                last = mm(p_c[:, i % 2, k * P:(k + 1) * P], grp[g][:, i, k * P:(k + 1) * P], ident[:, :], start=g == 0, stop=g == 1)
                        last.then_inc(ct_ps, 1)
                    if i > 0:
                        pe.wait_ge(ct_ok, CH * c + i)
                        wait(pe, o_ok, CH * c + i - 1)
                        out_product((i - 1) % 2).then_inc(o_ps, 1)

            def out_product(par):
                for k in range(DC):
                    mm(p_o[:, 0:D], cT[:, par, k, :], wT[:, k, 3 * D:], start=k == 0, stop=False)
                return mm(p_o[:, 0:D], ones_bf[:, :], bias3[:, 3 * D:], start=False, stop=True)

            tiles([(i, i % 2) for i in range(PRO)])
            project(0)
            project(1)
            rest(0)
            with pe.Fori(1, CHUNKS // 2) as g:
                project(2 * g)
                rest(2 * g - 1)
                project(2 * g + 1)
                rest(2 * g)
            rest(CHUNKS - 1)
            pe.wait_ge(f_den, 1)
            nc.tensor.transpose(p_x[0:HEADS, 0, 0:P], r0[:, 0, :], ident[:, :]).then_inc(f_tr, 1)
            pe.wait_ge(f_trd, 1)
            nc.tensor.transpose(p_x[:, 1, 0:HEADS], r0T[:, 0:P], ident[0:HEADS, 0:HEADS]).then_inc(f_tr, 1)
            pe.wait_ge(f_den, 2)
            mm(p_x[:, 0, 0:HEADS], blk[:, :], r0[:, 3, :], start=True, stop=True).then_inc(f_tr, 1)

            def first_sum(first, last):
                for i in range(CH):
                    ins = mm(p_v[:, 0:D], blk[:, :], prd[:, i, :], start=first and i == 0, stop=last and i == CH - 1)
                return ins

            pe.sem_inc(f_used, 1)
            pe.wait_ge(f_prod, 1)
            first_sum(True, False).then_inc(f_used, 1)
            with pe.Fori(1, CHUNKS - 1) as c:
                pe.wait_ge(f_prod, c + 1)
                first_sum(False, False).then_inc(f_used, 1)
            pe.wait_ge(f_prod, CHUNKS)
            first_sum(False, True).then_inc(f_sum, 1)
            pe.wait_ge(f_ctx, 1)
            for k in range(DC):
                last = nc.tensor.transpose(p_x[:, 1, k * P:(k + 1) * P], prd[:, 0, k * P:(k + 1) * P], ident[:, :])
            last.then_inc(f_tr, 1)
            pe.wait_ge(f_ctx, 2)
            pe.wait_ge(o_ok, TILES)
            out_product(0).then_inc(f_tr, 1)


def ln_stats(nc, ch, bn, mean, tmp, done):
    half = lambda i: bn[:, :, i]
    ch.mark(nc.vector.tensor_tensor(mean[:, :], half(1), half(4), ALU.add))
    ch.mark(nc.vector.tensor_tensor(tmp[:, 0, :], half(2), half(5), ALU.add))
    ch.then(nc.vector.tensor_tensor(tmp[:, 1, :], half(1), half(4), ALU.subtract))
    ch.mark(nc.vector.tensor_scalar(mean[:, :], mean[:, :], 0.5, None, ALU.mult))
    ch.mark(nc.vector.tensor_scalar(tmp[:, 0, :], tmp[:, 0, :], 1.0 / D, EPS, ALU.mult, ALU.add))
    ch.then(nc.vector.tensor_tensor(tmp[:, 1, :], tmp[:, 1, :], tmp[:, 1, :], ALU.mult))
    nc.vector.scalar_tensor_tensor(tmp[:, 0, :], tmp[:, 1, :], 0.25, tmp[:, 0, :], ALU.mult, ALU.add).then_inc(done, 1)


def split3(nc, ch, rest, part, done):
    for i in range(3):
        copy = nc.vector.tensor_copy(part[:, i, :], rest[:, i % 2, :])
        if i == 2:
            copy.then_inc(done, 1)
        else:
            ch.then(copy)
            ch.then(nc.vector.tensor_tensor(rest[:, 1 - i % 2, :], rest[:, i % 2, :], part[:, i, :], ALU.subtract))


def band_tables(np):
    tok = np.arange(N_TOK).reshape(P, TILES)
    i = (tok % SEQ).astype(np.float32)
    bias = lambda diff: (np.exp(np.float32(-0.5) * (diff / np.float32(2.0)) ** 2)
                         + np.cos(np.float32(2.0 * np.pi) * diff / np.float32(401.0))).astype(np.float32)
    table = np.full((P, TILES, NOFF), -1e9, np.float32)
    for d in range(NOFF - 1):
        j = i + d - REACH
        table[:, :, d] = np.where((j >= 0) & (j < SEQ), bias(i - j), np.float32(-1e9))
    table[:, :, NOFF - 1] = np.where(i > REACH, bias(i), np.float32(-1e9))
    return table, bias(i)


EXPERTS, FF = 16, 1024
CAP = N_TOK // EXPERTS
FC = FF // P
ET = CAP // P
CT = 8
RC = TILES // CT
PAIRS = RC // 2
HT = 2
PAY = D + 4
MEAN, RSTD, GATE, NUM = range(D, PAY)


def stage_moe(nc, name, x, wg, w1, w2, tok, rows, out, zero_rows, skip):
    x_v = x[0:N_TOK, :].rearrange("(t p) n -> p t n", p=P)
    o_v = out[0:N_TOK, :].rearrange("(t p) n -> p t n", p=P)
    rows_v = rows[0:N_TOK, :].rearrange("(e p c) n -> e p (c n)", p=P, c=ET)
    w1_v = w1.rearrange("e (c p) f -> e p c f", p=P)
    w2_v = w2.rearrange("e (j p) n -> e p j n", p=P)
    with Stage(nc, name) as st:
        sb, ps, sem = st.sb, st.ps, st.sem
        ident = sb("ident", [P, P])
        before = sb("before", [P, P], BF16)
        ones = sb("ones", [P, P], BF16)
        wg_s = sb("wg", [P, DC, EXPERTS])
        table = sb("table", [P, 2 * TILES + 2 * EXPERTS])
        pay = sb("pay", [P, TILES, PAY])
        xs = sb("xs", [P, 2, CT, D])
        bn = sb("bn", [P, CT, 6])
        tmp = sb("tmp", [P, 2, 2, CT])
        xT = sb("xT", [P, HT, DC, 512])
        ex = sb("ex", [P, 2, CT, EXPERTS])
        pick = sb("pick", [P, CT, EXPERTS])
        loc = sb("loc", [P, CT, EXPERTS])
        hot = sb("hot", [P, CT, EXPERTS])
        hot_b = sb("hot_b", [P, CT, EXPERTS], BF16)
        seen = sb("seen", [P, 2, EXPERTS])
        seen_b = sb("seen_b", [P, EXPERTS], BF16)
        route = sb("route", [P, 7, CT])
        slot = sb("slot", [P, TILES], U32)
        taken = sb("taken", [P, EXPERTS, ET])
        spare = sb("spare", [P, 2, EXPERTS, ET])
        place_t = sb("place_t", [P, ET])
        dest = sb("dest", [P, 2, ET], U32)
        w1_s = sb("w1", [P, 2, DC, FF])
        w2_s = sb("w2", [P, 2, FC, D])
        xe = sb("xe", [P, 2, ET, PAY])
        xq = sb("xq", [P, ET, D])
        xeT = sb("xeT", [P, DC, CAP])
        hT = sb("hT", [P, FC, CAP])
        ye = sb("ye", [P, 2, ET, D])
        toks = table[:, 0:TILES]
        places = table[:, TILES:2 * TILES].rearrange("p (e c) -> p e c", c=ET)
        enum = table[:, 2 * TILES:2 * TILES + EXPERTS]
        first_row = table[:, 2 * TILES + EXPERTS:]

        p_x = ps("p_x", [P, HT, DC, 512])
        p_h = ps("p_h", [P, 2, 512])
        p_y = ps("p_y", [P, 2, 512])

        (const, tab_in, varok, sdok, normed, xt_ps, xt_ok, lg_ps, ex_in, ex_out, hot_ok, cum_ps, seen_ok,
         routed, zeroed, filled, scattered, xq_ok, xet_ps, xet_act, xet_dve, h_ps, h_act, h_dve, y_ps, y_ok, ye_free, go, dch, pch) = [sem(n) for n in (
             "const tab_in varok sdok normed xt_ps xt_ok lg_ps ex_in ex_out hot_ok cum_ps seen_ok "
             "routed zeroed filled scattered xq_ok xet_ps xet_act xet_dve h_ps h_act h_dve y_ps y_ok ye_free go dve_chain pool_chain ").split()]
        loaded, w_in, xe_in, x_out = [[sem(f"{n}{k}") for k in range(2)] for n in (
            "loaded", "w_in", "xe_in", "x_out")]
        YB = 2
        block = st.ctx.enter_context(nc.Block())
        chunk = lambda c: bass.ds(c * CT, CT)

        @block.sync
        def _(sp):
            def chunk_in(c, par):
                sp.dma_start(pay[:, chunk(c), 0:D], x_v[:, chunk(c), :]).then_inc(loaded[par], 16)

            def chunk_out(c, par, i):
                sp.wait_ge(loaded[par], 16 * i + 16)
                sp.dma_start(o_v[:, chunk(c), :], pay[:, chunk(c), 0:D]).then_inc(filled, 16)

            def weights_in(e, par):
                sp.dma_start(w1_s[:, par, :, :].unsqueeze(1), w1_v[bass.ds(e, 1)].rearrange("e p c f -> p e c f")).then_inc(w_in[par], 16)
                sp.dma_start(w2_s[:, par, :, :].unsqueeze(1), w2_v[bass.ds(e, 1)].rearrange("e p j n -> p e j n")).then_inc(w_in[par], 16)

            def tokens_in(e, par):
                sp.dma_start(xe[:, par, :, :].rearrange("p a n -> p (a n)").unsqueeze(1), rows_v[bass.ds(e, 1)].rearrange("e p n -> p e n")).then_inc(xe_in[par], 16)

            for par in range(2):
                chunk_in(par, par)
            with sp.Fori(1, PAIRS) as i:
                for par in range(2):
                    chunk_out(2 * i + par - 2, par, i - 1)
                    chunk_in(2 * i + par, par)
            for par in range(2):
                chunk_out(RC - 2 + par, par, PAIRS - 1)
            for par in range(2):
                weights_in(par, par)
            sp.wait_ge(scattered, 16 * TILES)
            for par in range(2):
                tokens_in(par, par)
            with sp.Fori(0, EXPERTS // 2 - 1) as g:
                for par in range(2):
                    sp.wait_ge(y_ok, ET * (2 * g + par) + ET + YB)
                    tokens_in(2 * g + 2 + par, par)
                    weights_in(2 * g + 2 + par, par)
                    sp.wait_ge(x_out[par], 16 * ET * (g + 1))
                    sp.sem_inc(ye_free, 1)
            for par in range(2):
                sp.wait_ge(x_out[par], 16 * ET * EXPERTS // 2)

        @block.gpsimd
        def _(pool):
            ch = Chain(pool, pch)
            pool.memset(ye[:, :, :, :], 0.0).then_inc(const, 1)
            pool.dma_start(wg_s[:, :, :], wg.rearrange("(c p) n -> p c n", p=P)).then_inc(tab_in, 16)
            pool.dma_start(table[:, :], tok).then_inc(tab_in, 16)
            ch.mark(pool.memset(ident[:, :], 0.0))
            ch.mark(pool.memset(before[:, :], 1.0))
            ch.then(pool.memset(ones[:, :], 1.0))
            pool.affine_select(out=ident[:, :], in_=ident[:, :], compare_op=ALU.not_equal, fill=1.0,
                               base=0, pattern=[[-1, P]], channel_multiplier=1).then_inc(const, 1)
            pool.affine_select(out=before[:, :], in_=before[:, :], compare_op=ALU.is_gt, fill=0.0,
                               base=0, pattern=[[1, P]], channel_multiplier=-1).then_inc(const, 1)
            if zero_rows:
                pool.wait_ge(zeroed, 16 * EXPERTS)

            for t in range(TILES):
                pool.wait_ge(routed, t // CT + 2)
                pool.indirect_dma_start(rows[:, :], bass.IndirectOffsetOnAxis(ap=slot[:, t:t + 1], axis=0), pay[:, t, :], None).then_inc(scattered, 16)
            pool.wait_ge(filled, 16 * RC)

            def put(e, par):
                for c in range(ET):
                    pool.wait_ge(y_ok, ET * e + c + 1 + YB)
                    pool.sem_inc(go, 1)
                    at = bass.IndirectOffsetOnAxis(ap=dest[:, par, c:c + 1], axis=0)
                    if skip:
                        dma = pool.indirect_dma_start(out[:, :], at, ye[:, par, c, :], None, bounds_check=N_TOK - 1, oob_is_err=False)
                    else:
                        dma = pool.indirect_dma_start(out[:, :], at, ye[:, par, c, :], None)
                    dma.then_inc(x_out[par], 16)

            with pool.Fori(0, EXPERTS // 2) as i:
                for par in range(2):
                    put(2 * i + par, par)

        @block.scalar
        def _(act):
            if zero_rows:
                act.wait_ge(const, 1)
                for e in range(EXPERTS):
                    act.dma_start(rows_v[e], ye[:, :, :, :].rearrange("p a c n -> p (a c n)")[:, 0:ET * PAY]).then_inc(zeroed, 16)

            def deviation(c, par):
                act.wait_ge(varok, c + 1)
                nc.scalar.activation(pay[:, chunk(c), RSTD], tmp[:, par, 0, :], ACT.Sqrt).then_inc(sdok, 1)

            def turned(c):
                for h in range(HT):
                    act.wait_ge(xt_ps, HT * c + h + 1)
                    wait(act, lg_ps, HT * c + h - 1)
                    nc.scalar.copy(xT[:, h, :, :], p_x[:, h, :, :]).then_inc(xt_ok, 1)

            def exponentials(c, par):
                act.wait_ge(ex_in, c + 1)
                nc.scalar.activation(ex[:, par, :, :], ex[:, par, :, :], ACT.Exp).then_inc(ex_out, 1)

            def step(c, par):
                deviation(c + 1, 1 - par)
                exponentials(c, par)
                turned(c + 1)

            deviation(0, 0)
            turned(0)
            step(0, 0)
            with act.Fori(1, PAIRS) as i:
                step(2 * i - 1, 1)
                step(2 * i, 0)
            exponentials(RC - 1, 1)
            if zero_rows:
                act.wait_ge(zeroed, 16 * EXPERTS)

            def tokens(e, par):
                act.wait_ge(xet_ps, e + 1)
                nc.scalar.copy(xeT[:, 0, :], p_x[:, par, 0, :]).then_inc(xet_act, 1)

            def hidden(e, ahead=True):
                for j in range(0, FC, 2):
                    act.wait_ge(h_ps, FC * e + j + 1)
                    nc.scalar.activation(hT[:, j, :], p_h[:, 0, :], ACT.Relu).then_inc(h_act, 1)

            expert_order(act, tokens, lambda e, par, half: None, hidden)

        @block.vector
        def _(dve):
            ch = Chain(dve, dch)
            V = nc.vector
            flat = lambda a: a.rearrange("p a n -> p (a n)")
            one = lambda a: a.unsqueeze(2)
            best, rden, idx, place, valid, at, miss = (route[:, i, :] for i in range(7))
            by_tok = lambda a: a.unsqueeze(2).to_broadcast([P, CT, EXPERTS])
            by_exp = enum.unsqueeze(1).to_broadcast([P, CT, EXPERTS])
            by_chunk = lambda a: a.rearrange("p (t e) -> p t e", e=EXPERTS)

            def stats(c, par, half):
                dve.wait_ge(loaded[par], 16 * half + 16)
                for t in range(CT):
                    ch.mark(V.bn_stats(bn[:, t, :], flat(pay[:, bass.ds(c * CT + t, 1), 0:D])))
                ch.settle()
                ln_stats(nc, ch, bn, pay[:, chunk(c), MEAN], tmp[:, par, :, :], varok)

            def normalise(c, par):
                dve.wait_ge(sdok, c + 1)
                ch.then(V.reciprocal(pay[:, chunk(c), RSTD], pay[:, chunk(c), RSTD]))
                wait(dve, xt_ps, HT * (c - 1))
                for t in range(CT):
                    row = lambda at, n=1: flat(pay[:, bass.ds(c * CT + t, 1), at:at + n])
                    V.tensor_scalar(xs[:, par, t, :], row(0, D), row(MEAN), row(RSTD),
                                    ALU.subtract, ALU.mult).then_inc(normed, 1)

            def choose(c, par):
                dve.wait_ge(lg_ps, HT * c + HT)
                lg = by_chunk(p_h[:, par, 0:CT * EXPERTS])
                ch.then(V.tensor_reduce(one(best), lg, AX.X, ALU.max))
                V.tensor_tensor(ex[:, par, :, :], lg, by_tok(best), ALU.subtract).then_inc(ex_in, 1)
                ch.then(V.tensor_tensor(pick[:, :, :], lg, by_tok(best), ALU.is_ge))
                ch.then(V.scalar_tensor_tensor(pick[:, :, :], pick[:, :, :], -float(EXPERTS), by_exp, ALU.mult, ALU.add))
                ch.then(V.tensor_reduce(one(idx), pick[:, :, :], AX.X, ALU.min))
                ch.then(V.tensor_scalar(idx, idx, float(EXPERTS), None, ALU.add))
                ch.then(V.tensor_tensor(hot[:, :, :], by_exp, by_tok(idx), ALU.is_equal))
                V.tensor_copy(hot_b[:, :, :], hot[:, :, :]).then_inc(hot_ok, 1)

            def settle_places(c, par):
                dve.wait_ge(ex_out, c + 1)
                ch.then(V.tensor_reduce(one(rden), ex[:, par, :, :], AX.X, ALU.add))
                ch.mark(V.reciprocal(rden, rden))
                ch.then(V.tensor_reduce(seen[:, 1, :].unsqueeze(2), hot[:, :, :].rearrange("p t e -> p e t"), AX.X, ALU.add))
                ch.then(V.tensor_tensor(seen[:, 0, :], seen[:, 0, :], seen[:, 1, :], ALU.add))
                dve.wait_ge(cum_ps, c + 1)
                V.tensor_copy(seen_b[:, :], seen[:, 0, :]).then_inc(seen_ok, 1)
                ch.then(V.tensor_tensor(loc[:, :, :], by_chunk(p_y[:, par, 0:CT * EXPERTS]), hot[:, :, :], ALU.mult))
                ch.then(V.tensor_reduce(one(place), loc[:, :, :], AX.X, ALU.add))
                num = toks[:, bass.ds(c * CT, CT)]
                ch.mark(V.tensor_scalar(valid, place, float(CAP), None, ALU.is_lt))
                ch.then(V.scalar_tensor_tensor(at, idx, float(CAP), place, ALU.mult, ALU.add))
                ch.mark(V.tensor_tensor(pay[:, chunk(c), GATE], rden, valid, ALU.mult))
                ch.mark(V.tensor_copy(pay[:, chunk(c), NUM], num))
                ch.then(V.scalar_tensor_tensor(miss, at, -float(N_TOK), num, ALU.add, ALU.subtract))
                ch.then(V.tensor_tensor(at, miss, valid, ALU.mult))
                V.scalar_tensor_tensor(slot[:, chunk(c)], at, float(N_TOK), num, ALU.add, ALU.add).then_inc(routed, 1)
                dve.wait_ge(routed, c + 2)

            def step(c, par, half):
                stats(c + 1, 1 - par, half)
                choose(c, par)
                normalise(c + 1, 1 - par)
                settle_places(c, par)

            dve.sem_inc(routed, 1)
            dve.sem_inc(y_ok, YB)
            dve.sem_inc(ye_free, 2)
            ch.then(V.memset(seen[:, 0, :], 0.0))
            V.memset(seen_b[:, :], 0.0).then_inc(seen_ok, 1)
            stats(0, 0, 0)
            normalise(0, 0)
            dve.wait_ge(tab_in, 32)
            step(0, 0, 0)
            with dve.Fori(1, PAIRS) as i:
                ch.enter(i - 1, 2 * (CT + 25))
                step(2 * i - 1, 1, i)
                step(2 * i, 0, i)
            ch.leave(PAIRS - 1)
            choose(RC - 1, 1)
            settle_places(RC - 1, 1)
            dve.wait_ge(cum_ps, RC + 1)
            ch.then(V.tensor_tensor(seen[:, 0, :], p_y[:, 0, 0:EXPERTS], first_row, ALU.add))
            ch.mark(V.tensor_tensor(taken[:, :, :], places, seen[:, 0, :].unsqueeze(2).to_broadcast([P, EXPERTS, ET]), ALU.is_lt))
            ch.then(V.tensor_scalar(spare[:, 0, :, :], places, float(N_TOK), None, ALU.add))
            ch.then(V.tensor_tensor(spare[:, 1, :, :], spare[:, 0, :, :], taken[:, :, :], ALU.mult))
            ch.then(V.tensor_tensor(spare[:, 0, :, :], spare[:, 0, :, :], spare[:, 1, :, :], ALU.subtract))

            def enter_expert(e, par, half):
                dve.wait_ge(xe_in[par], 16 * half + 16)
                wait(dve, xet_ps, e)
                for c in range(ET):
                    V.tensor_scalar(xq[:, c, :], xe[:, par, c, 0:D], xe[:, par, c, MEAN:MEAN + 1], xe[:, par, c, RSTD:RSTD + 1],
                                    ALU.subtract, ALU.mult).then_inc(xq_ok, 1)

            def tokens(e, par):
                dve.wait_ge(xet_ps, e + 1)
                V.tensor_copy(xeT[:, 1, :], p_x[:, par, 1, :]).then_inc(xet_dve, 1)

            def hidden(e, par, half, ahead=True):
                for j in range(1, FC, 2):
                    dve.wait_ge(h_ps, FC * e + j + 1)
                    V.tensor_scalar(hT[:, j, :], p_h[:, 1, :], 0.0, None, ALU.max).then_inc(h_dve, 1)
                    if j == FC // 2 - 1 and ahead:
                        enter_expert(e + 1, 1 - par, half if par == 0 else half + 1)

            def answers_(e, par, half):
                dve.wait_ge(ye_free, e + 1)
                ch.then(V.tensor_tensor(place_t[:, :], xe[:, par, :, NUM], flat(taken[:, bass.ds(e, 1), :]), ALU.mult))
                ch.then(V.tensor_tensor(dest[:, par, :], place_t[:, :], flat(spare[:, 0, bass.ds(e, 1), :]), ALU.add))
                for c in range(ET):
                    dve.wait_ge(y_ps, ET * e + c + 1)
                    V.scalar_tensor_tensor(ye[:, par, c, :], p_y[:, c % 2, 0:D], xe[:, par, c, GATE:GATE + 1], xe[:, par, c, 0:D], ALU.mult, ALU.add).then_inc(y_ok, 1)

            enter_expert(0, 0, 0)
            tokens(0, 0)
            hidden(0, 0, 0)
            with dve.Fori(0, EXPERTS // 2 - 1) as i:
                ch.enter(i, 4)
                tokens(2 * i + 1, 1)
                answers_(2 * i, 0, i)
                hidden(2 * i + 1, 1, i)
                tokens(2 * i + 2, 0)
                answers_(2 * i + 1, 1, i)
                hidden(2 * i + 2, 0, i + 1)
            ch.leave(EXPERTS // 2 - 1)
            e = EXPERTS - 1
            tokens(e, 1)
            answers_(e - 1, 0, e // 2)
            hidden(e, 1, e // 2, ahead=False)
            answers_(e, 1, e // 2)

        @block.tensor
        def _(pe):
            mm = nc.tensor.matmul
            pe.wait_ge(const, 3)

            def turned(c, par):
                for h in range(HT):
                    pe.wait_ge(normed, CT * c + (h + 1) * CT // HT)
                    wait(pe, xt_ok, HT * (c - 1) + h + 1)
                    for d in range(DC):
                        for i in range(4):
                            last = nc.tensor.transpose(p_x[:, h, d, i * P:(i + 1) * P], xs[:, par, 4 * h + i, d * P:(d + 1) * P], ident[:, :])
                    last.then_inc(xt_ps, 1)

            def logits(c, par):
                pe.wait_ge(routed, c)
                for h in range(HT):
                    pe.wait_ge(xt_ok, HT * c + h + 1)
                    for i in range(4):
                        t = 4 * h + i
                        for d in range(DC):
                            last = mm(p_h[:, par, t * EXPERTS:(t + 1) * EXPERTS], xT[:, h, d, i * P:(i + 1) * P], wg_s[:, d, :], start=d == 0, stop=d == DC - 1)
                    last.then_inc(lg_ps, 1)

            def count(c, par):
                pe.wait_ge(hot_ok, c + 1)
                pe.wait_ge(seen_ok, c + 1)
                pe.wait_ge(routed, c)
                to = lambda lo: p_y[:, par, lo * EXPERTS:CT * EXPERTS]
                few = lambda n: hot_b[:, 0:n, :].rearrange("p t e -> p (t e)")
                mm(to(0), before[:, :], few(CT), start=True, stop=False, skip_group_check=True)
                for s in range(1, CT):
                    mm(to(s), ones[:, :], few(CT - s), start=False, stop=False, skip_group_check=True)
                mm(to(0), ones[:, :], seen_b[:, :].unsqueeze(1).to_broadcast([P, CT, EXPERTS]), start=False, stop=True, skip_group_check=True).then_inc(cum_ps, 1)

            def step(c, par):
                count(c, par)
                turned(c + 1, 1 - par)
                logits(c + 1, 1 - par)

            turned(0, 0)
            pe.wait_ge(tab_in, 32)
            logits(0, 0)
            step(0, 0)
            with pe.Fori(1, PAIRS) as i:
                step(2 * i - 1, 1)
                step(2 * i, 0)
            count(RC - 1, 1)
            pe.wait_ge(seen_ok, RC + 1)
            pe.wait_ge(routed, RC + 1)
            mm(p_y[:, 0, 0:EXPERTS], ones[:, :], seen_b[:, :], start=True, stop=True).then_inc(cum_ps, 1)

            def tokens(e, par):
                pe.wait_ge(xq_ok, ET * e + ET)
                for c in range(DC):
                    for i in range(ET):
                        last = nc.tensor.transpose(p_x[:, par, c, i * P:(i + 1) * P], xq[:, i, c * P:(c + 1) * P], ident[:, :])
                last.then_inc(xet_ps, 1)

            def hidden(e, par, half):
                pe.wait_ge(w_in[par], 32 * half + 32)
                pe.wait_ge(xet_act, e + 1)
                pe.wait_ge(xet_dve, e + 1)
                for j in range(FC):
                    wait(pe, (h_act, h_dve)[j % 2], FC // 2 * e + j // 2)
                    for c in range(DC):
                        last = mm(p_h[:, j % 2, :], w1_s[:, par, c, j * P:(j + 1) * P], xeT[:, c, :], start=c == 0, stop=c == DC - 1)
                    last.then_inc(h_ps, 1)

            def answers_(e, par):
                pe.wait_ge(h_act, FC // 2 * e + FC // 2)
                pe.wait_ge(h_dve, FC // 2 * e + FC // 2)
                for c in range(ET):
                    pe.wait_ge(y_ok, ET * e + c - 1 + YB)
                    for j in range(FC):
                        last = mm(p_y[:, c % 2, 0:D], hT[:, j, c * P:(c + 1) * P], w2_s[:, par, j, :], start=j == 0, stop=j == FC - 1)
                    last.then_inc(y_ps, 1)

            tokens(0, 0)
            hidden(0, 0, 0)
            with pe.Fori(0, EXPERTS // 2 - 1) as i:
                tokens(2 * i + 1, 1)
                answers_(2 * i, 0)
                hidden(2 * i + 1, 1, i)
                tokens(2 * i + 2, 0)
                answers_(2 * i + 1, 1)
                hidden(2 * i + 2, 0, i + 1)
            e = EXPERTS - 1
            tokens(e, 1)
            answers_(e - 1, 0)
            hidden(e, 1, e // 2)
            answers_(e, 1)


def expert_order(eng, tokens, answers_, hidden):
    tokens(0, 0)
    hidden(0)
    with eng.Fori(0, EXPERTS // 2 - 1) as i:
        tokens(2 * i + 1, 1)
        answers_(2 * i, 0, i)
        hidden(2 * i + 1)
        tokens(2 * i + 2, 0)
        answers_(2 * i + 1, 1, i)
        hidden(2 * i + 2)
    e = EXPERTS - 1
    tokens(e, 1)
    answers_(e - 1, 0, e // 2)
    hidden(e)
    answers_(e, 1, e // 2)


def token_table(np):
    p = np.arange(P)[:, None]
    same = lambda a: np.tile(a, (P, 1))
    tokens = np.arange(TILES)[None, :] * P + p
    places = (np.arange(EXPERTS)[None, :, None] * CAP + p[:, :, None] * ET + np.arange(ET)[None, None, :]).reshape(P, -1)
    return np.concatenate([tokens, places, same(np.arange(EXPERTS)), same(np.arange(EXPERTS) * CAP)], 1).astype(np.float32)


BT = SEQ // P
POL = 3
SPLIT_Q = (0, 0, 0, 1, 1, 2)
SPLIT_K = (0, 1, 2, 0, 1, 0)
KR = len(SPLIT_Q) * HD
KM = KR + 3
VW = HD + 1
MASKED = -1e30
SPAN = (0, 512, 1024, 896)
WIDTH = 1280


def stage_b(nc, x, wq, bq, wk, bk, wv, bv, wo, bo, pw1, pb1, pw2, pb2, sw1, sb1, sw2, sb2, parts, out):
    x_v = x.rearrange("(t p) n -> p t n", p=P)
    o_v = out.rearrange("(t p) n -> p t n", p=P)
    w_view = parts.rearrange("s i j p n -> s p (i j) n")
    r_view = parts.rearrange("s i (w c) (h d) n -> s i w d (c h) n", c=DC, d=HD)
    with Stage(nc, "b") as st:
        sb, ps, sem = st.sb, st.ps, st.sem
        xn = sb("xn", [P, TILES, D])
        qs = sb("qs", [P, 2, HEADS, SEQ], BF16)
        ks = sb("ks", [P, 2, HEADS, SEQ], BF16)
        ident = sb("ident", [P, P])
        ident_b = sb("ident_b", [P, P], BF16)
        ones_b = sb("ones_b", [P, P], BF16)
        ones = sb("ones", [P, P])
        after = sb("after", [P, P])
        mask_s = sb("mask_s", [P, P], BF16)
        mask_t = sb("mask_t", [P, P], BF16)
        wT = sb("wT", [P, DC, 4 * D])
        bias3 = sb("bias3", [P, D], BF16)
        bvb = sb("bvb", [P, D])
        bcol = sb("bcol", [P, 4])
        stg = sb("stg", [P, BT, D])
        xT = sb("xT", [P, DC, SEQ])
        qf = sb("qf", [P, 4, SEQ])
        qp = sb("qp", [P, 3, 4, SEQ], BF16)
        vw = sb("vw", [P, BT, D])
        va = sb("va", [P, 2, BT, HEADS, VW])
        suf = sb("suf", [P, BT, HEADS, VW])
        ob = sb("ob", [P, HEADS, BT, VW])
        cx = sb("cx", [P, BT, D])
        pt = sb("pt", [P, 2, WIDTH])
        mneg = sb("mneg", [P, 2, HEADS, BT])
        mrest = sb("mrest", [P, 2, HEADS * BT])
        mpart = sb("mpart", [P, 4, HEADS * BT], BF16)
        mT = sb("mT", [P, 2, P], BF16)
        wm = sb("wm", [P, HEADS, BT])
        rd = sb("rd", [P, HEADS, BT])
        gq = sb("gq", [P, DC, BATCH])
        ng = sb("ng", [P, BATCH, HEADS])
        bn = pt[:, 0, 0:6 * TILES].rearrange("p (t n) -> p t n", n=6)
        mean = sb("mean", [P, TILES])
        rstd = sb("rstd", [P, TILES])
        tmp = qf[:, 0, 0:2 * TILES].rearrange("p (a n) -> p a n", a=2)
        mean_sq = tmp[:, 0, :]
        f32 = lambda a: a.rearrange("p h n -> p (h n)").bitcast(F32)
        wn = f32(qs[:, 0, :, :])[:, 0:8 * D].rearrange("p (w o n) -> p w o n", w=4, o=DC)
        hn = f32(qs[:, 0, :, :])[:, 8 * D:12 * D].rearrange("p (w n) -> p w n", w=4)
        hT_ = f32(qs[:, 1, :, :])[:, 0:8 * P].rearrange("p (w c n) -> p w c n", w=4, c=DC)
        pool_ = f32(qs[:, 1, :, :])[:, 8 * P:]
        take = lambda lo, n, parts_=P: pool_[0:parts_, lo:lo + n]
        sel = take(0, 31)
        hb = take(32, 4)
        w2n = take(64, P, POL * HEADS)
        s2n = take(192, P, POL)
        w2T = take(320, POL * HEADS + POL)
        xm = take(384, D, BATCH)
        xmT = take(640, DC * BATCH).rearrange("p (c b) -> p c b", c=DC)
        hid = take(680, 4 * BATCH).rearrange("p (w b) -> p w b", w=4)
        b2 = take(760, POL * HEADS + POL, BATCH)
        gl = take(820, POL * HEADS, BATCH).rearrange("p (a h) -> p a h", a=POL)
        pl = take(880, POL, BATCH)
        gs = take(890, 8, BATCH)
        gate = take(900, HEADS, BATCH)
        gch = take(920, D, BATCH)
        gdiag = take(1180, BATCH * HEADS, BATCH).rearrange("p (b h) -> p b h", b=BATCH)
        brow = f32(ks[:, 0, :, :])[0:1, 0:2 * D].rearrange("p (a n) -> p a n", a=2)
        bpart = ks[0:1, 1, 0:3, 0:D]

        p_s = ps("p_s", [P, 3, 512])
        p_t = ps("p_t", [P, 3, 512])
        p_p = ps("p_p", [P, 2, 512])

        loaded = [sem(f"loaded{c}") for c in range(CHUNKS)]
        names = ("const w_in b_in g_in varok sdok normed wt_ps wt_ok bsplit bias_in mean_ps mean_ok mlp_ps mlp_ok "
                 "gate_ps gate_ok gelu e_in e_out free_ok staged xt_ps xt_ok qk_ps qk_ev qk_hi q_parts v_ps v_ev va_ok "
                 "suf_ps suf_ev ct_ps ct_ok ctx_ok o_ps o_ev s_ps smax t_ps exp_ev pv_ps pv_ev m_ok mt_ps mt_ok "
                 "m_in parts_out xr_in x_out w_ready w_exp ld_free dch pch").split()
        S_ = {n: sem(n) for n in names}
        (const, w_in, b_in, g_in, varok, sdok, normed, wt_ps, wt_ok, bsplit, bias_in, mean_ps, mean_ok, mlp_ps, mlp_ok,
         gate_ps, gate_ok, gelu, e_in, e_out, free_ok, staged, xt_ps, xt_ok, qk_ps, qk_ev, qk_hi, q_parts, v_ps, v_ev, va_ok,
         suf_ps, suf_ev, ct_ps, ct_ok, ctx_ok, o_ps, o_ev, s_ps, smax, t_ps, exp_ev, pv_ps, pv_ev, m_ok, mt_ps, mt_ok,
         m_in, parts_out, xr_in, x_out, w_ready, w_exp, ld_free, dch, pch) = [S_[n] for n in names]
        stacked = [[sem(f"stacked{par}_{g}") for g in range(2)] for par in range(2)]
        block = st.ctx.enter_context(nc.Block())
        flat = lambda a: a.rearrange("p a n -> p (a n)")
        H3, M2 = 3 * HEADS, 2
        GH = HEADS // 2

        def steps(eng, step, ch=None, marks=0):
            step(0, 0, proj=True, s=False, t=False, fin=False)
            step(1, 1, proj=True, s=True, t=False, fin=False)
            step(2, 0, proj=True, s=True, t=True, fin=False)
            with eng.Fori(0, (BATCH - 4) // 2) as i:
                if ch:
                    ch.enter(i, 2 * marks)
                step(2 * i + 3, 1, half=i + 1)
                step(2 * i + 4, 0, half=i + 2)
            if ch:
                ch.leave((BATCH - 4) // 2)
            step(BATCH - 1, 1)
            step(BATCH, 0, proj=False)
            step(BATCH + 1, 1, proj=False, s=False)
            step(BATCH + 2, 0, proj=False, s=False, t=False)

        @block.sync
        def _(sp):
            for c in range(CHUNKS):
                sp.dma_start(xn[:, c * CH:(c + 1) * CH, :], x_v[:, c * CH:(c + 1) * CH, :]).then_inc(loaded[c], 16)
            sp.wait_ge(bsplit, 1)
            sp.wait_ge(const, 6)
            for i in range(3):
                sp.dma_start(bias3[i:i + 1, :], bpart[0:1, i, :]).then_inc(bias_in, 16)

            def step(k, par, proj=True, s=True, t=True, fin=True, half=None):
                half = k // 2 if half is None else half
                if t:
                    sp.wait_ge(mt_ok, k - 1)
                    for i in range(3):
                        sp.dma_start(qs[KR + i:KR + i + 1, par, :, :].rearrange("a h (i n) -> a (h i) n", n=P),
                                     mT[i % 2 * 64:i % 2 * 64 + 64, i // 2, :]).then_inc(m_in, 16)
                if fin:
                    sp.dma_start(xn[:, bass.ds(BT * (k - 3), BT), :], x_v[:, bass.ds(BT * (k - 3), BT), :]).then_inc(xr_in, 16)
                if proj:
                    sp.wait_ge(q_parts, k + 1)
                    sp.dma_start(w_view[par], qp[:, :, :, :].rearrange("p i j n -> p (i j) n")).then_inc(parts_out, 16)
                if fin:
                    sp.wait_ge(o_ev, BT * (k - 2))
                    sp.dma_start(o_v[:, bass.ds(BT * (k - 3), BT), :], xn[:, bass.ds(BT * (k - 3), BT), :]).then_inc(x_out, 16)
                if proj:
                    sp.wait_ge(parts_out, 16 * k + 16)
                    for g in range(2):
                        if t:
                            sp.wait_ge(t_ps, H3 * (k - 2) + 3 * GH * (g + 1))
                        for q, to, order in ((0, qs, SPLIT_Q), (1, ks, SPLIT_K)):
                            for r, part in enumerate(order):
                                sp.dma_start(to[r * HD:(r + 1) * HD, par, g * GH:(g + 1) * GH, :],
                                             r_view[par, part, q, :, g * GH:(g + 1) * GH, :]).then_inc(stacked[par][g], 16)

            sp.wait_ge(free_ok, 1)
            steps(sp, step)
            sp.wait_ge(x_out, 16 * BATCH)

        @block.gpsimd
        def _(pool):
            ch = Chain(pool, pch)
            for a, v in ((ident, 0.0), (ident_b, 0.0), (ones_b, 1.0), (ones, 1.0), (after, 1.0), (mask_s, 0.0), (mask_t, 0.0), (bias3, 0.0)):
                ch.mark(pool.memset(a[:, :], v))
            ch.mark(pool.memset(va[:, :, :, :, :], 1.0))
            ch.mark(pool.memset(sel, 0.0))
            ch.mark(pool.memset(mpart[:, 3, :], 0.0))
            ch.settle()
            aff = lambda a, op, fill, base, step, mult: pool.affine_select(out=a, in_=a, compare_op=op, fill=fill, base=base, pattern=[[step, a.shape[1]]], channel_multiplier=mult)
            aff(ident[:, :], ALU.not_equal, 1.0, 0, -1, 1).then_inc(const, 1)
            aff(ident_b[:, :], ALU.not_equal, 1.0, 0, -1, 1).then_inc(const, 1)
            aff(after[:, :], ALU.is_gt, 0.0, 0, -1, 1).then_inc(const, 1)
            aff(mask_s[:, :], ALU.is_ge, MASKED, 0, -1, 1).then_inc(const, 1)
            aff(mask_t[:, :], ALU.is_ge, MASKED, 0, 1, -1).then_inc(const, 1)
            pool.memset(sel[:, 15:16], 1.0 / SEQ).then_inc(const, 1)
            pool.wait_ge(free_ok, 1)
            pool.wait_ge(g_in, 112)

            def step(k, par, proj=True, s=True, t=True, fin=True, half=None):
                if s:
                    pool.wait_ge(v_ev, BT * k)
                    if t:
                        wait(pool, pv_ps, HEADS * (k - 2) + M2)
                        wait(pool, suf_ps, BT * (k - 2))
                    pool.tensor_tensor(va[:, 1 - par, :, :, 0:HD], vw[:, :, :].rearrange("p t (h c) -> p t h c", c=HD),
                                       bvb[:, :].rearrange("p (h c) -> p h c", c=HD).unsqueeze(1).to_broadcast([P, BT, HEADS, HD]), ALU.add).then_inc(va_ok, 1)
                if proj:
                    wait(pool, xt_ps, k)
                    pool.tensor_copy(stg[:, :, :], xn[:, bass.ds(BT * k, BT), :]).then_inc(staged, 1)
                    pool.wait_ge(qk_hi, k + 1)
                    ch.then(pool.tensor_tensor(flat(qp[:, 1, :, :]), flat(qf[:, :, :]), flat(qp[:, 0, :, :]), ALU.subtract))
                    ch.then(pool.tensor_tensor(flat(qf[:, :, :]), flat(qf[:, :, :]), flat(qp[:, 0, :, :]), ALU.subtract))
                    pool.tensor_tensor(flat(qp[:, 2, :, :]), flat(qf[:, :, :]), flat(qp[:, 1, :, :]), ALU.subtract).then_inc(q_parts, 1)

            steps(pool, step, ch, 2)

        @block.scalar
        def _(act):
            for i, w in enumerate((wq, wk, wv, wo)):
                act.dma_start(wn[:, i, :, :], w.rearrange("(c p) n -> p c n", p=P)).then_inc(w_in, 16)
            act.dma_start(hn[:, 0, :], sw1).then_inc(w_in, 16)
            act.dma_start(hn[:, 1:4, :], pw1.rearrange("a p n -> p a n")).then_inc(w_in, 16)
            act.dma_start(w2n, pw2.rearrange("a h p -> (a h) p")).then_inc(w_in, 16)
            act.dma_start(s2n, sw2).then_inc(w_in, 16)
            act.dma_start(brow[0:1, 0, :], bo.rearrange("(a n) -> a n", a=1)).then_inc(b_in, 16)
            act.dma_start(bvb[:, :], bv.rearrange("(a n) -> a n", a=1).to_broadcast([P, D])).then_inc(g_in, 16)
            with nc.allow_non_contiguous_dma(reason="a few hundred biases to their partitions"):
                for i, b in enumerate((bq, bk)):
                    act.dma_start(bcol[:, 2 * i:2 * i + 2], b.rearrange("(c p) -> p c", p=P)).then_inc(g_in, 16)
                act.dma_start(hb[:, 0:1], sb1.rearrange("(p a) -> p a", a=1)).then_inc(g_in, 16)
                act.dma_start(hb[:, 1:4], pb1.rearrange("a p -> p a")).then_inc(g_in, 16)
            act.dma_start(b2[:, 0:POL * HEADS], pb2.rearrange("(u a) h -> u (a h)", u=1).to_broadcast([BATCH, POL * HEADS])).then_inc(g_in, 16)
            act.dma_start(b2[:, POL * HEADS:], sb2.rearrange("(u a) -> u a", u=1).to_broadcast([BATCH, POL])).then_inc(g_in, 16)
            act.wait_ge(varok, 1)
            nc.scalar.activation(rstd[:, :], mean_sq, ACT.Sqrt).then_inc(sdok, 1)
            for i in range(4):
                act.wait_ge(wt_ps, i + 1)
                nc.scalar.copy(wT[:, :, i * D:(i + 1) * D], (p_s[:, i, :] if i < 3 else p_t[:, 0, :]).rearrange("p (c n) -> p c n", c=DC)).then_inc(wt_ok, 1)
            for i in range(2):
                act.wait_ge(wt_ps, 5 + i)
                nc.scalar.copy(hT_[:, 2 * i:2 * i + 2, :, :], p_t[:, 1 + i, :].rearrange("p (w c n) -> p w c n", w=2, c=DC)).then_inc(wt_ok, 1)
            act.wait_ge(wt_ps, 7)
            nc.scalar.copy(w2T, p_p[:, 0, 0:POL * HEADS + POL]).then_inc(wt_ok, 1)
            act.wait_ge(mlp_ps, 2)
            act.wait_ge(g_in, 112)
            for i in range(4):
                nc.scalar.activation(hid[:, i, :], p_t[:, 0, i * BATCH:(i + 1) * BATCH], ACT.Gelu, bias=hb[:, i:i + 1]).then_inc(gelu, 1)
            act.wait_ge(e_in, 1)
            nc.scalar.activation(gl, gl, ACT.Exp).then_inc(e_out, 1)
            nc.scalar.activation(pl, pl, ACT.Exp).then_inc(e_out, 1)
            act.wait_ge(free_ok, 1)
            act.sem_inc(exp_ev, 3)

            def step(k, par, proj=True, s=True, t=True, fin=True, half=None):
                if t:
                    act.wait_ge(mt_ps, k - 1)
                    wait(act, m_in, 48 * (k - 2))
                    nc.scalar.copy(mT[:, :, :], p_p[:, 1, 0:P].bitcast(BF16).rearrange("p (a n) -> p a n", a=2)).then_inc(mt_ok, 1)
                if proj:
                    act.wait_ge(xt_ps, k + 1)
                    nc.scalar.copy(xT[:, :, :], p_t[:, 0:2, :]).then_inc(xt_ok, 1)
                    act.wait_ge(qk_ev, 4 * k + 4)
                    wait(act, parts_out, 16 * k)
                    nc.scalar.copy(flat(qp[:, 0, :, :]), flat(qf[:, :, :])).then_inc(qk_hi, 1)
                    wait(act, va_ok, k)
                    for i in range(BT):
                        act.wait_ge(v_ps, BT * k + i + 1)
                        nc.scalar.copy(vw[:, i, :], p_p[:, i % 2, 0:D]).then_inc(v_ev, 1)
                if t:
                    wait(act, ctx_ok, k - 2)
                    for i in range(BT):
                        act.wait_ge(suf_ps, BT * (k - 2) + i + 1)
                        nc.scalar.copy(suf[:, i, :, :].rearrange("p h c -> p (h c)"), p_s[:, i % 3, 0:HEADS * VW]).then_inc(suf_ev, 1)
                    act.wait_ge(w_ready, k - 1)
                    nc.scalar.activation(wm[:, :, :], wm[:, :, :], ACT.Exp).then_inc(w_exp, 1)
                if fin:
                    act.wait_ge(ct_ps, k - 2)
                    nc.scalar.copy(xT[:, :, :], p_t[:, 0:2, :]).then_inc(ct_ok, 1)
                if t:
                    with act.Fori(0, HEADS // 2) as j:
                        for q in range(2):
                            head = HEADS * (k - 2) + 2 * j + q
                            act.wait_ge(pv_ps, head + 1)
                            for m, (lo, hi) in enumerate(((0, 512), (512, 1024), (1024, 1280))):
                                act.wait_ge(t_ps, 3 * head + m + 1)
                                nc.scalar.activation(pt[:, q, lo:hi], p_t[:, m, 0:hi - lo], ACT.Exp).then_inc(exp_ev, 1)

            steps(act, step)

        @block.vector
        def _(dve):
            ch = Chain(dve, dch)
            V = nc.vector
            for c in range(CHUNKS):
                dve.wait_ge(loaded[c], 16)
                with dve.Fori(c * CH, c * CH + CH) as t:
                    ch.enter(t - c * CH, 1)
                    ch.mark(V.bn_stats(flat(bn[:, bass.ds(t, 1), :]), flat(xn[:, bass.ds(t, 1), :])))
                ch.leave(CH)
            ch.settle()
            ln_stats(nc, ch, bn, mean, tmp, varok)
            dve.wait_ge(sdok, 1)
            ch.then(V.reciprocal(rstd[:, :], rstd[:, :]))
            with dve.Fori(0, TILES) as t:
                x_t = flat(xn[:, bass.ds(t, 1), :])
                V.tensor_scalar(x_t, x_t, mean[:, bass.ds(t, 1)], rstd[:, bass.ds(t, 1)], ALU.subtract, ALU.mult).then_inc(normed, 1)
            dve.wait_ge(b_in, 16)
            split3(nc, ch, brow, bpart, bsplit)
            dve.wait_ge(mean_ps, 1)
            V.tensor_copy(xm, p_p[0:BATCH, 1, 0:D]).then_inc(mean_ok, 1)
            dve.wait_ge(mlp_ps, 1)
            V.tensor_copy(flat(xmT), p_p[:, 1, 0:DC * BATCH]).then_inc(mlp_ok, 1)
            dve.wait_ge(gate_ps, 1)
            dve.wait_ge(g_in, 112)
            ch.mark(V.tensor_tensor(flat(gl), p_p[0:BATCH, 0, 0:POL * HEADS], b2[:, 0:POL * HEADS], ALU.add))
            ch.then(V.tensor_tensor(pl, p_p[0:BATCH, 0, POL * HEADS:POL * HEADS + POL], b2[:, POL * HEADS:], ALU.add))
            ch.mark(V.tensor_reduce(gs[:, 0:POL].unsqueeze(2), gl, AX.X, ALU.max))
            ch.then(V.tensor_reduce(gs[:, POL:POL + 1], pl, AX.X, ALU.max))
            ch.mark(V.tensor_tensor(gl, gl, gs[:, 0:POL].unsqueeze(2).to_broadcast([BATCH, POL, HEADS]), ALU.subtract))
            V.tensor_scalar(pl, pl, gs[:, POL:POL + 1], None, ALU.subtract).then_inc(e_in, 1)
            dve.wait_ge(e_out, 2)
            ch.mark(V.tensor_reduce(gs[:, 0:POL].unsqueeze(2), gl, AX.X, ALU.add))
            ch.then(V.tensor_reduce(gs[:, POL:POL + 1], pl, AX.X, ALU.add))
            ch.then(V.reciprocal(gs[:, 0:POL + 1], gs[:, 0:POL + 1]))
            ch.then(V.tensor_scalar(pl, pl, gs[:, POL:POL + 1], None, ALU.mult))
            ch.then(V.tensor_tensor(gs[:, 0:POL], gs[:, 0:POL], pl, ALU.mult))
            ch.then(V.tensor_scalar(gate, gl[:, 0, :], gs[:, 0:1], None, ALU.mult))
            for i in range(1, POL):
                ch.then(V.scalar_tensor_tensor(gate, gl[:, i, :], gs[:, i:i + 1], gate, ALU.mult, ALU.add))
            ch.then(V.tensor_scalar(gch.rearrange("p (h c) -> p h c", c=HD), gate.unsqueeze(2).to_broadcast([BATCH, HEADS, HD]), 0.25, None, ALU.mult))
            ch.then(V.tensor_scalar(gate, gate, -1e9, None, ALU.mult))
            V.tensor_tensor(gdiag, ident[0:BATCH, 0:BATCH].unsqueeze(2).to_broadcast([BATCH, BATCH, HEADS]),
                            gate.unsqueeze(1).to_broadcast([BATCH, BATCH, HEADS]), ALU.mult).then_inc(gate_ok, 1)
            dve.wait_ge(gate_ps, 2)
            ch.mark(V.tensor_copy(flat(gq[:, :, :]), p_p[:, 1, 0:DC * BATCH]))
            ch.settle()
            V.tensor_copy(flat(ng[:, :, :]), p_t[:, 1, 0:BATCH * HEADS]).then_inc(free_ok, 1)
            dve.wait_ge(free_ok, 1)
            dve.sem_inc(smax, 3)
            dve.sem_inc(pv_ev, 1)
            V.memset(ks[KR:P, :, :, :], 1.0).then_inc(ld_free, 1)

            def step(k, par, proj=True, s=True, t=True, fin=True, half=None):
                if proj:
                    wait(dve, q_parts, k)
                    for j in range(4):
                        dve.wait_ge(qk_ps, 4 * k + j + 1)
                        src = p_s[:, j, :] if j < 3 else p_t[:, 2, :]
                        if j < 2:
                            V.tensor_scalar(qf[:, j, :], src, bcol[:, j:j + 1], gq[:, j, bass.ds(k, 1)], ALU.add, ALU.mult).then_inc(qk_ev, 1)
                        else:
                            V.tensor_scalar(qf[:, j, :], src, bcol[:, j:j + 1], None, ALU.add).then_inc(qk_ev, 1)
                if t:
                    V.tensor_tensor(wm[:, :, :], mneg[:, par, :, :], ng[:, bass.ds(k - 2, 1), :].rearrange("p a h -> p h a").to_broadcast([P, HEADS, BT]), ALU.add).then_inc(w_ready, 1)
                if fin:
                    dve.wait_ge(xr_in, 16 * (k - 2))
                    for i in range(BT):
                        dve.wait_ge(o_ps, BT * (k - 3) + i + 1)
                        x_t = flat(xn[:, bass.ds(BT * (k - 3) + i, 1), :])
                        V.tensor_tensor(x_t, p_p[:, i % 2, 0:D], x_t, ALU.add).then_inc(o_ev, 1)
                if s:
                    for q in range(2):
                        head(k, par, q, s, t and q > 0, q)
                    with dve.Fori(1, HEADS // 2) as j:
                        for q in range(2):
                            head(k, par, 2 * j + q, s, t, q)
                elif t:
                    head(k, par, 1, False, True, 1)
                    with dve.Fori(1, HEADS // 2) as j:
                        for q in range(2):
                            head(k, par, 2 * j + q, False, True, q)
                if t:
                    head(k, par, HEADS, False, True, 0)
                if s:
                    dve.wait_ge(smax, H3 * k + 3)
                    wait(dve, mt_ps, k - 1)
                    m = mneg[:, 1 - par, :, :].rearrange("p h i -> p (h i)")
                    ch.then(V.tensor_copy(mpart[:, 0, :], m))
                    ch.then(V.tensor_tensor(mrest[:, 0, :], m, mpart[:, 0, :], ALU.subtract))
                    ch.then(V.tensor_copy(mpart[:, 1, :], mrest[:, 0, :]))
                    ch.then(V.tensor_tensor(mrest[:, 1, :], mrest[:, 0, :], mpart[:, 1, :], ALU.subtract))
                    V.tensor_copy(mpart[:, 2, :], mrest[:, 1, :]).then_inc(m_ok, 1)
                if t:
                    dve.wait_ge(pv_ev, HEADS * (k - 1) + 1)
                    dve.wait_ge(suf_ev, BT * (k - 1))
                    dve.wait_ge(w_exp, k - 1)
                    by = lambda a: a.rearrange("p i h c -> p h i c")
                    ch.then(V.tensor_tensor(by(suf[:, :, :, :]), by(suf[:, :, :, :]), wm[:, :, :].unsqueeze(3).to_broadcast([P, HEADS, BT, VW]), ALU.mult))
                    ch.then(V.tensor_tensor(ob[:, :, :, :], ob[:, :, :, :], by(suf[:, :, :, :]), ALU.add))
                    ch.then(V.reciprocal(rd[:, :, :].unsqueeze(3), ob[:, :, :, HD:VW]))
                    wait(dve, ct_ps, k - 2)
                    V.tensor_tensor(cx[:, :, :].rearrange("p i (h c) -> p h i c", c=HD), ob[:, :, :, 0:HD],
                                    rd[:, :, :].unsqueeze(3).to_broadcast([P, HEADS, BT, HD]), ALU.mult).then_inc(ctx_ok, 1)
                    dve.wait_ge(ctx_ok, k - 1)

            def head(k, par, h, s, t, q):
                if s:
                    first = 3 * (HEADS * (k - 1) + h)
                    to = lambda i: mneg[:, 1 - par, bass.ds(h, 1), i]
                    red = lambda i, src: V.tensor_reduce(to(i), src, AX.X, ALU.max, negate=True)
                    dve.wait_ge(s_ps, first + 1)
                    red(3, p_s[:, 0, :]).then_inc(smax, 1)
                    dve.wait_ge(s_ps, first + 2)
                    red(2, p_s[:, 1, 0:384])
                    red(0, p_s[:, 1, 384:512]).then_inc(smax, 1)
                    dve.wait_ge(s_ps, first + 3)
                    red(1, p_s[:, 2, 0:256]).then_inc(smax, 1)
                if t:
                    dve.wait_ge(pv_ps, HEADS * (k - 2) + h + M2)
                    V.tensor_copy(ob[:, bass.ds(h - 1, 1), :, :].rearrange("p a i c -> p (a i c)"), p_p[:, 1 - q, 0:BT * VW]).then_inc(pv_ev, 1)

            steps(dve, step, ch, 7)

        @block.tensor
        def _(pe):
            mm = nc.tensor.matmul
            tr = nc.tensor.transpose
            pe.wait_ge(const, 6)
            pe.wait_ge(w_in, 128)
            for i in range(4):
                dst = p_s[:, i, :] if i < 3 else p_t[:, 0, :]
                for c in range(DC):
                    for o in range(DC):
                        last = tr(dst[:, c * D + o * P:c * D + (o + 1) * P], wn[:, i, o, c * P:(c + 1) * P], ident[:, :])
                last.then_inc(wt_ps, 1)
            for i in range(2):
                for w in range(2):
                    for c in range(DC):
                        last = tr(p_t[:, 1 + i, (2 * w + c) * P:(2 * w + c + 1) * P], hn[:, 2 * i + w, c * P:(c + 1) * P], ident[:, :])
                last.then_inc(wt_ps, 1)
            tr(p_p[:, 0, 0:POL * HEADS], w2n, ident[0:POL * HEADS, 0:POL * HEADS])
            tr(p_p[:, 0, POL * HEADS:POL * HEADS + POL], s2n, ident[0:POL, 0:POL]).then_inc(wt_ps, 1)
            for b in range(BATCH):
                pe.wait_ge(normed, BT * (b + 1))
                for i in range(BT):
                    last = mm(p_p[0:BATCH, 1, 0:D], sel[:, 15 - b:31 - b], xn[:, BT * b + i, :], start=b + i == 0, stop=b == BATCH - 1 and i == BT - 1)
            last.then_inc(mean_ps, 1)
            pe.wait_ge(mean_ok, 1)
            for c in range(DC):
                last = tr(p_p[:, 1, c * BATCH:(c + 1) * BATCH], xm[:, c * P:(c + 1) * P], ident[0:BATCH, 0:BATCH])
            last.then_inc(mlp_ps, 1)
            pe.wait_ge(mlp_ok, 1)
            pe.wait_ge(wt_ok, 7)
            for w in range(4):
                for c in range(DC):
                    last = mm(p_t[:, 0, w * BATCH:(w + 1) * BATCH], hT_[:, w, c, :], xmT[:, c, :], start=c == 0, stop=c == DC - 1)
            last.then_inc(mlp_ps, 1)
            pe.wait_ge(gelu, 4)
            for a in range(POL):
                mm(p_p[0:BATCH, 0, a * HEADS:(a + 1) * HEADS], hid[:, 1 + a, :], w2T[:, a * HEADS:(a + 1) * HEADS], start=True, stop=True)
            mm(p_p[0:BATCH, 0, POL * HEADS:POL * HEADS + POL], hid[:, 0, :], w2T[:, POL * HEADS:], start=True, stop=True).then_inc(gate_ps, 1)
            pe.wait_ge(gate_ok, 1)
            for c in range(DC):
                tr(p_p[:, 1, c * BATCH:(c + 1) * BATCH], gch[:, c * P:(c + 1) * P], ident[0:BATCH, 0:BATCH])
            mm(p_t[:, 1, 0:BATCH * HEADS], ones[0:BATCH, :], gdiag.rearrange("p b h -> p (b h)"), start=True, stop=True).then_inc(gate_ps, 1)
            pe.wait_ge(free_ok, 1)
            pe.wait_ge(bias_in, 48)
            pe.wait_ge(ld_free, 1)
            pe.sem_inc(pv_ps, M2)

            def step(k, par, proj=True, s=True, t=True, fin=True, half=None):
                half = k // 2 if half is None else half
                if t:
                    pe.wait_ge(m_ok, k - 1)
                    pe.wait_ge(pv_ev, HEADS * (k - 2) + 1)
                    pe.wait_ge(v_ev, BT * k if proj else BT * min(k, BATCH))
                    for i in range(2):
                        last = tr(p_p[:, 1, i * P // 2:(i + 1) * P // 2].bitcast(BF16), mpart[:, 2 * i:2 * i + 2, :].rearrange("p a n -> p (a n)"), ident_b[:, :])
                    last.then_inc(mt_ps, 1)
                if proj:
                    pe.wait_ge(staged, k + 1)
                    if t:
                        wait(pe, exp_ev, H3 * (k - 2) + 3)
                    for c in range(DC):
                        for i in range(BT):
                            last = tr(p_t[:, c, i * P:(i + 1) * P], stg[:, i, c * P:(c + 1) * P], ident[:, :])
                    last.then_inc(xt_ps, 1)
                    pe.wait_ge(xt_ok, k + 1)
                    if s:
                        wait(pe, smax, H3 * (k - 1) + 3)
                    for j in range(4):
                        dst = p_s[:, j, :] if j < 3 else p_t[:, 2, :]
                        for c in range(DC):
                            last = mm(dst, wT[:, c, j * P:(j + 1) * P], xT[:, c, :], start=c == 0, stop=c == DC - 1)
                        last.then_inc(qk_ps, 1)
                    if t:
                        pe.wait_ge(mt_ok, k - 1)
                    for i in range(BT):
                        wait(pe, v_ev, BT * k + i - 1)
                        for c in range(DC):
                            last = mm(p_p[:, i % 2, 0:D], xT[:, c, i * P:(i + 1) * P], wT[:, c, 2 * D:3 * D], start=c == 0, stop=c == DC - 1)
                        last.then_inc(v_ps, 1)
                if t:
                    pe.wait_ge(va_ok, k - 1)
                    if proj:
                        pe.wait_ge(qk_ev, 4 * k + 3)
                    else:
                        pe.wait_ge(smax, H3 * min(k - 1, BATCH) + 3)
                    for i in range(BT):
                        if i == 3:
                            pe.wait_ge(suf_ev, BT * (k - 2) + 1)
                        val = lambda j: va[:, par, j, :, :].rearrange("p h c -> p (h c)")
                        dst = p_s[:, i % 3, 0:HEADS * VW]
                        last = mm(dst, after[:, :], val(i), start=True, stop=i == BT - 1)
                        for j in range(i + 1, BT):
                            last = mm(dst, ones[:, :], val(j), start=False, stop=j == BT - 1)
                        last.then_inc(suf_ps, 1)
                if fin:
                    pe.wait_ge(ctx_ok, k - 2)
                    if proj:
                        pe.wait_ge(v_ev, BT * k + BT)
                    else:
                        pe.wait_ge(exp_ev, H3 * (min(k, BATCH + 2) - 2) + 3)
                        pe.wait_ge(pv_ev, HEADS * (min(k, BATCH + 2) - 2) + 1)
                        if t:
                            pe.wait_ge(mt_ok, k - 1)
                    for c in range(DC):
                        for i in range(BT):
                            last = tr(p_t[:, c, i * P:(i + 1) * P], cx[:, i, c * P:(c + 1) * P], ident[:, :])
                    last.then_inc(ct_ps, 1)
                    pe.wait_ge(ct_ok, k - 2)
                    for i in range(BT):
                        if i >= 2:
                            pe.wait_ge(o_ev, BT * (k - 3) + i - 1)
                        for c in range(DC):
                            mm(p_p[:, i % 2, 0:D], xT[:, c, i * P:(i + 1) * P], wT[:, c, 3 * D:], start=c == 0, stop=False)
                        mm(p_p[:, i % 2, 0:D], ones_b[:, :], bias3[:, :], start=False, stop=True).then_inc(o_ps, 1)
                if s:
                    half_s = half - 1 if par == 0 else half
                    for g in range(2):
                        pe.wait_ge(stacked[1 - par][g], 192 * half_s + 192)
                if t:
                    pe.wait_ge(m_in, 48 * (k - 1))
                    wait(pe, suf_ev, BT * (k - 1))
                    wait(pe, o_ev, BT * (k - 2))
                    if proj:
                        pe.wait_ge(qk_ev, 4 * k + 4)
                        pe.wait_ge(v_ev, BT * k + BT)
                    else:
                        pe.wait_ge(mt_ok, k - 1)
                elif s:
                    pe.wait_ge(qk_ev, 4 * k + 4)
                if not (s or t):
                    return
                pair(k, par, 0, s, t, first=True)
                with pe.Fori(1, HEADS // 2) as j:
                    pair(k, par, j, s, t)
                if t:
                    sums(k, par, HEADS - 1, 1)

            def pair(k, par, j, s, t, first=False):
                for q in range(2):
                    h = 2 * j + q
                    if s:
                        scores(k, par, h)
                    if t:
                        weights(k, par, h)
                        if not (first and q == 0):
                            sums(k, par, h - 1, 1 - q)

            def scores(k, par, h):
                n = 3 * (HEADS * (k - 1) + h)
                query = lambda i: qs[0:KR, 1 - par, bass.ds(h, 1), i * P:(i + 1) * P].rearrange("p a n -> p (a n)")
                keys = lambda i: ks[0:KR, 1 - par, bass.ds(h, 1), 0:(i + 1) * P].rearrange("p a n -> p (a n)")
                for m, blocks in enumerate((((3, 0),), ((2, 0), (0, 384)), ((1, 0),))):
                    pe.wait_ge(smax, n + m + 1)
                    for i, lo in blocks:
                        hi = lo + (i + 1) * P
                        mm(p_s[:, m, lo:hi], query(i), keys(i), start=True, stop=False, skip_group_check=True)
                        last = mm(p_s[:, m, hi - P:hi], ident_b[:, :], mask_s[:, :], start=False, stop=True, skip_group_check=True)
                    last.then_inc(s_ps, 1)

            def weights(k, par, h):
                n = 3 * (HEADS * (k - 2) + h)
                key = lambda j: ks[0:KM, par, bass.ds(h, 1), j * P:(j + 1) * P].rearrange("p a n -> p (a n)")
                queries = lambda j: qs[0:KM, par, bass.ds(h, 1), j * P:SEQ].rearrange("p a n -> p (a n)")
                for m, blocks in enumerate((((0, 0),), ((1, 0), (3, 384)), ((2, 0),))):
                    pe.wait_ge(exp_ev, n + m + 1)
                    for j, lo in blocks:
                        mm(p_t[:, m, lo:lo + SEQ - j * P], key(j), queries(j), start=True, stop=False, skip_group_check=True)
                        last = mm(p_t[:, m, lo:lo + P], ident_b[:, :], mask_t[:, :], start=False, stop=True, skip_group_check=True)
                    last.then_inc(t_ps, 1)

            def sums(k, par, h, q):
                head = HEADS * (k - 2) + h
                pe.wait_ge(exp_ev, 3 * head + 6)
                wait(pe, pv_ev, head)
                for i in range(BT):
                    for j in range(i + 1):
                        lo = SPAN[j] + (i - j) * P
                        last = mm(p_p[:, q, i * VW:(i + 1) * VW], pt[:, q, lo:lo + P], va[:, par, j, bass.ds(h, 1), :].rearrange("p a c -> p (a c)"), start=j == 0, stop=j == i)
                last.then_inc(pv_ps, 1)

            steps(pe, step)


def build(nc, x, a, b, ffn, tables, out):
    dram = lambda name, shape, dt=F32: nc.dram_tensor(name, shape, dt, kind="Internal").ap()
    rows_of = lambda t: t.rearrange("b s n -> (b s) n")
    x1, x3 = dram("x1", (N_TOK, D)), dram("x3", (N_TOK, D))
    x2 = dram("x2", (2 * N_TOK, D))
    rows = dram("rows", (2 * N_TOK, PAY))
    parts = dram("parts", (2, 3, 4, P, SEQ), BF16)
    tok, band_bias, first_bias = tables
    stage_a(nc, rows_of(x), *a, band_bias, first_bias, x1)
    stage_moe(nc, "m", x1, *ffn, tok, rows, x2, zero_rows=True, skip=False)
    stage_b(nc, x2[0:N_TOK, :], *b, parts, x3)
    stage_moe(nc, "n", x3, *ffn, tok, rows, rows_of(out), zero_rows=False, skip=True)


ATTN = ("wq", "bq", "wk", "bk", "wv", "bv", "wo", "bo")
GATES = ("pw1", "pb1", "pw2", "pb2", "sw1", "sb1", "sw2", "sb2")


def kernel(**inputs):
    import numpy as np
    import concourse.bacc as bacc
    from concourse.bass_utils import run_bass_kernel_spmd

    nc = bacc.Bacc("TRN2", target_bir_lowering=False, num_devices=1)
    arrays = {}

    def given(name, array):
        arrays[name] = np.ascontiguousarray(array)
        return nc.dram_tensor(name, array.shape, mybir.dt.from_np(array.dtype), kind="ExternalInput").ap()

    take = lambda prefix, names: [given(f"in_{prefix}{n}", inputs[prefix + n]) for n in names]
    x, = take("L0_attn_a_", ("x",))
    a = take("L0_attn_a_", ATTN)
    b = take("L0_attn_b_", ATTN + GATES)
    ffn = take("L0_ffn_", ("Wg", "w1", "w2"))
    band_bias, first_bias = band_tables(np)
    tables = given("token_table", token_table(np)), given("band_bias", band_bias), given("first_bias", first_bias)
    out = nc.dram_tensor("out_x", (BATCH, SEQ, D), F32, kind="ExternalOutput").ap()
    build(nc, x, a, b, ffn, tables, out)
    r = run_bass_kernel_spmd(nc, [arrays], core_ids=[0])
    return r.results[0]["out_x"]
```

```python
from contextlib import ExitStack

import concourse.bass as bass
from concourse import mybir

F32 = mybir.dt.float32
BF16 = mybir.dt.bfloat16
U32 = mybir.dt.uint32
ALU = mybir.AluOpType
ACT = mybir.ActivationFunctionType
AX = mybir.AxisListType

P = 128
BATCH, SEQ, D = 16, 512, 256
HEADS, HD = 16, 16
N_TOK = BATCH * SEQ
TILES = N_TOK // P
DC = D // P
EPS = 1e-5


def wait(eng, sem, value):
    if not isinstance(value, int) or value > 0:
        eng.wait_ge(sem, value)


class Chain:

    def __init__(self, eng, sem):
        self.eng, self.sem, self.base, self.n, self.turn, self.per_turn = eng, sem, 0, 0, None, 0

    def enter(self, turn, per_turn):
        self.base, self.n, self.turn, self.per_turn = self.base + self.n, 0, turn, per_turn

    def leave(self, turns):
        assert self.n == self.per_turn, (self.n, self.per_turn)
        self.base, self.n, self.turn = self.base + turns * self.per_turn, 0, None

    def mark(self, instruction):
        self.n += 1
        instruction.then_inc(self.sem, 1)

    def settle(self):
        value = self.base + self.n
        if self.turn is not None:
            value = self.turn * self.per_turn + value
        self.eng.wait_ge(self.sem, value)

    def then(self, instruction):
        self.mark(instruction)
        self.settle()


class Stage:

    def __init__(self, nc, name):
        self.nc, self.name, self.ctx = nc, name, ExitStack()
        self.sems = []

    def __enter__(self):
        self.ctx.__enter__()
        self.ctx.callback(self.clear)
        return self

    def clear(self):
        self.nc.clear_and_free_semaphores(self.sems)
        self.nc.all_engine_barrier()

    def __exit__(self, *a):
        return self.ctx.__exit__(*a)

    def sb(self, name, shape, dt=F32):
        return self.ctx.enter_context(self.nc.sbuf_tensor(f"{self.name}_{name}", shape, dt))

    def ps(self, name, shape, dt=F32):
        return self.ctx.enter_context(self.nc.psum_tensor(f"{self.name}_{name}", shape, dt))

    def sem(self, name):
        self.sems.append(self.nc.alloc_semaphore(f"{self.name}_{name}"))
        return self.sems[-1]


CH = 8
CHUNKS = TILES // CH
REACH = 2
EXT = TILES + 2 * REACH
E_FIRST, E_MEAN = EXT, EXT + 1
OLD = 2 * REACH
SLOTS = CH + OLD
NOFF = 2 * REACH + 2
PRO = 2 + OLD
TPB = P // BATCH
PARTS = [(EXT - REACH, EXT + 1), (0, REACH)] + [(REACH + c * CH, REACH + (c + 1) * CH) for c in range(CHUNKS)]
HALO_TILES = 2 * REACH + 1
BETWEEN = 1


def stage_a(nc, x, wq, bq, wk, bk, wv, bv, wo, bo, band_bias, first_bias, out):
    x_v = x.rearrange("(p t) n -> p t n", p=P)
    o_v = out.rearrange("(p t) n -> p t n", p=P)
    x_b = x.rearrange("(b r) n -> b r n", b=BATCH)
    o_b = out.rearrange("(b r) n -> b r n", b=BATCH)
    with Stage(nc, "a") as st:
        sb, ps, sem = st.sb, st.ps, st.sem
        xv = sb("xv", [P, EXT + 2, D])
        qkb = sb("qkb", [P, 2 * SLOTS, 2 * D])
        qkz = sb("qkz", [P, 2 * D])
        wT = sb("wT", [P, DC, 4 * D])
        bias3 = sb("bias3", [P, 4 * D], BF16)
        ones_bf = sb("ones_bf", [P, P], BF16)
        ident = sb("ident", [P, P])
        blk = sb("blk", [P, P])
        stg = sb("stg", [P, 2, D])
        xT = sb("xT", [P, 2, DC, P])
        mean = sb("mean", [P, EXT + 1])
        rstd = sb("rstd", [P, EXT + 1])
        band = sb("band", [P, TILES, NOFF])
        fbias = sb("fbias", [P, TILES])
        prd = sb("prd", [P, CH, D])
        prp = sb("prp", [P, CH, D])
        s6 = sb("s6", [P, CH * HEADS, NOFF])
        e6 = sb("e6", [P, CH * HEADS, NOFF])
        sm = sb("sm", [P, 4, CH * HEADS])
        s0 = sb("s0", [P, TILES, HEADS])
        grp = [sb(f"grp{i}", [P, CH, D]) for i in range(2)]
        cT = sb("cT", [P, 2, DC, P])
        xr = sb("xr", [P, CH, D])
        ob = sb("ob", [P, CH, D])
        r0 = sb("r0", [P, 6, HEADS])
        r0T = sb("r0T", [HEADS, P + BATCH])
        wn = qkb[:, 0:4, :].rearrange("p a (b n) -> p a b n", b=2)
        brow = prd[0:1, :, :].rearrange("p a n -> p (a n)").rearrange("p (b n) -> p b n", b=2)
        bpart = prp[0:1, :, :].bitcast(BF16).rearrange("p a n -> p (a n)").rearrange("p (b n) -> p b n", b=4)
        bn = grp[0][:, 0:2, :].rearrange("p a n -> p (a n)")[:, 0:6 * (EXT + 1)].rearrange("p (a n) -> p a n", n=6)
        tmp = grp[1][:, 0, 0:2 * (EXT + 1)].rearrange("p (a n) -> p a n", a=2)
        first_e = prd[:, 0:4, :].rearrange("p a (b h) -> p (a b) h", h=HEADS)

        p_x = ps("p_x", [P, 2, 512])
        p_qk = ps("p_qk", [P, 2, 512])
        p_v = ps("p_v", [P, 512])
        p_c = ps("p_c", [P, 2, 512])
        p_o = ps("p_o", [P, 512])

        loaded = [sem(f"loaded{c}") for c in range(CHUNKS)]
        (halo, w_in, b_in, tab_in, const, wt_ps, wt_ok, bsplit, bias_in, varok, sdok, normed, sum_ps, mean_ok,
         staged, xt_ps, xt_ok, qkv_ps, qk_ok, wrapped, pooled, pool_red, s_done, e_in, e_out, p_ok, g_dve, g_pool,
         ct_ps, ct_ok, o_ps, o_ok, xr_in, y_ok, y_out, dch, pch, f_e, f_exp, f_tr, f_trd, f_prod, f_used,
         f_ctx, f_den, f_zero, f_x, f_y) = [sem(n) for n in (
             "halo", "w_in", "b_in", "tab_in", "const", "wt_ps", "wt_ok", "bsplit", "bias_in", "varok", "sdok",
             "normed", "sum_ps", "mean_ok", "staged", "xt_ps", "xt_ok", "qkv_ps", "qk_ok", "wrapped", "pooled",
             "pool_red", "s_done", "e_in", "e_out", "p_ok", "g_dve", "g_pool", "ct_ps", "ct_ok", "o_ps", "o_ok",
             "xr_in", "y_ok", "y_out", "dve_chain", "pool_chain", "first_e_in", "first_e_out", "first_tr",
             "first_tr_used", "first_prod", "first_used", "first_ctx", "first_den", "first_zero",
             "first_x", "first_y")]
        block = st.ctx.enter_context(nc.Block())
        behind_mean = lambda c: not isinstance(c, int) or c > 0
        number = lambda c, i: PRO + CH * c + i - (0 if behind_mean(c) else 1)
        side = lambda c, i: (i if behind_mean(c) else i + 1) % 2

        @block.sync
        def _(sp):
            def chunk_in(c):
                sp.dma_start(xv[:, REACH + c * CH:REACH + (c + 1) * CH, :],
                             x_v[:, c * CH:(c + 1) * CH, :]).then_inc(loaded[c], 16)

            sp.dma_start(xv[0:P - 1, EXT - REACH:EXT, :], x_v[1:P, 0:REACH, :]).then_inc(halo, 16)
            sp.dma_start(xv[P - 1:P, EXT - REACH:EXT, :], x_v[P - 1:P, 0:REACH, :]).then_inc(halo, 16)
            sp.dma_start(xv[1:P, 0:REACH, :], x_v[0:P - 1, TILES - REACH:TILES, :]).then_inc(halo, 16)
            sp.dma_start(xv[0:1, 0:REACH, :], x_v[0:1, 0:REACH, :]).then_inc(halo, 16)
            for g in range(TPB):
                sp.dma_start(xv[g:P:TPB, E_FIRST, :], x_b[:, 0, :]).then_inc(halo, 16)
            for c in range(CHUNKS):
                chunk_in(c)
            sp.wait_ge(bsplit, 1)
            for i in range(3):
                sp.dma_start(bias3[i:i + 1, :], bpart[0:1, i, :]).then_inc(bias_in, 16)
            sp.dma_start(xr[:, :, :], x_v[:, 0:CH, :]).then_inc(xr_in, 16)
            with sp.Fori(1, CHUNKS) as c:
                sp.wait_ge(y_ok, c)
                sp.dma_start(o_v[:, bass.ds(c * CH - CH, CH), :], xr[:, :, :]).then_inc(y_out, 16)
                sp.wait_ge(y_out, c * 16)
                sp.dma_start(xr[:, :, :], x_v[:, bass.ds(c * CH, CH), :]).then_inc(xr_in, 16)
            sp.wait_ge(y_ok, CHUNKS)
            sp.dma_start(o_v[:, (CHUNKS - 1) * CH:, :], xr[:, :, :]).then_inc(y_out, 16)
            sp.wait_ge(y_out, 16 * CHUNKS)
            sp.wait_ge(f_zero, 1)
            sp.dma_start(ob[0:P:TPB, 0, :], x_b[:, 0, :]).then_inc(f_x, 16)
            sp.wait_ge(f_y, 1)
            sp.dma_start(o_b[:, 0, :], ob[0:P:TPB, 1, :]).then_inc(y_out, 16)
            sp.wait_ge(y_out, 16 * CHUNKS + 16)

        @block.gpsimd
        def _(pool):
            ch = Chain(pool, pch)
            for m, v in ((ident, 0.0), (blk, 1.0), (ones_bf, 1.0), (bias3, 0.0)):
                pool.memset(m[:, :], v).then_inc(const, 1)
            pool.wait_ge(const, 4)
            pool.affine_select(out=ident[:, :], in_=ident[:, :], compare_op=ALU.not_equal, fill=1.0,
                               base=0, pattern=[[-1, P]], channel_multiplier=1).then_inc(const, 1)
            blk_v = blk[:, :].rearrange("p (b g) -> p b g", g=TPB)
            ch.then(pool.affine_select(out=blk_v, in_=blk_v, compare_op=ALU.is_ge, fill=0.0, base=0,
                                       pattern=[[-TPB, BATCH], [0, TPB]], channel_multiplier=1))
            pool.affine_select(out=blk_v, in_=blk_v, compare_op=ALU.is_ge, fill=0.0, base=TPB - 1,
                               pattern=[[TPB, BATCH], [0, TPB]], channel_multiplier=-1).then_inc(const, 1)

            def residual(c):
                pool.wait_ge(xr_in, 16 * c + 16)
                pool.wait_ge(o_ok, CH * c + CH)
                pool.tensor_tensor(xr[:, :, :], xr[:, :, :], ob[:, :, :], ALU.add).then_inc(y_ok, 1)

            def chunk(c, par, behind=True):
                own = slice(SLOTS * par + REACH, SLOTS * par + REACH + CH)
                pool.wait_ge(qk_ok, number(c, CH))
                wait(pool, pool_red, 2 * c)
                k0 = qkz[:, D:].unsqueeze(1).to_broadcast([P, CH, D])
                q0 = qkz[:, 0:D].unsqueeze(1).to_broadcast([P, CH, D])
                if behind:
                    pool.wait_ge(g_pool, c)
                pool.tensor_tensor(prp[:, :, :], qkb[:, own, 0:D], k0, ALU.mult).then_inc(pooled, 1)
                pool.wait_ge(pool_red, 2 * c + 1)
                pool.tensor_tensor(prp[:, :, :], qkb[:, own, D:], q0, ALU.mult).then_inc(pooled, 1)
                if behind:
                    residual(c - 1)
                if isinstance(c, int) and c == 0:
                    pool.wait_ge(qk_ok, PRO + CH)
                pool.wait_ge(p_ok, c + 1)
                pool.wait_ge(pool_red, 2 * c + 2)
                wait(pool, ct_ps, CH * c)
                by_head = lambda a: a.rearrange("p t (h c) -> p t h c", c=HD)
                weight = lambda a: a.rearrange("p (t h) o -> p t h o", h=HEADS).to_broadcast([P, CH, HEADS, HD])
                row = lambda e: by_head(xv[:, e:e + 1, :]).to_broadcast([P, CH, HEADS, HD])
                ch.mark(pool.tensor_tensor(by_head(grp[1][:, :, :]), by_head(xv[:, bass.ds(CH * c + OLD, CH), :]),
                                           weight(e6[:, :, OLD:OLD + 1]), ALU.mult))
                for w, e in ((e6[:, :, NOFF - 1:NOFF], E_FIRST), (sm[:, 1, :].unsqueeze(2), E_MEAN)):
                    ch.then(pool.tensor_tensor(by_head(prp[:, :, :]), row(e), weight(w), ALU.mult))
                    add = pool.tensor_tensor(grp[1][:, :, :], grp[1][:, :, :], prp[:, :, :], ALU.add)
                    if e == E_FIRST:
                        ch.then(add)
                    else:
                        add.then_inc(g_pool, 1)

            chunk(0, 0, behind=False)
            n = ch.n
            chunk(1, 1)
            per = 2 * (ch.n - n)
            with pool.Fori(0, CHUNKS // 2 - 1) as g:
                ch.enter(g, per)
                chunk(2 * g + 2, 0)
                chunk(2 * g + 3, 1)
            ch.leave(CHUNKS // 2 - 1)
            residual(CHUNKS - 1)
            pool.wait_ge(y_ok, CHUNKS)
            pool.memset(ob[:, 0, :], 0.0).then_inc(f_zero, 1)

        @block.scalar
        def _(act):
            for i, w in enumerate((wq, wk, wv, wo)):
                act.dma_start(wn[:, i, :, :], w.rearrange("(c p) n -> p c n", p=P)).then_inc(w_in, 16)
            for i, b in enumerate((bq, bk, bv, bo)):
                act.dma_start(brow[0:1, 0, i * D:(i + 1) * D], b.rearrange("(a n) -> a n", a=1)).then_inc(b_in, 16)
            act.dma_start(band[:, :, :], band_bias).then_inc(tab_in, 16)
            act.dma_start(fbias[:, :], first_bias).then_inc(tab_in, 16)
            for i in range(4):
                act.wait_ge(wt_ps, i + 1)
                src = (p_x[:, 0, :], p_x[:, 1, :], p_qk[:, 0, :], p_qk[:, 1, :])[i].rearrange("p (c n) -> p c n", c=DC)
                nc.scalar.activation(wT[:, :, i * D:(i + 1) * D], src, ACT.Copy, scale=0.25 if i == 0 else 1.0).then_inc(wt_ok, 1)
            for i, (lo, hi) in enumerate(PARTS):
                act.wait_ge(varok, i + 1)
                nc.scalar.activation(rstd[:, lo:hi], tmp[:, 0, lo:hi], ACT.Sqrt).then_inc(sdok, 1)

            def evac_qkv(e, n, dst, par):
                act.wait_ge(qkv_ps, n + 1)
                nc.scalar.copy(dst, p_qk[:, par, :])
                nc.scalar.copy(xv[:, bass.ds(e, 1), :], p_v[:, 0:D].unsqueeze(1)).then_inc(qk_ok, 1)

            def stage(item):
                e, n, dst, par = item
                wait(act, xt_ps, n - 1)
                nc.scalar.copy(stg[:, par:par + 1, :], xv[:, bass.ds(e, 1), :]).then_inc(staged, 1)

            def tiles(items, between=None):
                stage(items[0])
                for i, (e, n, dst, par) in enumerate(items):
                    act.wait_ge(xt_ps, n + 1)
                    wait(act, qkv_ps, n - 1)
                    nc.scalar.copy(xT[:, par, :, :], p_x[:, par, 0:D].rearrange("p (c n) -> p c n", c=DC)).then_inc(xt_ok, 1)
                    if i + 1 < len(items):
                        stage(items[i + 1])
                    if i:
                        evac_qkv(*items[i - 1])
                    if i == BETWEEN and between:
                        between()
                evac_qkv(*items[-1])

            def project(c, par, between=None):
                wait(act, s_done, c - 1)
                mine, other = SLOTS * par, SLOTS * (1 - par)
                if not isinstance(c, int) or c > 0:
                    act.wait_ge(qk_ok, number(c, 0))
                    nc.scalar.copy(qkb[:, mine:mine + OLD, :], qkb[:, other + CH:other + SLOTS, :])
                tiles([(CH * c + OLD + i, number(c, i), qkb[:, mine + OLD + i, :], side(c, i)) for i in range(CH)], between)

            def exponentials(c):
                act.wait_ge(e_in, c + 1)
                nc.scalar.activation(e6[:, :, :], e6[:, :, :], ACT.Exp).then_inc(e_out, 1)

            def rest(c):
                wait(act, y_ok, c)
                for i in range(CH + 1):
                    if i < CH:
                        act.wait_ge(ct_ps, CH * c + i + 1)
                        wait(act, o_ps, CH * c + i - 1)
                        nc.scalar.copy(cT[:, i % 2, :, :], p_c[:, i % 2, 0:D].rearrange("p (c n) -> p c n", c=DC)).then_inc(ct_ok, 1)
                    if i > 0:
                        act.wait_ge(o_ps, CH * c + i)
                        nc.scalar.copy(ob[:, i - 1, :], p_o[:, 0:D]).then_inc(o_ok, 1)

            act.wait_ge(normed, HALO_TILES)
            tiles([(E_FIRST, 0, qkz[:, :], 0)] + [(e, 1 + e, qkb[:, e, :], (1 + e) % 2) for e in range(OLD)])
            project(0, 0)
            act.wait_ge(sum_ps, 1)
            nc.scalar.activation(xv[:, E_MEAN, :], p_o[:, 0:D], ACT.Copy, scale=1.0 / SEQ).then_inc(mean_ok, 1)
            act.wait_ge(mean_ok, 1)
            tiles([(E_MEAN, PRO + CH - 1, qkb[:, SLOTS, :], 1)])
            project(1, 1, lambda: exponentials(0))
            rest(0)
            with act.Fori(1, CHUNKS // 2) as g:
                project(2 * g, 0, lambda: exponentials(2 * g - 1))
                rest(2 * g - 1)
                project(2 * g + 1, 1, lambda: exponentials(2 * g))
                rest(2 * g)
            exponentials(CHUNKS - 1)
            rest(CHUNKS - 1)
            act.wait_ge(f_e, 1)
            nc.scalar.activation(first_e, first_e, ACT.Exp).then_inc(f_exp, 1)

        @block.vector
        def _(dve):
            ch = Chain(dve, dch)
            heads = lambda a: a.rearrange("p t (h c) -> p (t h) c", c=HD)
            def bias_parts():
                dve.wait_ge(b_in, 64)
                ch.then(nc.vector.tensor_scalar(brow[0:1, 0, 0:D], brow[0:1, 0, 0:D], 0.25, None, ALU.mult))
                split3(nc, ch, brow, bpart, bsplit)

            def stats(i):
                lo, hi = PARTS[i]
                if i < 2:
                    dve.wait_ge(halo, 16 * (4 + TPB))
                else:
                    dve.wait_ge(loaded[i - 2], 16)
                for e in range(lo, hi):
                    ch.mark(nc.vector.bn_stats(bn[:, e, :], xv[:, e, :]))
                ch.settle()
                ln_stats(nc, ch, bn[:, lo:hi, :], mean[:, lo:hi], tmp[:, :, lo:hi], varok)

            stats(0)
            for i, (lo, hi) in enumerate(PARTS):
                if i + 1 < len(PARTS):
                    stats(i + 1)
                dve.wait_ge(sdok, i + 1)
                ch.then(nc.vector.reciprocal(rstd[:, lo:hi], rstd[:, lo:hi]))
                for e in range(lo, hi):
                    nc.vector.tensor_scalar(xv[:, e, :], xv[:, e, :], mean[:, e:e + 1], rstd[:, e:e + 1], ALU.subtract, ALU.mult).then_inc(normed, 1)
                if i == 1:
                    bias_parts()
            dve.wait_ge(tab_in, 32)
            dve.wait_ge(bias_in, 48)

            def chunk(c, par):
                s = SLOTS * par
                dve.wait_ge(qk_ok, number(c, CH))
                q = qkb[:, s + REACH:s + REACH + CH, 0:D]
                for d in range(NOFF - 1):
                    ch.then(nc.vector.tensor_tensor(prd[:, :, :], q, qkb[:, s + d:s + d + CH, D:], ALU.mult))
                    ch.then(nc.vector.tensor_reduce(s6[:, :, d:d + 1], heads(prd[:, :, :]), AX.X, ALU.add))
                    if d == 2:
                        dve.wait_ge(pooled, 2 * c + 1)
                        nc.vector.tensor_reduce(s6[:, :, NOFF - 1:NOFF], heads(prp[:, :, :]), AX.X, ALU.add).then_inc(pool_red, 1)
                dve.wait_ge(pooled, 2 * c + 2)
                nc.vector.tensor_reduce(s0[:, bass.ds(c * CH, CH), :].rearrange("p t h -> p (t h)").unsqueeze(2), heads(prp[:, :, :]), AX.X, ALU.add).then_inc(pool_red, 1)
                dve.wait_ge(pool_red, 2 * c + 2)
                s64 = s6[:, :, :].rearrange("p (t h) o -> p t h o", h=HEADS)
                bias = band[:, bass.ds(c * CH, CH), :].unsqueeze(2).to_broadcast([P, CH, HEADS, NOFF])
                every = lambda a: a.unsqueeze(2).to_broadcast([P, CH * HEADS, NOFF])
                nc.vector.tensor_tensor(s64, s64, bias, ALU.add).then_inc(s_done, 1)
                dve.wait_ge(s_done, c + 1)
                ch.then(nc.vector.tensor_reduce(sm[:, 0, :].unsqueeze(2), s6[:, :, :], AX.X, ALU.max))
                wait(dve, g_pool, c)
                ch.mark(nc.vector.tensor_scalar(sm[:, 1, :], sm[:, 0, :], 0.0, None, ALU.is_lt))
                ch.then(nc.vector.tensor_scalar(sm[:, 2, :], sm[:, 0, :], 0.0, None, ALU.max))
                nc.vector.tensor_tensor(e6[:, :, :], s6[:, :, :], every(sm[:, 2, :]), ALU.subtract).then_inc(e_in, 1)
                dve.wait_ge(e_out, c + 1)
                ch.then(nc.vector.scalar_tensor_tensor(e6[:, :, :], s6[:, :, :], 0.0, e6[:, :, :], ALU.is_ge, ALU.mult))
                ch.then(nc.vector.tensor_reduce(sm[:, 3, :].unsqueeze(2), e6[:, :, :], AX.X, ALU.add))
                ch.then(nc.vector.tensor_tensor(sm[:, 3, :], sm[:, 3, :], sm[:, 1, :], ALU.add))
                ch.then(nc.vector.reciprocal(sm[:, 3, :], sm[:, 3, :]))
                nc.vector.tensor_tensor(e6[:, :, :], e6[:, :, :], every(sm[:, 3, :]), ALU.mult).then_inc(p_ok, 1)
                dve.wait_ge(p_ok, c + 1)
                wait(dve, ct_ps, CH * c)
                for d in range(OLD):
                    to = grp[0] if d == 0 else prd
                    v = heads(xv[:, bass.ds(CH * c + d, CH), :])
                    ch.then(nc.vector.tensor_tensor(heads(to[:, :, :]), v, e6[:, :, d:d + 1].to_broadcast([P, CH * HEADS, HD]), ALU.mult))
                    if d > 0:
                        add = nc.vector.tensor_tensor(grp[0][:, :, :], grp[0][:, :, :], prd[:, :, :], ALU.add)
                        if d < OLD - 1:
                            ch.then(add)
                        else:
                            add.then_inc(g_dve, 1)
                dve.wait_ge(g_dve, c + 1)

            n = ch.base + ch.n
            chunk(0, 0)
            per = 2 * (ch.base + ch.n - n)
            chunk(1, 1)
            with dve.Fori(0, CHUNKS // 2 - 1) as g:
                ch.enter(g, per)
                chunk(2 * g + 2, 0)
                chunk(2 * g + 3, 1)
            ch.leave(CHUNKS // 2 - 1)

            hT = lambda a: a.rearrange("p t h -> p h t")
            over_t = lambda a: a.unsqueeze(1).to_broadcast([P, TILES, HEADS])
            ch.then(nc.vector.tensor_tensor(s0[:, :, :], s0[:, :, :], fbias[:, :].unsqueeze(2).to_broadcast([P, TILES, HEADS]), ALU.add))
            nc.vector.tensor_reduce(r0[:, 0, :].unsqueeze(2), hT(s0[:, :, :]), AX.X, ALU.max).then_inc(f_den, 1)
            dve.wait_ge(f_tr, 1)
            ch.then(nc.vector.tensor_reduce(r0T[:, P:].unsqueeze(2), p_x[0:HEADS, 0, 0:P].rearrange("p (b g) -> p b g", g=TPB), AX.X, ALU.max))
            nc.vector.tensor_copy(r0T[:, 0:P].rearrange("p (b g) -> p b g", g=TPB), r0T[:, P:].unsqueeze(2).to_broadcast([HEADS, BATCH, TPB])).then_inc(f_trd, 1)
            dve.wait_ge(f_tr, 2)
            ch.mark(nc.vector.tensor_scalar(r0[:, 1, :], p_x[:, 1, 0:HEADS], 0.0, None, ALU.is_lt))
            ch.then(nc.vector.tensor_scalar(r0[:, 2, :], p_x[:, 1, 0:HEADS], 0.0, None, ALU.max))
            nc.vector.tensor_tensor(first_e, s0[:, :, :], over_t(r0[:, 2, :]), ALU.subtract).then_inc(f_e, 1)
            dve.wait_ge(f_exp, 1)
            flat = lambda a: a.rearrange("p t h -> p (t h)")
            ch.then(nc.vector.scalar_tensor_tensor(flat(s0[:, :, :]), flat(s0[:, :, :]), 0.0, flat(first_e), ALU.is_ge, ALU.mult))
            nc.vector.tensor_reduce(r0[:, 3, :].unsqueeze(2), hT(s0[:, :, :]), AX.X, ALU.add).then_inc(f_den, 1)
            dve.wait_ge(f_tr, 3)
            ch.then(nc.vector.tensor_tensor(r0[:, 4, :], p_x[:, 0, 0:HEADS], r0[:, 1, :], ALU.add))
            ch.then(nc.vector.reciprocal(r0[:, 4, :], r0[:, 4, :]))
            ch.then(nc.vector.tensor_tensor(s0[:, :, :], s0[:, :, :], over_t(r0[:, 4, :]), ALU.mult))
            dve.wait_ge(g_pool, CHUNKS)
            with dve.Fori(0, CHUNKS // 2) as i:
                for par, products in enumerate((prd, prp)):
                    c = 2 * i + par
                    dve.wait_ge(f_used, c + 1)
                    nc.vector.tensor_tensor(heads(products[:, :, :]), heads(xv[:, bass.ds(CH * c + REACH, CH), :]),
                                            flat(s0[:, bass.ds(CH * c, CH), :]).unsqueeze(2).to_broadcast([P, CH * HEADS, HD]), ALU.mult).then_inc(f_prod, 1)
            dve.wait_ge(f_used, CHUNKS + 2)
            by_head = lambda a: a.rearrange("p (h c) -> p h c", c=HD)
            ch.then(nc.vector.tensor_tensor(by_head(prd[:, 0, :]), by_head(xv[:, E_MEAN, :]), r0[:, 1, :].unsqueeze(2).to_broadcast([P, HEADS, HD]), ALU.mult))
            nc.vector.tensor_tensor(prd[:, 0, :], prd[:, 0, :], p_v[:, 0:D], ALU.add).then_inc(f_ctx, 1)
            dve.wait_ge(f_tr, 4)
            nc.vector.tensor_copy(cT[:, 0, :, :], p_x[:, 1, 0:D].rearrange("p (c n) -> p c n", c=DC)).then_inc(f_ctx, 1)
            dve.wait_ge(f_tr, 5)
            dve.wait_ge(f_x, 16)
            nc.vector.tensor_tensor(ob[:, 1, :], p_o[:, 0:D], ob[:, 0, :], ALU.add).then_inc(f_y, 1)

        @block.tensor
        def _(pe):
            mm = nc.tensor.matmul
            pe.wait_ge(const, 6)
            pe.wait_ge(w_in, 64)
            for i in range(4):
                dst = (p_x[:, 0, :], p_x[:, 1, :], p_qk[:, 0, :], p_qk[:, 1, :])[i]
                for c in range(DC):
                    for o in range(DC):
                        last = nc.tensor.transpose(dst[:, c * D + o * P:c * D + (o + 1) * P], wn[:, i, o, c * P:(c + 1) * P], ident[:, :])
                last.then_inc(wt_ps, 1)
            pe.wait_ge(wt_ok, 4)
            pe.wait_ge(bias_in, 48)

            def matmuls(n, par):
                pe.wait_ge(xt_ok, n + 1)
                for lo, hi, dst in ((0, 2 * D, p_qk[:, par, :]), (2 * D, 3 * D, p_v[:, 0:D])):
                    wait(pe, qk_ok, n if lo else n - 1)
                    for c in range(DC):
                        mm(dst, xT[:, par, c, :], wT[:, c, lo:hi], start=c == 0, stop=False)
                    last = mm(dst, ones_bf[:, :], bias3[:, lo:hi], start=False, stop=True)
                last.then_inc(qkv_ps, 1)

            def tiles(items):
                for i, (n, par) in enumerate(items):
                    pe.wait_ge(staged, n + 1)
                    wait(pe, xt_ok, n - 1)
                    for c in range(DC):
                        last = nc.tensor.transpose(p_x[:, par, c * P:(c + 1) * P], stg[:, par, c * P:(c + 1) * P], ident[:, :])
                    last.then_inc(xt_ps, 1)
                    if i:
                        matmuls(*items[i - 1])
                matmuls(*items[-1])

            def project(c):
                tiles([(number(c, i), side(c, i)) for i in range(CH)])

            def rest(c):
                pe.wait_ge(g_dve, c + 1)
                pe.wait_ge(g_pool, c + 1)
                for i in range(CH + 1):
                    if i < CH:
                        wait(pe, ct_ok, CH * c + i - 1)
                        for k in range(DC):
                            for g in range(2):
                                last = mm(p_c[:, i % 2, k * P:(k + 1) * P], grp[g][:, i, k * P:(k + 1) * P], ident[:, :], start=g == 0, stop=g == 1)
                        last.then_inc(ct_ps, 1)
                    if i > 0:
                        pe.wait_ge(ct_ok, CH * c + i)
                        wait(pe, o_ok, CH * c + i - 1)
                        out_product((i - 1) % 2).then_inc(o_ps, 1)

            def out_product(par):
                for k in range(DC):
                    mm(p_o[:, 0:D], cT[:, par, k, :], wT[:, k, 3 * D:], start=k == 0, stop=False)
                return mm(p_o[:, 0:D], ones_bf[:, :], bias3[:, 3 * D:], start=False, stop=True)

            def sum_tokens(lo, hi):
                for e in range(lo, hi):
                    pe.wait_ge(normed, HALO_TILES + e + 1)
                    last = mm(p_o[:, 0:D], blk[:, :], xv[:, REACH + e, :], start=e == 0, stop=e == TILES - 1, skip_group_check=True)
                return last

            sum_tokens(0, 2 * CH)
            tiles([(i, i % 2) for i in range(PRO - 1)])
            project(0)
            sum_tokens(2 * CH, TILES).then_inc(sum_ps, 1)
            tiles([(PRO + CH - 1, 1)])
            project(1)
            rest(0)
            with pe.Fori(1, CHUNKS // 2) as g:
                project(2 * g)
                rest(2 * g - 1)
                project(2 * g + 1)
                rest(2 * g)
            rest(CHUNKS - 1)
            pe.wait_ge(f_den, 1)
            nc.tensor.transpose(p_x[0:HEADS, 0, 0:P], r0[:, 0, :], ident[:, :]).then_inc(f_tr, 1)
            pe.wait_ge(f_trd, 1)
            nc.tensor.transpose(p_x[:, 1, 0:HEADS], r0T[:, 0:P], ident[0:HEADS, 0:HEADS]).then_inc(f_tr, 1)
            pe.wait_ge(f_den, 2)
            mm(p_x[:, 0, 0:HEADS], blk[:, :], r0[:, 3, :], start=True, stop=True).then_inc(f_tr, 1)

            def first_sums(i, first, last):
                for par, products in enumerate((prd, prp)):
                    pe.wait_ge(f_prod, 2 * i + par + 1)
                    for t in range(CH):
                        ins = mm(p_v[:, 0:D], blk[:, :], products[:, t, :], start=first and par + t == 0, stop=last and par == 1 and t == CH - 1)
                    ins.then_inc(f_used, 1)

            pe.sem_inc(f_used, 2)
            first_sums(0, True, False)
            with pe.Fori(1, CHUNKS // 2 - 1) as i:
                first_sums(i, False, False)
            first_sums(CHUNKS // 2 - 1, False, True)
            pe.wait_ge(f_ctx, 1)
            for k in range(DC):
                last = nc.tensor.transpose(p_x[:, 1, k * P:(k + 1) * P], prd[:, 0, k * P:(k + 1) * P], ident[:, :])
            last.then_inc(f_tr, 1)
            pe.wait_ge(f_ctx, 2)
            pe.wait_ge(o_ok, TILES)
            out_product(0).then_inc(f_tr, 1)


def ln_stats(nc, ch, bn, mean, tmp, done):
    half = lambda i: bn[:, :, i]
    ch.mark(nc.vector.tensor_tensor(mean[:, :], half(1), half(4), ALU.add))
    ch.mark(nc.vector.tensor_tensor(tmp[:, 0, :], half(2), half(5), ALU.add))
    ch.then(nc.vector.tensor_tensor(tmp[:, 1, :], half(1), half(4), ALU.subtract))
    ch.mark(nc.vector.tensor_scalar(mean[:, :], mean[:, :], 0.5, None, ALU.mult))
    ch.mark(nc.vector.tensor_scalar(tmp[:, 0, :], tmp[:, 0, :], 1.0 / D, EPS, ALU.mult, ALU.add))
    ch.then(nc.vector.tensor_tensor(tmp[:, 1, :], tmp[:, 1, :], tmp[:, 1, :], ALU.mult))
    nc.vector.scalar_tensor_tensor(tmp[:, 0, :], tmp[:, 1, :], 0.25, tmp[:, 0, :], ALU.mult, ALU.add).then_inc(done, 1)


def split3(nc, ch, rest, part, done):
    for i in range(3):
        copy = nc.vector.tensor_copy(part[:, i, :], rest[:, i % 2, :])
        if i == 2:
            copy.then_inc(done, 1)
        else:
            ch.then(copy)
            ch.then(nc.vector.tensor_tensor(rest[:, 1 - i % 2, :], rest[:, i % 2, :], part[:, i, :], ALU.subtract))


def band_tables(np):
    tok = np.arange(N_TOK).reshape(P, TILES)
    i = (tok % SEQ).astype(np.float32)
    bias = lambda diff: (np.exp(np.float32(-0.5) * (diff / np.float32(2.0)) ** 2)
                         + np.cos(np.float32(2.0 * np.pi) * diff / np.float32(401.0))).astype(np.float32)
    table = np.full((P, TILES, NOFF), -1e9, np.float32)
    for d in range(NOFF - 1):
        j = i + d - REACH
        table[:, :, d] = np.where((j >= 0) & (j < SEQ), bias(i - j), np.float32(-1e9))
    table[:, :, NOFF - 1] = np.where(i > REACH, bias(i), np.float32(-1e9))
    return table, bias(i)


EXPERTS, FF = 16, 1024
CAP = N_TOK // EXPERTS
FC = FF // P
ET = CAP // P
CT = 8
RC = TILES // CT
PAIRS = RC // 2
HT = 2
PAY = D + 4
MEAN, RSTD, GATE, NUM = range(D, PAY)


def stage_moe(nc, name, x, wg, w1, w2, tok, rows, out, zero_rows, skip):
    x_v = x[0:N_TOK, :].rearrange("(t p) n -> p t n", p=P)
    o_v = out[0:N_TOK, :].rearrange("(t p) n -> p t n", p=P)
    rows_v = rows[0:N_TOK, :].rearrange("(e p c) n -> e p (c n)", p=P, c=ET)
    w1_v = w1.rearrange("e (c p) f -> e p c f", p=P)
    w2_v = w2.rearrange("e (j p) n -> e p j n", p=P)
    with Stage(nc, name) as st:
        sb, ps, sem = st.sb, st.ps, st.sem
        ident = sb("ident", [P, P])
        before = sb("before", [P, P], BF16)
        ones = sb("ones", [P, P], BF16)
        wg_s = sb("wg", [P, DC, EXPERTS])
        table = sb("table", [P, 2 * TILES + 2 * EXPERTS])
        pay = sb("pay", [P, TILES, PAY])
        xs = sb("xs", [P, 2, CT, D])
        bn = sb("bn", [P, CT, 6])
        shift = sb("shift", [P, 2, CT])
        tmp = sb("tmp", [P, 2, 2, CT])
        xT = sb("xT", [P, HT, DC, 512])
        ex = sb("ex", [P, 2, CT, EXPERTS])
        pick = sb("pick", [P, CT, EXPERTS])
        loc = sb("loc", [P, CT, EXPERTS])
        hot = sb("hot", [P, CT, EXPERTS])
        hot_b = sb("hot_b", [P, CT, EXPERTS], BF16)
        seen = sb("seen", [P, 2, EXPERTS])
        seen_b = sb("seen_b", [P, EXPERTS], BF16)
        route = sb("route", [P, 7, CT])
        slot = sb("slot", [P, TILES], U32)
        taken = sb("taken", [P, EXPERTS, ET])
        spare = sb("spare", [P, 2, EXPERTS, ET])
        place_t = sb("place_t", [P, ET])
        dest = sb("dest", [P, 2, ET], U32)
        w1_s = sb("w1", [P, 2, DC, FF])
        w2_s = sb("w2", [P, 2, FC, D])
        xe = sb("xe", [P, 2, ET, PAY])
        xq = sb("xq", [P, ET, D])
        xeT = sb("xeT", [P, DC, CAP])
        hT = sb("hT", [P, FC, CAP])
        ye = sb("ye", [P, 2, ET, D])
        toks = table[:, 0:TILES]
        places = table[:, TILES:2 * TILES].rearrange("p (e c) -> p e c", c=ET)
        enum = table[:, 2 * TILES:2 * TILES + EXPERTS]
        first_row = table[:, 2 * TILES + EXPERTS:]

        p_x = ps("p_x", [P, HT, DC, 512])
        p_h = ps("p_h", [P, 2, 512])
        p_y = ps("p_y", [P, 2, 512])

        (const, tab_in, varok, sdok, shift_ok, normed, xt_ps, xt_ok, lg_ps, ex_in, ex_out, hot_ok, cum_ps, seen_ok,
         routed, zeroed, filled, scattered, xq_ok, xet_ps, xet_act, xet_dve, h_ps, h_act, h_dve, y_ps, y_ok, ye_free, go, dch, pch) = [sem(n) for n in (
             "const tab_in varok sdok shift_ok normed xt_ps xt_ok lg_ps ex_in ex_out hot_ok cum_ps seen_ok "
             "routed zeroed filled scattered xq_ok xet_ps xet_act xet_dve h_ps h_act h_dve y_ps y_ok ye_free go dve_chain pool_chain ").split()]
        loaded, w_in, xe_in, x_out = [[sem(f"{n}{k}") for k in range(2)] for n in (
            "loaded", "w_in", "xe_in", "x_out")]
        YB = 2
        block = st.ctx.enter_context(nc.Block())
        chunk = lambda c: bass.ds(c * CT, CT)

        @block.sync
        def _(sp):
            def chunk_in(c, par):
                sp.dma_start(pay[:, chunk(c), 0:D], x_v[:, chunk(c), :]).then_inc(loaded[par], 16)

            def chunk_out(c, par, i):
                sp.wait_ge(loaded[par], 16 * i + 16)
                sp.dma_start(o_v[:, chunk(c), :], pay[:, chunk(c), 0:D]).then_inc(filled, 16)

            def weights_in(e, par):
                sp.dma_start(w1_s[:, par, :, :].unsqueeze(1), w1_v[bass.ds(e, 1)].rearrange("e p c f -> p e c f")).then_inc(w_in[par], 16)
                sp.dma_start(w2_s[:, par, :, :].unsqueeze(1), w2_v[bass.ds(e, 1)].rearrange("e p j n -> p e j n")).then_inc(w_in[par], 16)

            def tokens_in(e, par):
                sp.dma_start(xe[:, par, :, :].rearrange("p a n -> p (a n)").unsqueeze(1), rows_v[bass.ds(e, 1)].rearrange("e p n -> p e n")).then_inc(xe_in[par], 16)

            for par in range(2):
                chunk_in(par, par)
            with sp.Fori(1, PAIRS) as i:
                for par in range(2):
                    chunk_out(2 * i + par - 2, par, i - 1)
                    chunk_in(2 * i + par, par)
            for par in range(2):
                chunk_out(RC - 2 + par, par, PAIRS - 1)
            for par in range(2):
                weights_in(par, par)
            sp.wait_ge(scattered, 16 * TILES)
            for par in range(2):
                tokens_in(par, par)
            with sp.Fori(0, EXPERTS // 2 - 1) as g:
                for par in range(2):
                    sp.wait_ge(y_ok, ET * (2 * g + par) + ET + YB)
                    tokens_in(2 * g + 2 + par, par)
                    weights_in(2 * g + 2 + par, par)
                    sp.wait_ge(x_out[par], 16 * ET * (g + 1))
                    sp.sem_inc(ye_free, 1)
            for par in range(2):
                sp.wait_ge(x_out[par], 16 * ET * EXPERTS // 2)

        @block.gpsimd
        def _(pool):
            ch = Chain(pool, pch)
            pool.memset(ye[:, :, :, :], 0.0).then_inc(const, 1)
            pool.dma_start(wg_s[:, :, :], wg.rearrange("(c p) n -> p c n", p=P)).then_inc(tab_in, 16)
            pool.dma_start(table[:, :], tok).then_inc(tab_in, 16)
            ch.mark(pool.memset(ident[:, :], 0.0))
            ch.mark(pool.memset(before[:, :], 1.0))
            ch.then(pool.memset(ones[:, :], 1.0))
            pool.affine_select(out=ident[:, :], in_=ident[:, :], compare_op=ALU.not_equal, fill=1.0,
                               base=0, pattern=[[-1, P]], channel_multiplier=1).then_inc(const, 1)
            pool.affine_select(out=before[:, :], in_=before[:, :], compare_op=ALU.is_gt, fill=0.0,
                               base=0, pattern=[[1, P]], channel_multiplier=-1).then_inc(const, 1)
            if zero_rows:
                pool.wait_ge(zeroed, 16 * EXPERTS)

            for t in range(TILES):
                pool.wait_ge(routed, t // CT + 2)
                pool.indirect_dma_start(rows[:, :], bass.IndirectOffsetOnAxis(ap=slot[:, t:t + 1], axis=0), pay[:, t, :], None).then_inc(scattered, 16)
            pool.wait_ge(filled, 16 * RC)

            def put(e, par):
                for c in range(ET):
                    pool.wait_ge(y_ok, ET * e + c + 1 + YB)
                    pool.sem_inc(go, 1)
                    at = bass.IndirectOffsetOnAxis(ap=dest[:, par, c:c + 1], axis=0)
                    if skip:
                        dma = pool.indirect_dma_start(out[:, :], at, ye[:, par, c, :], None, bounds_check=N_TOK - 1, oob_is_err=False)
                    else:
                        dma = pool.indirect_dma_start(out[:, :], at, ye[:, par, c, :], None)
                    dma.then_inc(x_out[par], 16)

            with pool.Fori(0, EXPERTS // 2) as i:
                for par in range(2):
                    put(2 * i + par, par)

        @block.scalar
        def _(act):
            if zero_rows:
                act.wait_ge(const, 1)
                for e in range(EXPERTS):
                    act.dma_start(rows_v[e], ye[:, :, :, :].rearrange("p a c n -> p (a c n)")[:, 0:ET * PAY]).then_inc(zeroed, 16)

            def deviation(c, par):
                act.wait_ge(varok, c + 1)
                nc.scalar.activation(pay[:, chunk(c), RSTD], tmp[:, par, 0, :], ACT.Sqrt).then_inc(sdok, 1)

            def turned(c):
                for h in range(HT):
                    act.wait_ge(xt_ps, HT * c + h + 1)
                    wait(act, lg_ps, HT * c + h - 1)
                    nc.scalar.copy(xT[:, h, :, :], p_x[:, h, :, :]).then_inc(xt_ok, 1)

            def normalise(c, par):
                act.wait_ge(shift_ok, c + 1)
                wait(act, xt_ps, HT * (c - 1))
                for t in range(CT):
                    row = lambda at, n=1: pay[:, bass.ds(c * CT + t, 1), at:at + n].rearrange("p a n -> p (a n)")
                    nc.scalar.activation(xs[:, par, t, :], row(0, D), ACT.Identity, scale=row(RSTD), bias=shift[:, par, t:t + 1]).then_inc(normed, 1)

            def exponentials(c, par):
                act.wait_ge(ex_in, c + 1)
                nc.scalar.activation(ex[:, par, :, :], ex[:, par, :, :], ACT.Exp).then_inc(ex_out, 1)

            def enter(c, par):
                deviation(c, par)
                normalise(c, par)
                turned(c)

            def step(c, par):
                exponentials(c, par)
                enter(c + 2, par)

            for par in range(2):
                enter(par, par)
            for par in range(2):
                step(par, par)
            with act.Fori(1, PAIRS - 1) as i:
                for par in range(2):
                    step(2 * i + par, par)
            for par in range(2):
                exponentials(RC - 2 + par, par)
            if zero_rows:
                act.wait_ge(zeroed, 16 * EXPERTS)

            def tokens(e, par):
                act.wait_ge(xet_ps, e + 1)
                nc.scalar.copy(xeT[:, 0, :], p_x[:, par, 0, :]).then_inc(xet_act, 1)

            def hidden(e, ahead=True):
                for j in range(0, FC, 2):
                    act.wait_ge(h_ps, FC * e + j + 1)
                    nc.scalar.activation(hT[:, j, :], p_h[:, 0, :], ACT.Relu).then_inc(h_act, 1)

            expert_order(act, tokens, lambda e, par, half: None, hidden)

        @block.vector
        def _(dve):
            ch = Chain(dve, dch)
            V = nc.vector
            flat = lambda a: a.rearrange("p a n -> p (a n)")
            one = lambda a: a.unsqueeze(2)
            best, rden, idx, place, valid, at, miss = (route[:, i, :] for i in range(7))
            by_tok = lambda a: a.unsqueeze(2).to_broadcast([P, CT, EXPERTS])
            by_exp = enum.unsqueeze(1).to_broadcast([P, CT, EXPERTS])
            by_chunk = lambda a: a.rearrange("p (t e) -> p t e", e=EXPERTS)

            def stats(c, par, half):
                dve.wait_ge(loaded[par], 16 * half + 16)
                for t in range(CT):
                    ch.mark(V.bn_stats(bn[:, t, :], flat(pay[:, bass.ds(c * CT + t, 1), 0:D])))
                ch.settle()
                ln_stats(nc, ch, bn, pay[:, chunk(c), MEAN], tmp[:, par, :, :], varok)

            def scales(c, par):
                dve.wait_ge(sdok, c + 1)
                ch.then(V.reciprocal(pay[:, chunk(c), RSTD], pay[:, chunk(c), RSTD]))
                V.scalar_tensor_tensor(shift[:, par, :], pay[:, chunk(c), MEAN], -1.0, pay[:, chunk(c), RSTD], ALU.mult, ALU.mult).then_inc(shift_ok, 1)

            def choose(c, par):
                dve.wait_ge(lg_ps, HT * c + HT)
                lg = by_chunk(p_h[:, par, 0:CT * EXPERTS])
                ch.then(V.tensor_reduce(one(best), lg, AX.X, ALU.max))
                V.tensor_tensor(ex[:, par, :, :], lg, by_tok(best), ALU.subtract).then_inc(ex_in, 1)
                ch.then(V.tensor_tensor(pick[:, :, :], lg, by_tok(best), ALU.is_ge))
                ch.then(V.scalar_tensor_tensor(pick[:, :, :], pick[:, :, :], -float(EXPERTS), by_exp, ALU.mult, ALU.add))
                ch.then(V.tensor_reduce(one(idx), pick[:, :, :], AX.X, ALU.min))
                ch.then(V.tensor_scalar(idx, idx, float(EXPERTS), None, ALU.add))
                ch.then(V.tensor_tensor(hot[:, :, :], by_exp, by_tok(idx), ALU.is_equal))
                V.tensor_copy(hot_b[:, :, :], hot[:, :, :]).then_inc(hot_ok, 1)

            def settle_places(c, par):
                dve.wait_ge(ex_out, c + 1)
                ch.then(V.tensor_reduce(one(rden), ex[:, par, :, :], AX.X, ALU.add))
                ch.mark(V.reciprocal(rden, rden))
                ch.then(V.tensor_reduce(seen[:, 1, :].unsqueeze(2), hot[:, :, :].rearrange("p t e -> p e t"), AX.X, ALU.add))
                ch.then(V.tensor_tensor(seen[:, 0, :], seen[:, 0, :], seen[:, 1, :], ALU.add))
                dve.wait_ge(cum_ps, c + 1)
                V.tensor_copy(seen_b[:, :], seen[:, 0, :]).then_inc(seen_ok, 1)
                ch.then(V.tensor_tensor(loc[:, :, :], by_chunk(p_y[:, par, 0:CT * EXPERTS]), hot[:, :, :], ALU.mult))
                ch.then(V.tensor_reduce(one(place), loc[:, :, :], AX.X, ALU.add))
                num = toks[:, bass.ds(c * CT, CT)]
                ch.mark(V.tensor_scalar(valid, place, float(CAP), None, ALU.is_lt))
                ch.then(V.scalar_tensor_tensor(at, idx, float(CAP), place, ALU.mult, ALU.add))
                ch.mark(V.tensor_tensor(pay[:, chunk(c), GATE], rden, valid, ALU.mult))
                ch.mark(V.tensor_copy(pay[:, chunk(c), NUM], num))
                ch.then(V.scalar_tensor_tensor(miss, at, -float(N_TOK), num, ALU.add, ALU.subtract))
                ch.then(V.tensor_tensor(at, miss, valid, ALU.mult))
                V.scalar_tensor_tensor(slot[:, chunk(c)], at, float(N_TOK), num, ALU.add, ALU.add).then_inc(routed, 1)
                dve.wait_ge(routed, c + 2)

            def step(c, par, half):
                choose(c, par)
                stats(c + 2, par, half)
                scales(c + 2, par)
                settle_places(c, par)

            dve.sem_inc(routed, 1)
            dve.sem_inc(y_ok, YB)
            dve.sem_inc(ye_free, 2)
            ch.then(V.memset(seen[:, 0, :], 0.0))
            V.memset(seen_b[:, :], 0.0).then_inc(seen_ok, 1)
            for par in range(2):
                stats(par, par, 0)
                scales(par, par)
            dve.wait_ge(tab_in, 32)
            for par in range(2):
                step(par, par, 1)
            with dve.Fori(1, PAIRS - 1) as i:
                ch.enter(i - 1, 2 * (CT + 25))
                for par in range(2):
                    step(2 * i + par, par, i + 1)
            ch.leave(PAIRS - 2)
            for par in range(2):
                choose(RC - 2 + par, par)
                settle_places(RC - 2 + par, par)
            dve.wait_ge(cum_ps, RC + 1)
            ch.then(V.tensor_tensor(seen[:, 0, :], p_y[:, 0, 0:EXPERTS], first_row, ALU.add))
            ch.mark(V.tensor_tensor(taken[:, :, :], places, seen[:, 0, :].unsqueeze(2).to_broadcast([P, EXPERTS, ET]), ALU.is_lt))
            ch.then(V.tensor_scalar(spare[:, 0, :, :], places, float(N_TOK), None, ALU.add))
            ch.then(V.tensor_tensor(spare[:, 1, :, :], spare[:, 0, :, :], taken[:, :, :], ALU.mult))
            ch.then(V.tensor_tensor(spare[:, 0, :, :], spare[:, 0, :, :], spare[:, 1, :, :], ALU.subtract))

            def enter_expert(e, par, half):
                dve.wait_ge(xe_in[par], 16 * half + 16)
                wait(dve, xet_ps, e)
                for c in range(ET):
                    V.tensor_scalar(xq[:, c, :], xe[:, par, c, 0:D], xe[:, par, c, MEAN:MEAN + 1], xe[:, par, c, RSTD:RSTD + 1],
                                    ALU.subtract, ALU.mult).then_inc(xq_ok, 1)

            def tokens(e, par):
                dve.wait_ge(xet_ps, e + 1)
                V.tensor_copy(xeT[:, 1, :], p_x[:, par, 1, :]).then_inc(xet_dve, 1)

            def hidden(e, par, half, ahead=True):
                for j in range(1, FC, 2):
                    dve.wait_ge(h_ps, FC * e + j + 1)
                    V.tensor_scalar(hT[:, j, :], p_h[:, 1, :], 0.0, None, ALU.max).then_inc(h_dve, 1)
                    if j == FC // 2 - 1 and ahead:
                        enter_expert(e + 1, 1 - par, half if par == 0 else half + 1)

            def answers_(e, par, half):
                dve.wait_ge(ye_free, e + 1)
                ch.then(V.tensor_tensor(place_t[:, :], xe[:, par, :, NUM], flat(taken[:, bass.ds(e, 1), :]), ALU.mult))
                ch.then(V.tensor_tensor(dest[:, par, :], place_t[:, :], flat(spare[:, 0, bass.ds(e, 1), :]), ALU.add))
                for c in range(ET):
                    dve.wait_ge(y_ps, ET * e + c + 1)
                    V.scalar_tensor_tensor(ye[:, par, c, :], p_y[:, c % 2, 0:D], xe[:, par, c, GATE:GATE + 1], xe[:, par, c, 0:D], ALU.mult, ALU.add).then_inc(y_ok, 1)

            enter_expert(0, 0, 0)
            tokens(0, 0)
            hidden(0, 0, 0)
            with dve.Fori(0, EXPERTS // 2 - 1) as i:
                ch.enter(i, 4)
                tokens(2 * i + 1, 1)
                answers_(2 * i, 0, i)
                hidden(2 * i + 1, 1, i)
                tokens(2 * i + 2, 0)
                answers_(2 * i + 1, 1, i)
                hidden(2 * i + 2, 0, i + 1)
            ch.leave(EXPERTS // 2 - 1)
            e = EXPERTS - 1
            tokens(e, 1)
            answers_(e - 1, 0, e // 2)
            hidden(e, 1, e // 2, ahead=False)
            answers_(e, 1, e // 2)

        @block.tensor
        def _(pe):
            mm = nc.tensor.matmul
            pe.wait_ge(const, 3)

            def turned(c, par):
                for h in range(HT):
                    pe.wait_ge(normed, CT * c + (h + 1) * CT // HT)
                    wait(pe, xt_ok, HT * (c - 1) + h + 1)
                    for d in range(DC):
                        for i in range(4):
                            last = nc.tensor.transpose(p_x[:, h, d, i * P:(i + 1) * P], xs[:, par, 4 * h + i, d * P:(d + 1) * P], ident[:, :])
                    last.then_inc(xt_ps, 1)

            def logits(c, par):
                if not isinstance(c, int) or c > 1:
                    pe.wait_ge(hot_ok, c - 1)
                for h in range(HT):
                    pe.wait_ge(xt_ok, HT * c + h + 1)
                    for i in range(4):
                        t = 4 * h + i
                        for d in range(DC):
                            last = mm(p_h[:, par, t * EXPERTS:(t + 1) * EXPERTS], xT[:, h, d, i * P:(i + 1) * P], wg_s[:, d, :], start=d == 0, stop=d == DC - 1)
                    last.then_inc(lg_ps, 1)

            def count(c, par):
                pe.wait_ge(hot_ok, c + 1)
                pe.wait_ge(seen_ok, c + 1)
                pe.wait_ge(routed, c)
                to = lambda lo: p_y[:, par, lo * EXPERTS:CT * EXPERTS]
                few = lambda n: hot_b[:, 0:n, :].rearrange("p t e -> p (t e)")
                mm(to(0), before[:, :], few(CT), start=True, stop=False, skip_group_check=True)
                for s in range(1, CT):
                    mm(to(s), ones[:, :], few(CT - s), start=False, stop=False, skip_group_check=True)
                mm(to(0), ones[:, :], seen_b[:, :].unsqueeze(1).to_broadcast([P, CT, EXPERTS]), start=False, stop=True, skip_group_check=True).then_inc(cum_ps, 1)

            def enter(c, par):
                turned(c, par)
                logits(c, par)

            pe.wait_ge(tab_in, 32)
            for par in range(2):
                enter(par, par)
            for par in range(2):
                count(par, par)
                enter(par + 2, par)
            with pe.Fori(1, PAIRS - 1) as i:
                for par in range(2):
                    count(2 * i + par, par)
                    enter(2 * i + par + 2, par)
            for par in range(2):
                count(RC - 2 + par, par)
            pe.wait_ge(seen_ok, RC + 1)
            pe.wait_ge(routed, RC + 1)
            mm(p_y[:, 0, 0:EXPERTS], ones[:, :], seen_b[:, :], start=True, stop=True).then_inc(cum_ps, 1)

            def tokens(e, par):
                pe.wait_ge(xq_ok, ET * e + ET)
                for c in range(DC):
                    for i in range(ET):
                        last = nc.tensor.transpose(p_x[:, par, c, i * P:(i + 1) * P], xq[:, i, c * P:(c + 1) * P], ident[:, :])
                last.then_inc(xet_ps, 1)

            def hidden(e, par, half):
                pe.wait_ge(w_in[par], 32 * half + 32)
                pe.wait_ge(xet_act, e + 1)
                pe.wait_ge(xet_dve, e + 1)
                for j in range(FC):
                    wait(pe, (h_act, h_dve)[j % 2], FC // 2 * e + j // 2)
                    for c in range(DC):
                        last = mm(p_h[:, j % 2, :], w1_s[:, par, c, j * P:(j + 1) * P], xeT[:, c, :], start=c == 0, stop=c == DC - 1)
                    last.then_inc(h_ps, 1)

            def answers_(e, par):
                pe.wait_ge(h_act, FC // 2 * e + FC // 2)
                pe.wait_ge(h_dve, FC // 2 * e + FC // 2)
                for c in range(ET):
                    pe.wait_ge(y_ok, ET * e + c - 1 + YB)
                    for j in range(FC):
                        last = mm(p_y[:, c % 2, 0:D], hT[:, j, c * P:(c + 1) * P], w2_s[:, par, j, :], start=j == 0, stop=j == FC - 1)
                    last.then_inc(y_ps, 1)

            tokens(0, 0)
            hidden(0, 0, 0)
            with pe.Fori(0, EXPERTS // 2 - 1) as i:
                tokens(2 * i + 1, 1)
                answers_(2 * i, 0)
                hidden(2 * i + 1, 1, i)
                tokens(2 * i + 2, 0)
                answers_(2 * i + 1, 1)
                hidden(2 * i + 2, 0, i + 1)
            e = EXPERTS - 1
            tokens(e, 1)
            answers_(e - 1, 0)
            hidden(e, 1, e // 2)
            answers_(e, 1)


def expert_order(eng, tokens, answers_, hidden):
    tokens(0, 0)
    hidden(0)
    with eng.Fori(0, EXPERTS // 2 - 1) as i:
        tokens(2 * i + 1, 1)
        answers_(2 * i, 0, i)
        hidden(2 * i + 1)
        tokens(2 * i + 2, 0)
        answers_(2 * i + 1, 1, i)
        hidden(2 * i + 2)
    e = EXPERTS - 1
    tokens(e, 1)
    answers_(e - 1, 0, e // 2)
    hidden(e)
    answers_(e, 1, e // 2)


def token_table(np):
    p = np.arange(P)[:, None]
    same = lambda a: np.tile(a, (P, 1))
    tokens = np.arange(TILES)[None, :] * P + p
    places = (np.arange(EXPERTS)[None, :, None] * CAP + p[:, :, None] * ET + np.arange(ET)[None, None, :]).reshape(P, -1)
    return np.concatenate([tokens, places, same(np.arange(EXPERTS)), same(np.arange(EXPERTS) * CAP)], 1).astype(np.float32)


BT = SEQ // P
POL = 3
SPLIT_Q = (0, 0, 0, 1, 1, 2)
SPLIT_K = (0, 1, 2, 0, 1, 0)
KR = len(SPLIT_Q) * HD
KM = KR + 3
VW = HD + 1
MASKED = -1e30
SPAN = (0, 512, 1024, 896)
GH = 4
HG = HEADS // GH
XC = 4
GW = P // GH
WIDTH = 1280


def stage_b(nc, x, wq, bq, wk, bk, wv, bv, wo, bo, pw1, pb1, pw2, pb2, sw1, sb1, sw2, sb2, parts, out):
    x_v = x.rearrange("(t p) n -> p t n", p=P)
    o_v = out.rearrange("(t p) n -> p t n", p=P)
    w_view = parts.rearrange("s i j p n -> s p (i j) n")
    r_view = parts.rearrange("s i (w c) (h d) n -> s i w d (c h) n", c=DC, d=HD)
    with Stage(nc, "b") as st:
        sb, ps, sem = st.sb, st.ps, st.sem
        qs = sb("qs", [P, 2, HEADS, SEQ], BF16)
        ks = sb("ks", [P, 2, HEADS, SEQ], BF16)
        ident = sb("ident", [P, P])
        ident_b = sb("ident_b", [P, P], BF16)
        ones_b = sb("ones_b", [P, P], BF16)
        ones = sb("ones", [P, P])
        after = sb("after", [P, P])
        mask_s = sb("mask_s", [P, P], BF16)
        mask_t = sb("mask_t", [P, P], BF16)
        wT = sb("wT", [P, DC, 4 * D])
        bias3 = sb("bias3", [P, D], BF16)
        bvb = sb("bvb", [P, D])
        bcol = sb("bcol", [P, 4])
        xb = sb("xb", [P, BT, D])
        xr = sb("xr", [P, BT, D])
        stg = sb("stg", [P, BT, D])
        xT = sb("xT", [P, DC, SEQ])
        qf = sb("qf", [P, 4, SEQ])
        qp = sb("qp", [P, 3, 4, SEQ], BF16)
        vw = sb("vw", [P, BT, D])
        va = sb("va", [P, 2, BT, HEADS, VW])
        vs = sb("vs", [P, 2, HEADS, VW])
        suf = sb("suf", [P, BT, HEADS, VW])
        vg = sb("vg", [P, BT, GH, GW])
        oT = sb("oT", [P, HG, SEQ])
        ob = sb("ob", [P, BT, HEADS, VW])
        cx = sb("cx", [P, BT, D])
        pt = sb("pt", [P, GH, WIDTH])
        mneg = sb("mneg", [P, 2, HEADS, BT])
        mrest = sb("mrest", [P, 2, HEADS * BT])
        mpart = sb("mpart", [P, 4, HEADS * BT], BF16)
        mT = sb("mT", [P, 2, P], BF16)
        wm = sb("wm", [P, HEADS, BT])
        rd = sb("rd", [P, BT, HEADS])
        gq = sb("gq", [P, DC, BATCH])
        ng = sb("ng", [P, BATCH, HEADS])
        first_pass = pt[:, :, :].rearrange("p g n -> p (g n)")
        bn = first_pass[:, 0:6 * CH].rearrange("p (t n) -> p t n", n=6)
        brow = first_pass[0:1, 512:512 + 2 * D].rearrange("p (a n) -> p a n", a=2)
        bpart = first_pass[0:1, 1024:1024 + 3 * D // 2].bitcast(BF16).rearrange("p (i n) -> p i n", i=3)
        xc = ks[:, :, :, :].rearrange("p s h n -> p (s h n)").bitcast(F32).rearrange("p (s t n) -> p s t n", s=XC, t=CH)
        mean = sb("mean", [P, TILES])
        rstd = sb("rstd", [P, TILES])
        tmp = qf[:, 0, 0:2 * TILES].rearrange("p (a n) -> p a n", a=2)
        f32 = lambda a: a.rearrange("p h n -> p (h n)").bitcast(F32)
        wn = f32(qs[:, 0, :, :])[:, 0:8 * D].rearrange("p (w o n) -> p w o n", w=4, o=DC)
        hn = f32(qs[:, 0, :, :])[:, 8 * D:12 * D].rearrange("p (w n) -> p w n", w=4)
        hT_ = f32(qs[:, 1, :, :])[:, 0:8 * P].rearrange("p (w c n) -> p w c n", w=4, c=DC)
        pool_ = f32(qs[:, 1, :, :])[:, 8 * P:]
        take = lambda lo, n, parts_=P: pool_[0:parts_, lo:lo + n]
        sel = take(0, 31)
        hb = take(32, 4)
        w2n = take(64, P, POL * HEADS)
        s2n = take(192, P, POL)
        w2T = take(320, POL * HEADS + POL)
        xm = take(384, D, BATCH)
        xmT = take(640, DC * BATCH).rearrange("p (c b) -> p c b", c=DC)
        hid = take(680, 4 * BATCH).rearrange("p (w b) -> p w b", w=4)
        b2 = take(760, POL * HEADS + POL, BATCH)
        gl = take(820, POL * HEADS, BATCH).rearrange("p (a h) -> p a h", a=POL)
        pl = take(880, POL, BATCH)
        gs = take(890, 8, BATCH)
        gate = take(900, HEADS, BATCH)
        gch = take(920, D, BATCH)
        gdiag = take(1180, BATCH * HEADS, BATCH).rearrange("p (b h) -> p b h", b=BATCH)

        p_s = ps("p_s", [P, 3, 512])
        p_t = ps("p_t", [P, 3, 512])
        p_p = ps("p_p", [P, 2, 512])

        loaded = [sem(f"loaded{c}") for c in range(XC)]
        names = ("const w_in b_in g_in varok sdok normed wt_ps wt_ok bsplit bias_in mean_ok mlp_ps mlp_ok "
                 "gate_ps gate_ok gelu e_in e_out free_ok staged xt_ps xt_ok qk_ps qk_ev qk_hi q_parts v_ps v_ev va_ok "
                 "suf_ps suf_ev ct_ps ct_ok ctx_ok o_ps o_ev s_ps smax t_ps exp_ev pv_ps m_ok mt_ps mt_ok "
                 "m_in parts_out xr_in x_out w_ready w_exp ones_in mean_used xb_in back_ps back_ev sw_ok vg_ok ot_ok heads_on out_seen vs_ok dch pch").split()
        (const, w_in, b_in, g_in, varok, sdok, normed, wt_ps, wt_ok, bsplit, bias_in, mean_ok, mlp_ps, mlp_ok,
         gate_ps, gate_ok, gelu, e_in, e_out, free_ok, staged, xt_ps, xt_ok, qk_ps, qk_ev, qk_hi, q_parts, v_ps, v_ev, va_ok,
         suf_ps, suf_ev, ct_ps, ct_ok, ctx_ok, o_ps, o_ev, s_ps, smax, t_ps, exp_ev, pv_ps, m_ok, mt_ps, mt_ok,
         m_in, parts_out, xr_in, x_out, w_ready, w_exp, ones_in, mean_used, xb_in, back_ps, back_ev, sw_ok, vg_ok, ot_ok, heads_on, out_seen, vs_ok, dch, pch) = [sem(n) for n in names]
        stacked = [[sem(f"stacked{par}_{g}") for g in range(2)] for par in range(2)]
        block = st.ctx.enter_context(nc.Block())
        flat = lambda a: a.rearrange("p a n -> p (a n)")
        H3 = 3 * HEADS
        H2 = 2 * HEADS
        SH = HEADS // 2
        BACK = (p_s[:, 0, :], p_s[:, 1, :], p_s[:, 2, :], p_t[:, 2, :])
        QK = (p_t[:, 0, :], p_t[:, 1, :], p_s[:, 0, :], p_s[:, 1, :])
        SUF = (p_s[:, 2, :], p_t[:, 2, :], p_t[:, 0, :], p_t[:, 1, :])

        def steps(eng, step, ch=None, marks=0):
            step(0, 0, proj=True, s=False, t=False, fin=False)
            step(1, 1, proj=True, s=True, t=False, fin=False)
            step(2, 0, proj=True, s=True, t=True, fin=False)
            with eng.Fori(0, (BATCH - 4) // 2) as i:
                if ch:
                    ch.enter(i, 2 * marks)
                step(2 * i + 3, 1, half=i + 1)
                step(2 * i + 4, 0, half=i + 2)
            if ch:
                ch.leave((BATCH - 4) // 2)
            step(BATCH - 1, 1)
            step(BATCH, 0, proj=False)
            step(BATCH + 1, 1, proj=False, s=False)
            step(BATCH + 2, 0, proj=False, s=False, t=False)

        @block.sync
        def _(sp):
            for c in range(CHUNKS):
                if c >= XC:
                    sp.wait_ge(mean_used, c - XC + 1)
                sp.dma_start(xc[:, c % XC, :, :], x_v[:, c * CH:(c + 1) * CH, :]).then_inc(loaded[c % XC], 16)
            sp.dma_start(xb[:, :, :], x_v[:, 0:BT, :]).then_inc(xb_in, 16)
            sp.wait_ge(bsplit, 1)
            sp.wait_ge(const, 6)
            for i in range(3):
                sp.dma_start(bias3[i:i + 1, :], bpart[0:1, i, :]).then_inc(bias_in, 16)

            def step(k, par, proj=True, s=True, t=True, fin=True, half=None):
                if proj and not (isinstance(k, int) and k == BATCH - 1):
                    sp.wait_ge(staged, BT * (k + 1))
                    sp.dma_start(xb[:, :, :], x_v[:, bass.ds(BT * (k + 1), BT), :]).then_inc(xb_in, 16)
                if t:
                    sp.wait_ge(mt_ok, k - 1)
                    for i in range(3):
                        sp.dma_start(qs[KR + i:KR + i + 1, par, :, :].rearrange("a h (i n) -> a (h i) n", n=P),
                                     mT[i % 2 * 64:i % 2 * 64 + 64, i // 2, :]).then_inc(m_in, 16)
                if fin:
                    sp.dma_start(xr[:, :, :], x_v[:, bass.ds(BT * (k - 3), BT), :]).then_inc(xr_in, 16)
                if proj:
                    sp.wait_ge(q_parts, k + 1)
                    sp.dma_start(w_view[par], qp[:, :, :, :].rearrange("p i j n -> p (i j) n")).then_inc(parts_out, 16)
                if fin:
                    sp.wait_ge(o_ev, BT * (k - 2))
                    sp.dma_start(o_v[:, bass.ds(BT * (k - 3), BT), :], xr[:, :, :]).then_inc(x_out, 16)
                if proj:
                    sp.wait_ge(parts_out, 16 * k + 16)
                    for g in range(2):
                        if t:
                            sp.wait_ge(t_ps, H2 * (k - 2) + 2 * SH * (g + 1))
                        for q, to, order in ((0, qs, SPLIT_Q), (1, ks, SPLIT_K)):
                            for r, part in enumerate(order):
                                sp.dma_start(to[r * HD:(r + 1) * HD, par, g * SH:(g + 1) * SH, :],
                                             r_view[par, part, q, :, g * SH:(g + 1) * SH, :]).then_inc(stacked[par][g], 16)
                if fin:
                    sp.wait_ge(x_out, 16 * (k - 2))
                    sp.sem_inc(out_seen, 1)

            sp.wait_ge(free_ok, 1)
            for par in range(2):
                sp.dma_start(ks[KR:KM, par, :, :].rearrange("p h (i n) -> p (h i) n", n=P), ones_b[0:3, :].unsqueeze(1).to_broadcast([3, HEADS * BT, P])).then_inc(ones_in, 16)
            steps(sp, step)
            sp.wait_ge(x_out, 16 * BATCH)

        @block.gpsimd
        def _(pool):
            ch = Chain(pool, pch)
            for a, v in ((ident, 0.0), (ident_b, 0.0), (ones_b, 1.0), (ones, 1.0), (after, 1.0), (mask_s, 0.0), (mask_t, 0.0), (bias3, 0.0)):
                ch.mark(pool.memset(a[:, :], v))
            ch.mark(pool.memset(va[:, :, :, :, :], 1.0))
            ch.mark(pool.memset(vg[:, :, :, :], 0.0))
            ch.mark(pool.memset(sel, 0.0))
            ch.mark(pool.memset(mpart[:, 3, :], 0.0))
            ch.settle()
            aff = lambda a, op, fill, base, step, mult: pool.affine_select(out=a, in_=a, compare_op=op, fill=fill, base=base, pattern=[[step, a.shape[1]]], channel_multiplier=mult)
            aff(ident[:, :], ALU.not_equal, 1.0, 0, -1, 1).then_inc(const, 1)
            aff(ident_b[:, :], ALU.not_equal, 1.0, 0, -1, 1).then_inc(const, 1)
            aff(after[:, :], ALU.is_gt, 0.0, 0, -1, 1).then_inc(const, 1)
            aff(mask_s[:, :], ALU.is_ge, MASKED, 0, -1, 1).then_inc(const, 1)
            aff(mask_t[:, :], ALU.is_ge, MASKED, 0, 1, -1).then_inc(const, 1)
            pool.memset(sel[:, 15:16], 1.0 / SEQ).then_inc(const, 1)
            pool.wait_ge(free_ok, 1)
            pool.wait_ge(g_in, 112)

            def step(k, par, proj=True, s=True, t=True, fin=True, half=None):
                if s:
                    pool.wait_ge(v_ev, BT * k)
                    if t:
                        wait(pool, vg_ok, HG * (k - 2))
                        wait(pool, suf_ps, BT * (k - 2))
                    pool.tensor_tensor(va[:, 1 - par, :, :, 0:HD], vw[:, :, :].rearrange("p t (h c) -> p t h c", c=HD),
                                       bvb[:, :].rearrange("p (h c) -> p h c", c=HD).unsqueeze(1).to_broadcast([P, BT, HEADS, HD]), ALU.add).then_inc(va_ok, 1)
                if proj:
                    pool.wait_ge(qk_hi, k + 1)
                    ch.then(pool.tensor_tensor(flat(qp[:, 1, :, :]), flat(qf[:, :, :]), flat(qp[:, 0, :, :]), ALU.subtract))
                    ch.then(pool.tensor_tensor(flat(qf[:, :, :]), flat(qf[:, :, :]), flat(qp[:, 0, :, :]), ALU.subtract))
                    pool.tensor_tensor(flat(qp[:, 2, :, :]), flat(qf[:, :, :]), flat(qp[:, 1, :, :]), ALU.subtract).then_inc(q_parts, 1)
                if t:
                    with pool.Fori(0, HG) as j:
                        pool.wait_ge(va_ok, k - 1)
                        pool.wait_ge(pv_ps, HG * (k - 2) + j + 1)
                        pool.tensor_copy(vg[:, :, :, 0:VW], va[:, par, :, bass.ds(GH * j, GH), :]).then_inc(vg_ok, 1)
                    pool.wait_ge(suf_ev, BT * (k - 1))
                    pool.wait_ge(w_exp, k - 1)
                    pool.tensor_tensor(suf[:, :, :, :], suf[:, :, :, :], wm[:, :, :].rearrange("p h i -> p i h").unsqueeze(3).to_broadcast([P, BT, HEADS, VW]), ALU.mult).then_inc(sw_ok, 1)
                if s:
                    pool.wait_ge(va_ok, k)
                    if t:
                        pool.wait_ge(suf_ps, BT * (k - 1))
                    ch.then(pool.tensor_tensor(vs[:, 1, :, :], va[:, 1 - par, 2, :, :], va[:, 1 - par, 3, :, :], ALU.add))
                    pool.tensor_tensor(vs[:, 0, :, :], va[:, 1 - par, 1, :, :], vs[:, 1, :, :], ALU.add).then_inc(vs_ok, 1)

            steps(pool, step, ch, 3)

        @block.scalar
        def _(act):
            for i, w in enumerate((wq, wk, wv, wo)):
                act.dma_start(wn[:, i, :, :], w.rearrange("(c p) n -> p c n", p=P)).then_inc(w_in, 16)
            act.dma_start(hn[:, 0, :], sw1).then_inc(w_in, 16)
            act.dma_start(hn[:, 1:4, :], pw1.rearrange("a p n -> p a n")).then_inc(w_in, 16)
            act.dma_start(w2n, pw2.rearrange("a h p -> (a h) p")).then_inc(w_in, 16)
            act.dma_start(s2n, sw2).then_inc(w_in, 16)
            act.dma_start(brow[0:1, 0, :], bo.rearrange("(a n) -> a n", a=1)).then_inc(b_in, 16)
            act.dma_start(bvb[:, :], bv.rearrange("(a n) -> a n", a=1).to_broadcast([P, D])).then_inc(g_in, 16)
            with nc.allow_non_contiguous_dma(reason="a few hundred biases to their partitions"):
                for i, b in enumerate((bq, bk)):
                    act.dma_start(bcol[:, 2 * i:2 * i + 2], b.rearrange("(c p) -> p c", p=P)).then_inc(g_in, 16)
                act.dma_start(hb[:, 0:1], sb1.rearrange("(p a) -> p a", a=1)).then_inc(g_in, 16)
                act.dma_start(hb[:, 1:4], pb1.rearrange("a p -> p a")).then_inc(g_in, 16)
            act.dma_start(b2[:, 0:POL * HEADS], pb2.rearrange("(u a) h -> u (a h)", u=1).to_broadcast([BATCH, POL * HEADS])).then_inc(g_in, 16)
            act.dma_start(b2[:, POL * HEADS:], sb2.rearrange("(u a) -> u a", u=1).to_broadcast([BATCH, POL])).then_inc(g_in, 16)
            for c in range(CHUNKS):
                act.wait_ge(varok, c + 1)
                nc.scalar.activation(rstd[:, c * CH:(c + 1) * CH], tmp[:, 0, c * CH:(c + 1) * CH], ACT.Sqrt).then_inc(sdok, 1)
            for i in range(4):
                act.wait_ge(wt_ps, i + 1)
                nc.scalar.copy(wT[:, :, i * D:(i + 1) * D], (p_s[:, i, :] if i < 3 else p_t[:, 0, :]).rearrange("p (c n) -> p c n", c=DC)).then_inc(wt_ok, 1)
            for i in range(2):
                act.wait_ge(wt_ps, 5 + i)
                nc.scalar.copy(hT_[:, 2 * i:2 * i + 2, :, :], p_t[:, 1 + i, :].rearrange("p (w c n) -> p w c n", w=2, c=DC)).then_inc(wt_ok, 1)
            act.wait_ge(wt_ps, 7)
            nc.scalar.copy(w2T, p_p[:, 0, 0:POL * HEADS + POL]).then_inc(wt_ok, 1)
            act.wait_ge(mlp_ps, 2)
            act.wait_ge(g_in, 112)
            for i in range(4):
                nc.scalar.activation(hid[:, i, :], p_t[:, 0, i * BATCH:(i + 1) * BATCH], ACT.Gelu, bias=hb[:, i:i + 1]).then_inc(gelu, 1)
            act.wait_ge(e_in, 1)
            nc.scalar.activation(gl, gl, ACT.Exp).then_inc(e_out, 1)
            nc.scalar.activation(pl, pl, ACT.Exp).then_inc(e_out, 1)
            act.wait_ge(free_ok, 1)
            act.sem_inc(exp_ev, 2)

            def step(k, par, proj=True, s=True, t=True, fin=True, half=None):
                if t:
                    act.wait_ge(mt_ps, k - 1)
                    wait(act, m_in, 48 * (k - 2))
                    nc.scalar.copy(mT[:, :, :], p_p[:, 1, 0:P].bitcast(BF16).rearrange("p (a n) -> p a n", a=2)).then_inc(mt_ok, 1)
                if proj:
                    act.wait_ge(xt_ps, k + 1)
                    nc.scalar.copy(xT[:, :, :], p_t[:, 0:2, :]).then_inc(xt_ok, 1)
                    act.wait_ge(qk_ev, 4 * k + 4)
                    wait(act, parts_out, 16 * k)
                    nc.scalar.copy(flat(qp[:, 0, :, :]), flat(qf[:, :, :])).then_inc(qk_hi, 1)
                    wait(act, va_ok, k)
                    for i in range(BT):
                        act.wait_ge(v_ps, BT * k + i + 1)
                        nc.scalar.copy(vw[:, i, :], p_p[:, i % 2, 0:D]).then_inc(v_ev, 1)
                if t:
                    wait(act, back_ev, BT * (k - 2))
                    for i in range(BT):
                        act.wait_ge(suf_ps, BT * (k - 2) + i + 1)
                        nc.scalar.copy(suf[:, i, :, :].rearrange("p h c -> p (h c)"), SUF[i][:, 0:HEADS * VW]).then_inc(suf_ev, 1)
                    act.wait_ge(w_ready, k - 1)
                    nc.scalar.activation(wm[:, :, :], wm[:, :, :], ACT.Exp).then_inc(w_exp, 1)
                if fin:
                    act.wait_ge(ct_ps, k - 2)
                    nc.scalar.copy(xT[:, :, :], p_s[:, 0:2, :]).then_inc(ct_ok, 1)
                if t:
                    with act.Fori(0, HG) as j:
                        group = HG * (k - 2) + j
                        for g in range(GH):
                            if g == 0:
                                act.wait_ge(pv_ps, group + 1)
                            for m, (lo, hi) in enumerate(((0, 512), (512, WIDTH))):
                                act.wait_ge(t_ps, 2 * (GH * group + g) + m + 1)
                                nc.scalar.activation(pt[:, g, lo:hi], p_t[:, :, :].rearrange("p a n -> p (a n)")[:, lo:hi], ACT.Exp).then_inc(exp_ev, 1)

            steps(act, step)

        @block.vector
        def _(dve):
            ch = Chain(dve, dch)
            V = nc.vector
            def stats(c):
                dve.wait_ge(loaded[c % XC], 16 * (c // XC) + 16)
                for t in range(CH):
                    ch.mark(V.bn_stats(bn[:, t, :], xc[:, c % XC, t, :]))
                ch.settle()
                of = slice(c * CH, (c + 1) * CH)
                ln_stats(nc, ch, bn, mean[:, of], tmp[:, :, of], varok)
                dve.wait_ge(varok, c + 1)

            stats(0)
            for c in range(CHUNKS):
                if c + 1 < CHUNKS:
                    stats(c + 1)
                dve.wait_ge(sdok, c + 1)
                of = rstd[:, c * CH:(c + 1) * CH]
                ch.then(V.reciprocal(of, of))
                for t in range(CH):
                    at = c * CH + t
                    V.tensor_scalar(xc[:, c % XC, t, :], xc[:, c % XC, t, :], mean[:, at:at + 1], rstd[:, at:at + 1], ALU.subtract, ALU.mult).then_inc(normed, 1)
            dve.wait_ge(b_in, 16)
            split3(nc, ch, brow, bpart, bsplit)
            dve.wait_ge(mean_used, CHUNKS)
            V.tensor_copy(xm, p_p[0:BATCH, 1, 0:D]).then_inc(mean_ok, 1)
            dve.wait_ge(mlp_ps, 1)
            V.tensor_copy(flat(xmT), p_p[:, 1, 0:DC * BATCH]).then_inc(mlp_ok, 1)
            dve.wait_ge(gate_ps, 1)
            dve.wait_ge(g_in, 112)
            ch.mark(V.tensor_tensor(flat(gl), p_p[0:BATCH, 0, 0:POL * HEADS], b2[:, 0:POL * HEADS], ALU.add))
            ch.then(V.tensor_tensor(pl, p_p[0:BATCH, 0, POL * HEADS:POL * HEADS + POL], b2[:, POL * HEADS:], ALU.add))
            ch.mark(V.tensor_reduce(gs[:, 0:POL].unsqueeze(2), gl, AX.X, ALU.max))
            ch.then(V.tensor_reduce(gs[:, POL:POL + 1], pl, AX.X, ALU.max))
            ch.mark(V.tensor_tensor(gl, gl, gs[:, 0:POL].unsqueeze(2).to_broadcast([BATCH, POL, HEADS]), ALU.subtract))
            V.tensor_scalar(pl, pl, gs[:, POL:POL + 1], None, ALU.subtract).then_inc(e_in, 1)
            dve.wait_ge(e_out, 2)
            ch.mark(V.tensor_reduce(gs[:, 0:POL].unsqueeze(2), gl, AX.X, ALU.add))
            ch.then(V.tensor_reduce(gs[:, POL:POL + 1], pl, AX.X, ALU.add))
            ch.then(V.reciprocal(gs[:, 0:POL + 1], gs[:, 0:POL + 1]))
            ch.then(V.tensor_scalar(pl, pl, gs[:, POL:POL + 1], None, ALU.mult))
            ch.then(V.tensor_tensor(gs[:, 0:POL], gs[:, 0:POL], pl, ALU.mult))
            ch.then(V.tensor_scalar(gate, gl[:, 0, :], gs[:, 0:1], None, ALU.mult))
            for i in range(1, POL):
                ch.then(V.scalar_tensor_tensor(gate, gl[:, i, :], gs[:, i:i + 1], gate, ALU.mult, ALU.add))
            ch.then(V.tensor_scalar(gch.rearrange("p (h c) -> p h c", c=HD), gate.unsqueeze(2).to_broadcast([BATCH, HEADS, HD]), 0.25, None, ALU.mult))
            ch.then(V.tensor_scalar(gate, gate, -1e9, None, ALU.mult))
            V.tensor_tensor(gdiag, ident[0:BATCH, 0:BATCH].unsqueeze(2).to_broadcast([BATCH, BATCH, HEADS]),
                            gate.unsqueeze(1).to_broadcast([BATCH, BATCH, HEADS]), ALU.mult).then_inc(gate_ok, 1)
            dve.wait_ge(gate_ps, 2)
            ch.mark(V.tensor_copy(flat(gq[:, :, :]), p_p[:, 1, 0:DC * BATCH]))
            ch.settle()
            V.tensor_copy(flat(ng[:, :, :]), p_t[:, 1, 0:BATCH * HEADS]).then_inc(free_ok, 1)
            dve.wait_ge(free_ok, 1)
            dve.sem_inc(smax, 3)

            def step(k, par, proj=True, s=True, t=True, fin=True, half=None):
                if fin:
                    dve.wait_ge(sw_ok, k - 2)
                    for i in range(BT):
                        dve.wait_ge(back_ps, BT * (k - 3) + i + 1)
                        V.tensor_tensor(ob[:, i, :, :], BACK[i].rearrange("p (h c) -> p h c", c=GW)[:, :, 0:VW], suf[:, i, :, :], ALU.add).then_inc(back_ev, 1)
                    dve.wait_ge(back_ev, BT * (k - 2))
                    ch.then(V.reciprocal(rd[:, :, :].unsqueeze(3), ob[:, :, :, HD:VW]))
                    V.tensor_tensor(cx[:, :, :].rearrange("p i (h c) -> p i h c", c=HD), ob[:, :, :, 0:HD],
                                    rd[:, :, :].unsqueeze(3).to_broadcast([P, BT, HEADS, HD]), ALU.mult).then_inc(ctx_ok, 1)
                if proj:
                    wait(dve, q_parts, k)
                    for j in range(4):
                        dve.wait_ge(qk_ps, 4 * k + j + 1)
                        src = QK[j]
                        if j < 2:
                            V.tensor_scalar(qf[:, j, :], src, bcol[:, j:j + 1], gq[:, j, bass.ds(k, 1)], ALU.add, ALU.mult).then_inc(qk_ev, 1)
                        else:
                            V.tensor_scalar(qf[:, j, :], src, bcol[:, j:j + 1], None, ALU.add).then_inc(qk_ev, 1)
                if t:
                    wait(dve, sw_ok, k - 2)
                    V.tensor_tensor(wm[:, :, :], mneg[:, par, :, :], ng[:, bass.ds(k - 2, 1), :].rearrange("p a h -> p h a").to_broadcast([P, HEADS, BT]), ALU.add).then_inc(w_ready, 1)
                if fin:
                    dve.wait_ge(xr_in, 16 * (k - 2))
                    for i in range(BT):
                        dve.wait_ge(o_ps, BT * (k - 3) + i + 1)
                        x_t = xr[:, i, :]
                        V.tensor_tensor(x_t, p_p[:, i % 2, 0:D], x_t, ALU.add).then_inc(o_ev, 1)
                if proj and not (isinstance(k, int) and k == BATCH - 1):
                    normalise(k + 1)
                def sums_out(j):
                    dve.wait_ge(pv_ps, HG * (k - 2) + j + 2)
                    V.tensor_copy(flat(oT[:, bass.ds(j, 1), :]), p_p[:, 0, :]).then_inc(ot_ok, 1)

                if s or t:
                    with dve.Fori(0, HG - 1) as j:
                        if s:
                            for g in range(GH):
                                maxima(k, par, GH * j + g)
                        if t:
                            sums_out(j)
                if s:
                    for g in range(GH):
                        maxima(k, par, GH * (HG - 1) + g)
                if s:
                    dve.wait_ge(smax, H3 * k + 3)
                    wait(dve, mt_ps, k - 1)
                    m = mneg[:, 1 - par, :, :].rearrange("p h i -> p (h i)")
                    ch.then(V.tensor_copy(mpart[:, 0, :], m))
                    ch.then(V.tensor_tensor(mrest[:, 0, :], m, mpart[:, 0, :], ALU.subtract))
                    ch.then(V.tensor_copy(mpart[:, 1, :], mrest[:, 0, :]))
                    ch.then(V.tensor_tensor(mrest[:, 1, :], mrest[:, 0, :], mpart[:, 1, :], ALU.subtract))
                    V.tensor_copy(mpart[:, 2, :], mrest[:, 1, :]).then_inc(m_ok, 1)
                if t:
                    sums_out(HG - 1)
            def normalise(k):
                dve.wait_ge(xb_in, 16 * k + 16)
                wait(dve, xt_ps, k)
                for i in range(BT):
                    V.tensor_scalar(stg[:, i, :], xb[:, i, :], mean[:, bass.ds(BT * k + i, 1)], rstd[:, bass.ds(BT * k + i, 1)], ALU.subtract, ALU.mult).then_inc(staged, 1)

            def maxima(k, par, h):
                first = 3 * (HEADS * (k - 1) + h)
                to = lambda i: mneg[:, 1 - par, bass.ds(h, 1), i]
                red = lambda i, src: V.tensor_reduce(to(i), src, AX.X, ALU.max, negate=True)
                dve.wait_ge(s_ps, first + 1)
                red(3, p_s[:, 0, :]).then_inc(smax, 1)
                dve.wait_ge(s_ps, first + 2)
                red(2, p_s[:, 1, 0:384])
                red(0, p_s[:, 1, 384:512]).then_inc(smax, 1)
                dve.wait_ge(s_ps, first + 3)
                red(1, p_s[:, 2, 0:256]).then_inc(smax, 1)

            normalise(0)
            steps(dve, step, ch, 5)

        @block.tensor
        def _(pe):
            mm = nc.tensor.matmul
            tr = nc.tensor.transpose
            pe.wait_ge(const, 6)
            pe.wait_ge(w_in, 128)
            for i in range(4):
                dst = p_s[:, i, :] if i < 3 else p_t[:, 0, :]
                for c in range(DC):
                    for o in range(DC):
                        last = tr(dst[:, c * D + o * P:c * D + (o + 1) * P], wn[:, i, o, c * P:(c + 1) * P], ident[:, :])
                last.then_inc(wt_ps, 1)
            for i in range(2):
                for w in range(2):
                    for c in range(DC):
                        last = tr(p_t[:, 1 + i, (2 * w + c) * P:(2 * w + c + 1) * P], hn[:, 2 * i + w, c * P:(c + 1) * P], ident[:, :])
                last.then_inc(wt_ps, 1)
            tr(p_p[:, 0, 0:POL * HEADS], w2n, ident[0:POL * HEADS, 0:POL * HEADS])
            tr(p_p[:, 0, POL * HEADS:POL * HEADS + POL], s2n, ident[0:POL, 0:POL]).then_inc(wt_ps, 1)
            for b in range(BATCH):
                pe.wait_ge(normed, BT * (b + 1))
                for i in range(BT):
                    last = mm(p_p[0:BATCH, 1, 0:D], sel[:, 15 - b:31 - b], xc[:, b // 2 % XC, BT * (b % 2) + i, :], start=b + i == 0, stop=b == BATCH - 1 and i == BT - 1)
                if b % 2:
                    last.then_inc(mean_used, 1)
            pe.wait_ge(mean_ok, 1)
            for c in range(DC):
                last = tr(p_p[:, 1, c * BATCH:(c + 1) * BATCH], xm[:, c * P:(c + 1) * P], ident[0:BATCH, 0:BATCH])
            last.then_inc(mlp_ps, 1)
            pe.wait_ge(mlp_ok, 1)
            pe.wait_ge(wt_ok, 7)
            for w in range(4):
                for c in range(DC):
                    last = mm(p_t[:, 0, w * BATCH:(w + 1) * BATCH], hT_[:, w, c, :], xmT[:, c, :], start=c == 0, stop=c == DC - 1)
            last.then_inc(mlp_ps, 1)
            pe.wait_ge(gelu, 4)
            for a in range(POL):
                mm(p_p[0:BATCH, 0, a * HEADS:(a + 1) * HEADS], hid[:, 1 + a, :], w2T[:, a * HEADS:(a + 1) * HEADS], start=True, stop=True)
            mm(p_p[0:BATCH, 0, POL * HEADS:POL * HEADS + POL], hid[:, 0, :], w2T[:, POL * HEADS:], start=True, stop=True).then_inc(gate_ps, 1)
            pe.wait_ge(gate_ok, 1)
            for c in range(DC):
                tr(p_p[:, 1, c * BATCH:(c + 1) * BATCH], gch[:, c * P:(c + 1) * P], ident[0:BATCH, 0:BATCH])
            mm(p_t[:, 1, 0:BATCH * HEADS], ones[0:BATCH, :], gdiag.rearrange("p b h -> p (b h)"), start=True, stop=True).then_inc(gate_ps, 1)
            pe.wait_ge(free_ok, 1)
            pe.wait_ge(bias_in, 48)
            pe.sem_inc(pv_ps, 1)
            pe.sem_inc(ot_ok, 1)

            def step(k, par, proj=True, s=True, t=True, fin=True, half=None):
                half = k // 2 if half is None else half
                if t:
                    pe.wait_ge(m_ok, k - 1)
                    pe.wait_ge(v_ev, BT * k if proj else BT * min(k, BATCH))
                    for i in range(2):
                        last = tr(p_p[:, 1, i * P // 2:(i + 1) * P // 2].bitcast(BF16), mpart[:, 2 * i:2 * i + 2, :].rearrange("p a n -> p (a n)"), ident_b[:, :])
                    last.then_inc(mt_ps, 1)
                if s or t:
                    pe.wait_ge(smax, H3 * (k - 1) + 3 if proj else H3 * (min(k, BATCH + 1) - 1) + 3)
                if t or fin:
                    pe.wait_ge(exp_ev, H2 * (k - 2) + 2 if proj else H2 * (min(k, BATCH + 2) - 2) + 2)
                if proj:
                    pe.wait_ge(staged, BT * k + BT)
                    for c in range(DC):
                        for i in range(BT):
                            last = tr(p_t[:, c, i * P:(i + 1) * P], stg[:, i, c * P:(c + 1) * P], ident[:, :])
                    last.then_inc(xt_ps, 1)
                if fin:
                    pe.wait_ge(ot_ok, HG * (k - 2) + 1)
                    for i in range(BT):
                        for j in range(HG):
                            last = tr(BACK[i][:, j * P:(j + 1) * P], oT[:, j, i * P:(i + 1) * P], ident[:, :])
                        last.then_inc(back_ps, 1)
                if proj:
                    pe.wait_ge(xt_ok, k + 1)
                    for j in range(4):
                        if fin and j >= 2:
                            pe.wait_ge(back_ev, BT * (k - 3) + j - 1)
                        for c in range(DC):
                            last = mm(QK[j], wT[:, c, j * P:(j + 1) * P], xT[:, c, :], start=c == 0, stop=c == DC - 1)
                        last.then_inc(qk_ps, 1)
                    if t:
                        pe.wait_ge(mt_ok, k - 1)
                    for i in range(BT):
                        if i >= 2:
                            pe.wait_ge(v_ev, BT * k + i - 1)
                        for c in range(DC):
                            last = mm(p_p[:, i % 2, 0:D], xT[:, c, i * P:(i + 1) * P], wT[:, c, 2 * D:3 * D], start=c == 0, stop=c == DC - 1)
                        last.then_inc(v_ps, 1)
                if t:
                    pe.wait_ge(vs_ok, k - 1)
                    for i in range(BT):
                        if fin and i < 2:
                            pe.wait_ge(back_ev, BT * (k - 3) + 3 + i)
                        if proj and i >= 2:
                            pe.wait_ge(qk_ev, 4 * k + i - 1)
                        val = lambda j: va[:, par, j, :, :].rearrange("p h c -> p (h c)")
                        dst = SUF[i][:, 0:HEADS * VW]
                        last = mm(dst, after[:, :], val(i), start=True, stop=i == BT - 1)
                        if i < BT - 1:
                            behind = vs[:, i, :, :].rearrange("p h c -> p (h c)") if i < 2 else val(BT - 1)
                            last = mm(dst, ones[:, :], behind, start=False, stop=True)
                        last.then_inc(suf_ps, 1)
                if fin:
                    pe.wait_ge(ctx_ok, k - 2)
                    if proj:
                        pe.wait_ge(qk_ev, 4 * k + 4)
                        pe.wait_ge(v_ev, BT * k + BT)
                    elif t:
                        pe.wait_ge(mt_ok, k - 1)
                    pe.wait_ge(back_ev, BT * (k - 2))
                    for c in range(DC):
                        for i in range(BT):
                            last = tr(p_s[:, c, i * P:(i + 1) * P], cx[:, i, c * P:(c + 1) * P], ident[:, :])
                    last.then_inc(ct_ps, 1)
                    pe.wait_ge(ct_ok, k - 2)
                    for i in range(BT):
                        if i >= 2:
                            pe.wait_ge(o_ev, BT * (k - 3) + i - 1)
                        for c in range(DC):
                            mm(p_p[:, i % 2, 0:D], xT[:, c, i * P:(i + 1) * P], wT[:, c, 3 * D:], start=c == 0, stop=False)
                        mm(p_p[:, i % 2, 0:D], ones_b[:, :], bias3[:, :], start=False, stop=True).then_inc(o_ps, 1)
                if s:
                    half_s = half - 1 if par == 0 else half
                    for g in range(2):
                        pe.wait_ge(stacked[1 - par][g], 192 * half_s + 192)
                if t:
                    pe.wait_ge(ones_in, 32)
                    pe.wait_ge(m_in, 48 * (k - 1))
                    wait(pe, suf_ev, BT * (k - 1))
                    wait(pe, o_ev, BT * (k - 2))
                    if proj:
                        pe.wait_ge(qk_ev, 4 * k + 4)
                        pe.wait_ge(v_ev, BT * k + BT)
                    else:
                        pe.wait_ge(mt_ok, k - 1)
                elif s:
                    pe.wait_ge(qk_ev, 4 * k + 4)
                if not (s or t):
                    return
                pe.sem_inc(heads_on, 1)
                with pe.Fori(0, HG) as j:
                    for g in range(GH):
                        if t:
                            weights(k, par, GH * j + g)
                        if s:
                            scores(k, par, GH * j + g)
                    if t:
                        sums(k, par, j)

            def scores(k, par, h):
                n = 3 * (HEADS * (k - 1) + h)
                query = lambda i: qs[0:KR, 1 - par, bass.ds(h, 1), i * P:(i + 1) * P].rearrange("p a n -> p (a n)")
                keys = lambda i: ks[0:KR, 1 - par, bass.ds(h, 1), 0:(i + 1) * P].rearrange("p a n -> p (a n)")
                for m, blocks in enumerate((((3, 0),), ((2, 0), (0, 384)), ((1, 0),))):
                    pe.wait_ge(smax, n + m + 1)
                    for i, lo in blocks:
                        hi = lo + (i + 1) * P
                        mm(p_s[:, m, lo:hi], query(i), keys(i), start=True, stop=False, skip_group_check=True)
                        last = mm(p_s[:, m, hi - P:hi], ident_b[:, :], mask_s[:, :], start=False, stop=True, skip_group_check=True)
                    last.then_inc(s_ps, 1)

            def weights(k, par, h):
                n = 2 * (HEADS * (k - 2) + h)
                key = lambda j: ks[0:KM, par, bass.ds(h, 1), j * P:(j + 1) * P].rearrange("p a n -> p (a n)")
                queries = lambda j: qs[0:KM, par, bass.ds(h, 1), j * P:SEQ].rearrange("p a n -> p (a n)")
                for m, blocks in enumerate((((0, 0, 0),), ((1, 1, 0), (3, 1, 384), (2, 2, 0)))):
                    pe.wait_ge(exp_ev, n + m + 1)
                    for j, bank, lo in blocks:
                        mm(p_t[:, bank, lo:lo + SEQ - j * P], key(j), queries(j), start=True, stop=False, skip_group_check=True)
                        last = mm(p_t[:, bank, lo:lo + P], ident_b[:, :], mask_t[:, :], start=False, stop=True, skip_group_check=True)
                    last.then_inc(t_ps, 1)

            def sums(k, par, j):
                group = HG * (k - 2) + j
                pe.wait_ge(vg_ok, group + 1)
                pe.wait_ge(ot_ok, group + 1)
                pe.wait_ge(exp_ev, 2 * GH * group + 2 * GH + 2)
                for b in range(BT):
                    for g in range(GH):
                        last = mm(p_p[g * GW:(g + 1) * GW, 0, b * P:SEQ], vg[:, b, g, :], pt[:, g, SPAN[b]:SPAN[b] + SEQ - b * P],
                                  start=b == 0, stop=b == BT - 1, skip_group_check=True)
                last.then_inc(pv_ps, 1)

            steps(pe, step)


def build(nc, x, a, b, ffn, tables, out):
    dram = lambda name, shape, dt=F32: nc.dram_tensor(name, shape, dt, kind="Internal").ap()
    rows_of = lambda t: t.rearrange("b s n -> (b s) n")
    x1, x3 = dram("x1", (N_TOK, D)), dram("x3", (N_TOK, D))
    x2 = dram("x2", (2 * N_TOK, D))
    rows = dram("rows", (2 * N_TOK, PAY))
    parts = dram("parts", (2, 3, 4, P, SEQ), BF16)
    tok, band_bias, first_bias = tables
    stage_a(nc, rows_of(x), *a, band_bias, first_bias, x1)
    stage_moe(nc, "m", x1, *ffn, tok, rows, x2, zero_rows=True, skip=False)
    stage_b(nc, x2[0:N_TOK, :], *b, parts, x3)
    stage_moe(nc, "n", x3, *ffn, tok, rows, rows_of(out), zero_rows=False, skip=True)


ATTN = ("wq", "bq", "wk", "bk", "wv", "bv", "wo", "bo")
GATES = ("pw1", "pb1", "pw2", "pb2", "sw1", "sb1", "sw2", "sb2")


def kernel(**inputs):
    import numpy as np
    import concourse.bacc as bacc
    from concourse.bass_utils import run_bass_kernel_spmd

    nc = bacc.Bacc("TRN2", target_bir_lowering=False, num_devices=1)
    arrays = {}

    def given(name, array):
        arrays[name] = np.ascontiguousarray(array)
        return nc.dram_tensor(name, array.shape, mybir.dt.from_np(array.dtype), kind="ExternalInput").ap()

    take = lambda prefix, names: [given(f"in_{prefix}{n}", inputs[prefix + n]) for n in names]
    x, = take("L0_attn_a_", ("x",))
    a = take("L0_attn_a_", ATTN)
    b = take("L0_attn_b_", ATTN + GATES)
    ffn = take("L0_ffn_", ("Wg", "w1", "w2"))
    band_bias, first_bias = band_tables(np)
    tables = given("token_table", token_table(np)), given("band_bias", band_bias), given("first_bias", first_bias)
    out = nc.dram_tensor("out_x", (BATCH, SEQ, D), F32, kind="ExternalOutput").ap()
    build(nc, x, a, b, ffn, tables, out)
    r = run_bass_kernel_spmd(nc, [arrays], core_ids=[0])
    return r.results[0]["out_x"]
```
